# Optimizing a Trainium2 kernel written in Bass

```python
import numpy as np
import jax
import jax.numpy as jnp

def _softmax(x, axis=-1):
    return jax.nn.softmax(x, axis=axis)

def _gelu(x):
    return jax.nn.gelu(x, approximate=True)

def _silu(x):
    return jax.nn.silu(x)

def _sigmoid(x):
    return jax.nn.sigmoid(x)

def _layernorm(x, axis=-1, eps=1e-05):
    m = jnp.mean(x, axis=axis, keepdims=True)
    v = jnp.var(x, axis=axis, keepdims=True)
    return (x - m) / jnp.sqrt(v + eps)

def _scatter_add(tgt, idx, src, axis=0):
    return tgt.at[idx].add(src)

def _segment_sum(src, seg, n):
    return jax.ops.segment_sum(src, seg, n)
kernel_name = 'mk_flamingo_gated_d2_seqx_r8_83b7a9'

def setup_inputs(seed: int=0):
    np.random.seed(seed)
    _w = jnp.asarray

    def _rec_inputs():
        import jax
        import jax.numpy as jnp
        _rk = jax.random.key(seed)
        x = 4.136e-05 + 0.9999 * jax.random.normal(jax.random.fold_in(_rk, 1), (4, 256, 256), jnp.float32)
        _lenS = 256 - jax.random.randint(jax.random.fold_in(_rk, 7), (4,), 0, max(1, 256 // 4) + 1, jnp.int32)
        _lenS2 = 256 - jax.random.randint(jax.random.fold_in(_rk, 8), (4,), 0, max(1, 256 // 4) + 1, jnp.int32)
        _ctx_1024P = jax.random.normal(jax.random.fold_in(_rk, 11), (4, 16, 128), jnp.float32)
        _ctx_1024c = jax.random.dirichlet(jax.random.fold_in(_rk, 511), 0.3 * jnp.ones((16,), jnp.float32), (4, 256))
        _ctx_1024t = jnp.einsum('bsk,bkd->bsd', _ctx_1024c, _ctx_1024P)
        _ctx_1024t = _ctx_1024t * jax.lax.rsqrt(jnp.mean(jnp.square(_ctx_1024t)) + 1e-12) * 0.953939
        ctx_1024 = -0.000292821 + 1.00034 * (_ctx_1024t + 0.3 * jax.random.normal(jax.random.fold_in(_rk, 611), (4, 256, 128), jnp.float32))
        _g = jax.random.normal(jax.random.fold_in(_rk, 9001), (2, 2), jnp.float32)
        _g = jnp.sign(_g) * jnp.maximum(jnp.abs(_g), 1.0) + (_g == 0) * 1.0
        g_xattn = _g[0]
        g_ffn = _g[1]
        return (x, ctx_1024, g_xattn, g_ffn)
    x, ctx_1024, g_xattn, g_ffn = _rec_inputs()

    def _L0_xattn_setup():
        import jax, jax.numpy as jnp
        import numpy as np
        import math
        B, L, DM = (2, 256, 128)
        DS, DC, EXP = (16, 4, 2)
        DI = EXP * DM
        DR = math.ceil(DM / 16)
        DT_MIN, DT_MAX, DT_FLOOR = (0.001, 0.1, 0.0001)

        def _ssm_forward(hidden_states, z, in_proj_w, conv_w, conv_b, x_proj_w, dt_proj_w, dt_proj_b, A_log, D):
            b = hidden_states.shape[0]
            x = jnp.einsum('ed,bld->bel', in_proj_w, hidden_states)
            xp = jnp.pad(x, ((0, 0), (0, 0), (DC - 1, 0)))
            xc = jax.lax.conv_general_dilated(xp, conv_w[:, None, :], window_strides=(1,), padding='VALID', dimension_numbers=('NCH', 'OIH', 'NCH'), feature_group_count=DI)
            u = jax.nn.silu(xc + conv_b[None, :, None])
            x_dbl = jnp.einsum('ke,bel->bkl', x_proj_w, u)
            dt_lo = x_dbl[:, :DR]
            Bm = x_dbl[:, DR:DR + DS]
            Cm = x_dbl[:, DR + DS:]
            delta = jax.nn.softplus(jnp.einsum('er,brl->bel', dt_proj_w, dt_lo) + dt_proj_b[None, :, None])
            A = -jnp.exp(A_log)

            def step(state, xs):
                d_t, B_t, C_t, u_t = xs
                dA = jnp.exp(d_t[..., None] * A)
                state = state * dA + (d_t * u_t)[..., None] * B_t[:, None, :]
                y_t = jnp.einsum('ben,bn->be', state, C_t)
                return (state, y_t)
            xs = (jnp.moveaxis(delta, -1, 0), jnp.moveaxis(Bm, -1, 0), jnp.moveaxis(Cm, -1, 0), jnp.moveaxis(u, -1, 0))
            state0 = jnp.zeros((b, DI, DS), delta.dtype)
            _, ys = jax.lax.scan(step, state0, xs)
            y = jnp.moveaxis(ys, 0, -1)
            y = y + D[None, :, None] * u
            y = y * jax.nn.silu(z)
            return jnp.swapaxes(y, 1, 2)
        key = jax.random.key(seed)
        ks = jax.random.split(key, 8)
        hidden_states = jax.random.normal(ks[0], (B, L, DM), jnp.float32)
        z = jax.random.normal(ks[1], (B, DI, L), jnp.float32)
        in_proj_w = jax.random.normal(ks[2], (DI, DM), jnp.float32) * DM ** (-0.5)
        conv_w = jax.random.normal(ks[3], (DI, DC), jnp.float32) * DC ** (-0.5)
        conv_b = jnp.zeros((DI,), jnp.float32)
        x_proj_w = jax.random.normal(ks[4], (DR + 2 * DS, DI), jnp.float32) * DI ** (-0.5)
        dt_std = DR ** (-0.5)
        dt_proj_w = jax.random.uniform(ks[5], (DI, DR), jnp.float32, -dt_std, dt_std)
        dt = jnp.exp(jax.random.uniform(ks[6], (DI,), jnp.float32) * (math.log(DT_MAX) - math.log(DT_MIN)) + math.log(DT_MIN))
        dt = jnp.clip(dt, DT_FLOOR)
        dt_proj_b = dt + jnp.log(-jnp.expm1(-dt))
        A_log = jnp.log(jnp.broadcast_to(jnp.arange(1, DS + 1, dtype=jnp.float32), (DI, DS)))
        D = jnp.ones((DI,), jnp.float32)
        return dict(hidden_states=hidden_states, z=z, in_proj_w=in_proj_w, conv_w=conv_w, conv_b=conv_b, x_proj_w=x_proj_w, dt_proj_w=dt_proj_w, dt_proj_b=dt_proj_b, A_log=A_log, D=D)
    _L0_xattn_all = _L0_xattn_setup()
    _L0_xattn_in = {k: v for k, v in _L0_xattn_all.items() if k in ('in_proj_w', 'conv_w', 'conv_b', 'x_proj_w', 'dt_proj_w', 'dt_proj_b', 'A_log', 'D')}
    del _L0_xattn_all

    def _L0_ffn_setup():
        import jax, jax.numpy as jnp
        import numpy as np
        from jax import lax
        B, S, H = (2, 64, 256)
        I = 96
        E = 64
        K = 8
        key = jax.random.key(seed)
        k1, k2, k3, k4 = jax.random.split(key, 4)
        hidden_states = jax.random.normal(k1, (B, S, H), jnp.float32)
        gate_weight = jax.random.normal(k2, (E, H), jnp.float32) * 0.02
        gate_up_weights = jax.random.normal(k3, (E, H, 2 * I), jnp.float32) * 0.02
        down_weights = jax.random.normal(k4, (E, I, H), jnp.float32) * 0.02
        return {'hidden_states': hidden_states, 'gate_weight': gate_weight, 'gate_up_weights': gate_up_weights, 'down_weights': down_weights}
    _L0_ffn_all = _L0_ffn_setup()
    _L0_ffn_in = {k: v for k, v in _L0_ffn_all.items() if k in ('gate_weight', 'gate_up_weights', 'down_weights')}
    del _L0_ffn_all

    def _L1_xattn_setup():
        import jax, jax.numpy as jnp
        import numpy as np
        B_, L_, D_MODEL = (4, 256, 128)
        D_STATE, D_CONV, EXPAND = (16, 4, 2)
        D_INNER = EXPAND * D_MODEL
        DT_RANK = (D_MODEL + 15) // 16

        def silu(x):
            return x * jax.nn.sigmoid(x)
        key = jax.random.key(seed)
        ks = jax.random.split(key, 10)
        f32 = jnp.float32
        hidden_states = jax.random.normal(ks[0], (B_, L_, D_MODEL), dtype=f32)
        z = jax.random.normal(ks[1], (B_, D_INNER, L_), dtype=f32)
        in_proj_w = jax.random.normal(ks[2], (D_INNER, D_MODEL), dtype=f32) * 0.02
        conv_w = jax.random.normal(ks[3], (D_INNER, 1, D_CONV), dtype=f32) * 0.1
        conv_b = jax.random.normal(ks[4], (D_INNER,), dtype=f32) * 0.02
        x_proj_w = jax.random.normal(ks[5], (DT_RANK + 2 * D_STATE, D_INNER), dtype=f32) * 0.02
        dt_proj_w = jax.random.uniform(ks[6], (D_INNER, DT_RANK), dtype=f32, minval=-DT_RANK ** (-0.5), maxval=DT_RANK ** (-0.5))
        dt = jnp.exp(jax.random.uniform(ks[7], (D_INNER,), dtype=f32, minval=np.log(0.001), maxval=np.log(0.1)))
        dt_proj_b = jnp.log(jnp.expm1(dt))
        A_log = jnp.log(jnp.broadcast_to(jnp.arange(1, D_STATE + 1, dtype=f32), (D_INNER, D_STATE)))
        D = jnp.ones((D_INNER,), f32)
        return {'hidden_states': hidden_states, 'z': z, 'in_proj_w': in_proj_w, 'conv_w': conv_w, 'conv_b': conv_b, 'x_proj_w': x_proj_w, 'dt_proj_w': dt_proj_w, 'dt_proj_b': dt_proj_b, 'A_log': A_log, 'D': D}
    _L1_xattn_all = _L1_xattn_setup()
    _L1_xattn_in = {k: v for k, v in _L1_xattn_all.items() if k in ('in_proj_w', 'conv_w', 'conv_b', 'x_proj_w', 'dt_proj_w', 'dt_proj_b', 'A_log', 'D')}
    del _L1_xattn_all

    def _L1_ffn_setup():
        import jax, jax.numpy as jnp
        import numpy as np
        EPS = 1e-05

        def fwht(x):
            orig_shape = x.shape
            n = orig_shape[-1]
            x = x.reshape(-1, n)
            h = 1
            while h < n:
                x = x.reshape(-1, n // (2 * h), 2, h)
                a, b = (x[:, :, 0, :], x[:, :, 1, :])
                x = jnp.stack([a + b, a - b], axis=2).reshape(-1, n)
                h *= 2
            return (x * (1.0 / np.sqrt(n))).reshape(orig_shape)

        def act_quant(x):
            scale = 127.0 / jnp.clip(jnp.max(jnp.abs(x), axis=-1, keepdims=True), EPS)
            q = jnp.clip(jnp.round(x * scale), -128.0, 127.0) / scale
            return x + jax.lax.stop_gradient(q - x)

        def weight_quant(w):
            scale = jnp.clip(jnp.mean(jnp.abs(w)), EPS)
            q = jnp.clip(jnp.round(w / scale), -1.0, 1.0) * scale
            return w + jax.lax.stop_gradient(q - w)

        def h_bitlinear(x, w):
            xq = act_quant(fwht(x))
            wq = weight_quant(w)
            return jnp.einsum('bsh,oh->bso', xq, wq)
        key = jax.random.key(seed)
        k1, k2, k3, k4 = jax.random.split(key, 4)
        H, I = (256, 1024)
        B, S = (2, 256)
        hidden_states = jax.random.normal(k1, (B, S, H), dtype=jnp.float32)
        w_gate = jax.random.normal(k2, (I, H), dtype=jnp.float32) * 0.02
        w_up = jax.random.normal(k3, (I, H), dtype=jnp.float32) * 0.02
        w_down = jax.random.normal(k4, (H, I), dtype=jnp.float32) * 0.02
        return {'hidden_states': hidden_states, 'w_gate': w_gate, 'w_up': w_up, 'w_down': w_down}
    _L1_ffn_all = _L1_ffn_setup()
    _L1_ffn_in = {k: v for k, v in _L1_ffn_all.items() if k in ('w_gate', 'w_up', 'w_down')}
    del _L1_ffn_all
    return {'x': x, 'ctx_1024': ctx_1024, 'g_xattn': g_xattn, 'g_ffn': g_ffn, 'L0_xattn_in_proj_w': _L0_xattn_in['in_proj_w'], 'L0_xattn_conv_w': _L0_xattn_in['conv_w'], 'L0_xattn_conv_b': _L0_xattn_in['conv_b'], 'L0_xattn_x_proj_w': _L0_xattn_in['x_proj_w'], 'L0_xattn_dt_proj_w': _L0_xattn_in['dt_proj_w'], 'L0_xattn_dt_proj_b': _L0_xattn_in['dt_proj_b'], 'L0_xattn_A_log': _L0_xattn_in['A_log'], 'L0_xattn_D': _L0_xattn_in['D'], 'L0_ffn_gate_weight': _L0_ffn_in['gate_weight'], 'L0_ffn_gate_up_weights': _L0_ffn_in['gate_up_weights'], 'L0_ffn_down_weights': _L0_ffn_in['down_weights'], 'L1_xattn_in_proj_w': _L1_xattn_in['in_proj_w'], 'L1_xattn_conv_w': _L1_xattn_in['conv_w'], 'L1_xattn_conv_b': _L1_xattn_in['conv_b'], 'L1_xattn_x_proj_w': _L1_xattn_in['x_proj_w'], 'L1_xattn_dt_proj_w': _L1_xattn_in['dt_proj_w'], 'L1_xattn_dt_proj_b': _L1_xattn_in['dt_proj_b'], 'L1_xattn_A_log': _L1_xattn_in['A_log'], 'L1_xattn_D': _L1_xattn_in['D'], 'L1_ffn_w_gate': _L1_ffn_in['w_gate'], 'L1_ffn_w_up': _L1_ffn_in['w_up'], 'L1_ffn_w_down': _L1_ffn_in['w_down']}

def reference(x, ctx_1024, g_xattn, g_ffn, L0_xattn_in_proj_w, L0_xattn_conv_w, L0_xattn_conv_b, L0_xattn_x_proj_w, L0_xattn_dt_proj_w, L0_xattn_dt_proj_b, L0_xattn_A_log, L0_xattn_D, L0_ffn_gate_weight, L0_ffn_gate_up_weights, L0_ffn_down_weights, L1_xattn_in_proj_w, L1_xattn_conv_w, L1_xattn_conv_b, L1_xattn_x_proj_w, L1_xattn_dt_proj_w, L1_xattn_dt_proj_b, L1_xattn_A_log, L1_xattn_D, L1_ffn_w_gate, L1_ffn_w_up, L1_ffn_w_down):
    import jax
    import jax.numpy as jnp

    def _L0_xattn_ref(hidden_states, z, in_proj_w, conv_w, conv_b, x_proj_w, dt_proj_w, dt_proj_b, A_log, D):
        import jax, jax.numpy as jnp
        import numpy as np
        import math
        B, L, DM = (2, 256, 128)
        DS, DC, EXP = (16, 4, 2)
        DI = EXP * DM
        DR = math.ceil(DM / 16)
        DT_MIN, DT_MAX, DT_FLOOR = (0.001, 0.1, 0.0001)

        def _ssm_forward(hidden_states, z, in_proj_w, conv_w, conv_b, x_proj_w, dt_proj_w, dt_proj_b, A_log, D):
            b = hidden_states.shape[0]
            x = jnp.einsum('ed,bld->bel', in_proj_w, hidden_states)
            xp = jnp.pad(x, ((0, 0), (0, 0), (DC - 1, 0)))
            xc = jax.lax.conv_general_dilated(xp, conv_w[:, None, :], window_strides=(1,), padding='VALID', dimension_numbers=('NCH', 'OIH', 'NCH'), feature_group_count=DI)
            u = jax.nn.silu(xc + conv_b[None, :, None])
            x_dbl = jnp.einsum('ke,bel->bkl', x_proj_w, u)
            dt_lo = x_dbl[:, :DR]
            Bm = x_dbl[:, DR:DR + DS]
            Cm = x_dbl[:, DR + DS:]
            delta = jax.nn.softplus(jnp.einsum('er,brl->bel', dt_proj_w, dt_lo) + dt_proj_b[None, :, None])
            A = -jnp.exp(A_log)

            def step(state, xs):
                d_t, B_t, C_t, u_t = xs
                dA = jnp.exp(d_t[..., None] * A)
                state = state * dA + (d_t * u_t)[..., None] * B_t[:, None, :]
                y_t = jnp.einsum('ben,bn->be', state, C_t)
                return (state, y_t)
            xs = (jnp.moveaxis(delta, -1, 0), jnp.moveaxis(Bm, -1, 0), jnp.moveaxis(Cm, -1, 0), jnp.moveaxis(u, -1, 0))
            state0 = jnp.zeros((b, DI, DS), delta.dtype)
            _, ys = jax.lax.scan(step, state0, xs)
            y = jnp.moveaxis(ys, 0, -1)
            y = y + D[None, :, None] * u
            y = y * jax.nn.silu(z)
            return jnp.swapaxes(y, 1, 2)
        return _ssm_forward(hidden_states, z, in_proj_w, conv_w, conv_b, x_proj_w, dt_proj_w, dt_proj_b, A_log, D)

    def _L0_ffn_ref(hidden_states, gate_weight, gate_up_weights, down_weights):
        import jax, jax.numpy as jnp
        import numpy as np
        from jax import lax
        B, S, H = (2, 64, 256)
        I = 96
        E = 64
        K = 8
        orig_shape = hidden_states.shape
        x = hidden_states.reshape(-1, H)
        T = x.shape[0]
        logits = x @ gate_weight.T
        probs = jax.nn.softmax(logits.astype(jnp.float32), axis=-1)
        routing_weights, selected_experts = lax.top_k(probs, K)
        wsum = routing_weights.sum(axis=-1, keepdims=True)
        wsum = jnp.where(wsum == 0, 1.0, wsum)
        routing_weights = (routing_weights / wsum).astype(x.dtype)
        combine = jnp.zeros((T, E), x.dtype).at[jnp.arange(T)[:, None], selected_experts].add(routing_weights)

        def body(acc, ws):
            wgu, wd, we = ws
            gu = x @ wgu
            gate, up = jnp.split(gu, 2, axis=-1)
            act = jax.nn.silu(gate) * up
            out = act @ wd
            return (acc + we[:, None] * out, None)
        init = jnp.zeros_like(x)
        final, _ = lax.scan(body, init, (gate_up_weights, down_weights, combine.T))
        return final.reshape(orig_shape)

    def _L1_xattn_ref(hidden_states, z, in_proj_w, conv_w, conv_b, x_proj_w, dt_proj_w, dt_proj_b, A_log, D):
        import jax, jax.numpy as jnp
        import numpy as np
        B_, L_, D_MODEL = (4, 256, 128)
        D_STATE, D_CONV, EXPAND = (16, 4, 2)
        D_INNER = EXPAND * D_MODEL
        DT_RANK = (D_MODEL + 15) // 16

        def silu(x):
            return x * jax.nn.sigmoid(x)
        Bsz, L, _ = hidden_states.shape
        d_inner, _, d_conv = conv_w.shape
        dt_rank = dt_proj_w.shape[1]
        d_state = A_log.shape[1]
        x = jnp.einsum('bld,ed->bel', hidden_states, in_proj_w)
        xc = jax.lax.conv_general_dilated(x, conv_w, window_strides=(1,), padding=[(d_conv - 1, 0)], feature_group_count=d_inner, dimension_numbers=('NCH', 'OIH', 'NCH'))
        x = silu(xc + conv_b[None, :, None])
        x_dbl = jnp.einsum('bdl,ed->bel', x, x_proj_w)
        dt_low, Bm, Cm = jnp.split(x_dbl, [dt_rank, dt_rank + d_state], axis=1)
        dt = jnp.einsum('brl,dr->bdl', dt_low, dt_proj_w)
        dt = jax.nn.softplus(dt + dt_proj_b[None, :, None])
        A = -jnp.exp(A_log)
        dt_t = jnp.moveaxis(dt, -1, 0)
        B_t = jnp.moveaxis(Bm, -1, 0)
        C_t = jnp.moveaxis(Cm, -1, 0)
        u_t = jnp.moveaxis(x, -1, 0)

        def step(state, inp):
            d, b, c, u = inp
            dA = jnp.exp(d[..., None] * A)
            state = state * dA + (d * u)[..., None] * b[:, None, :]
            y = jnp.einsum('bdn,bn->bd', state, c)
            return (state, y)
        state0 = jnp.zeros((Bsz, d_inner, d_state), x.dtype)
        _, ys = jax.lax.scan(step, state0, (dt_t, B_t, C_t, u_t))
        y = jnp.moveaxis(ys, 0, 2)
        y = y + D[None, :, None] * x
        y = y * silu(z)
        return jnp.swapaxes(y, 1, 2)

    def _L1_ffn_ref(hidden_states, w_gate, w_up, w_down):
        import jax, jax.numpy as jnp
        import numpy as np
        EPS = 1e-05

        def fwht(x):
            orig_shape = x.shape
            n = orig_shape[-1]
            x = x.reshape(-1, n)
            h = 1
            while h < n:
                x = x.reshape(-1, n // (2 * h), 2, h)
                a, b = (x[:, :, 0, :], x[:, :, 1, :])
                x = jnp.stack([a + b, a - b], axis=2).reshape(-1, n)
                h *= 2
            return (x * (1.0 / np.sqrt(n))).reshape(orig_shape)

        def act_quant(x):
            scale = 127.0 / jnp.clip(jnp.max(jnp.abs(x), axis=-1, keepdims=True), EPS)
            q = jnp.clip(jnp.round(x * scale), -128.0, 127.0) / scale
            return x + jax.lax.stop_gradient(q - x)

        def weight_quant(w):
            scale = jnp.clip(jnp.mean(jnp.abs(w)), EPS)
            q = jnp.clip(jnp.round(w / scale), -1.0, 1.0) * scale
            return w + jax.lax.stop_gradient(q - w)

        def h_bitlinear(x, w):
            xq = act_quant(fwht(x))
            wq = weight_quant(w)
            return jnp.einsum('bsh,oh->bso', xq, wq)
        gate = h_bitlinear(hidden_states, w_gate)
        up = h_bitlinear(hidden_states, w_up)
        return h_bitlinear(jax.nn.silu(gate) * up, w_down)
    x = x + jnp.tanh(g_xattn[0]) * _L0_xattn_ref(ctx_1024, _layernorm(x, axis=-1), L0_xattn_in_proj_w, L0_xattn_conv_w, L0_xattn_conv_b, L0_xattn_x_proj_w, L0_xattn_dt_proj_w, L0_xattn_dt_proj_b, L0_xattn_A_log, L0_xattn_D)
    x = x + jnp.tanh(g_ffn[0]) * _L0_ffn_ref(_layernorm(x, axis=-1), L0_ffn_gate_weight, L0_ffn_gate_up_weights, L0_ffn_down_weights)
    x = x + jnp.tanh(g_xattn[1]) * _L1_xattn_ref(ctx_1024, _layernorm(x, axis=-1), L1_xattn_in_proj_w, L1_xattn_conv_w, L1_xattn_conv_b, L1_xattn_x_proj_w, L1_xattn_dt_proj_w, L1_xattn_dt_proj_b, L1_xattn_A_log, L1_xattn_D)
    x = x + jnp.tanh(g_ffn[1]) * _L1_ffn_ref(_layernorm(x, axis=-1), L1_ffn_w_gate, L1_ffn_w_up, L1_ffn_w_down)
    return x

_drawn_inputs = setup_inputs


def setup_inputs(seed=0):
    import zlib

    import numpy as np

    out = dict(_drawn_inputs(seed))
    spreads = {'g_ffn': (-1.0, 0.6),
     'L0_xattn_conv_b': (0.0, 0.1),
     'L0_xattn_D': (1.0, 0.2),
     'L1_xattn_D': (1.0, 0.6)}
    factors = {'L0_xattn_dt_proj_w': 7.953,
     'L0_xattn_dt_proj_b': 3.293,
     'L0_xattn_A_log': 2.889,
     'L0_ffn_gate_weight': 8.0,
     'L0_ffn_gate_up_weights': 8.0,
     'L0_ffn_down_weights': 8.0,
     'L1_xattn_in_proj_w': 4.714,
     'L1_xattn_conv_w': 4.825,
     'L1_xattn_conv_b': 8.0,
     'L1_xattn_x_proj_w': 8.0,
     'L1_xattn_dt_proj_w': 8.0,
     'L1_xattn_dt_proj_b': 8.0,
     'L1_xattn_A_log': 8.0,
     'L1_ffn_w_gate': 7.372,
     'L1_ffn_w_up': 7.344,
     'L1_ffn_w_down': 7.356}
    for name, (base, spread) in spreads.items():
        noise = np.random.default_rng([zlib.crc32(name.encode()), seed]).standard_normal(out[name].shape)
        drawn = base * np.exp(spread * noise) if base else spread * noise
        out[name] = jnp.asarray(drawn.astype(out[name].dtype))
    for name, factor in factors.items():
        out[name] = (out[name] * factor).astype(out[name].dtype)
    return out
```

```python
from contextlib import ExitStack

import concourse.bass as bass
from concourse import mybir

P = 128
F32 = mybir.dt.float32
F32R = mybir.dt.float32r
BF16 = mybir.dt.bfloat16
ALU = mybir.AluOpType
ACT = mybir.ActivationFunctionType
AX = mybir.AxisListType

B, L, D = 4, 256, 256
T = B * L
NT = T // P
DM = 128
DI = 256
NH = DI // P
DS = 16
DC = 4
DR = 8
LP = L + DC - 1
E, I = 64, 96
TOPK = 8
EC = 4
CW = EC * I
CB = CW // P
NCH = E // EC
GUW = 2 * 2 * CW
DWW = CB * D
WP = 256
HID = 1024
HB = HID // P
LN_EPS = 1e-5
Q_EPS = 1e-5
ROUND = 12582912.0
HALF_T = T // 2


def flamingo_gated_block(nc, a, out):
    ctx = ExitStack()
    with ctx:
        def sb(name, shape, dt=F32):
            return ctx.enter_context(nc.sbuf_tensor(name, shape, dt))

        def sem(name):
            return ctx.enter_context(nc.semaphore(name))

        PS = ctx.enter_context(nc.psum_tensor("banks", [P, 8, 512], F32))

        ident = sb("ident", [P, P])
        identb = sb("identb", [P, P], BF16)
        had = sb("had", [P, 2, D])
        sel = sb("sel", [80, DS, P], BF16)
        ones = sb("ones", [P, P])
        nhalf = sb("nhalf", [P, NT])
        gates_in = sb("gates_in", [P, 4])
        gates = sb("gates", [P, 4])
        hgates = sb("hgates", [P, 4])
        ctxp = sb("ctxp", [P, B, LP])
        inw = sb("inw", [P, DI])
        raw = [sb(f"raw{i}", [P, GUW + DWW]) for i in range(2)]
        convb = raw[0][:, 0:1024].rearrange("p (k e) -> p k e", k=DC)
        tapw = raw[0][:, 1024:2048].rearrange("p (k e) -> p k e", k=DC)
        xpw = sb("xpw", [P, NH, 2, 104])
        dtw = sb("dtw", [DR, DI])
        chan = sb("chan", [P, 2, NH, 3 + DS])
        Aneg = sb("Aneg", [P, 2, NH, DS])
        hcb = sb("hcb", [P, NH])
        xs = sb("xs", [P, NT, D])
        sz = sb("sz", [P, NT, D])
        stats = sb("stats", [P, NT, 6])
        mv = sb("mv", [P, NT, 2])
        rstd = sb("rstd", [P, NT])
        delta = sb("delta", [P, NH, T])
        duT = sb("duT", [P, NT, DI])
        BCt = sb("BCt", [P, NT, 2 * DS])
        u = sb("u", [P, NH, T])
        work = sb("work", [P, 4, 2048])
        yT = sb("yT", [P, NT, DI])

        th_ = work[:, 0, :].rearrange("p (h t) -> p h t", h=NH)
        ey_ = work[:, 1, :].rearrange("p (h t) -> p h t", h=NH)
        lw_ = work[:, 2, :].rearrange("p (h t) -> p h t", h=NH)
        w3_ = work[:, 3, :].rearrange("p (h t) -> p h t", h=NH)
        CS = sb("CS", [80, T], BF16)
        R0 = raw[1][0:80, 0:T]
        dtlo = raw[1][0:DR, T:2 * T]
        dA0 = work[:, 0, :].rearrange("p (i h t) -> p i h t", i=2, h=NH)
        dBuT0 = work[:, 1, :].rearrange("p (i j e) -> p i j e", i=2, j=4)
        h0 = work[:, 2, :].rearrange("p (i x) -> p i x", i=2)
        prod0 = work[:, 3, :].rearrange("p (i h t) -> p i h t", i=2, h=NH)
        xThi = sb("xThi", [P, 2, T], F32R)
        xTlo = sb("xTlo", [P, 2, T], F32R)
        gwT = sb("gwT", [P, 2, E])
        gwhi = sb("gwhi", [P, 2, E], F32R)
        gwlo = sb("gwlo", [P, 2, E], F32R)
        probs = sb("probs", [P, NT, E])
        left = sb("left", [P, NT, E])
        comb = sb("comb", [P, NT, E])
        top8 = sb("top8", [P, NT, TOPK])
        rsm = sb("rsm", [P, 4, NT])
        whi = [sb(f"whi{i}", [P, GUW + DWW], F32R) for i in range(2)]
        wlo = [sb(f"wlo{i}", [P, GUW + DWW], F32R) for i in range(2)]
        tg = work[:, 0, 0:2 * CW].rearrange("p (i f) -> p i f", i=2)
        ga = work[:, 0, 2 * CW:4 * CW].rearrange("p (i f) -> p i f", i=2)
        act = work[:, 1, 0:3 * CW].rearrange("p (i f) -> p i f", i=3)
        actw = work[:, 2, 0:3 * CW].rearrange("p (i f) -> p i f", i=3)
        aThi = sb("aThi", [P, 2, CW], F32R)
        aTlo = sb("aTlo", [P, 2, CW], F32R)
        dA1 = work[:, 3, 0:1024].rearrange("p (i h t) -> p i h t", i=2, h=NH)
        dBuT1 = work[:, 3, 1024:2048].rearrange("p (i q e) -> p i q e", i=2, q=2)
        h1 = sb("h1", [P, 2, 512])
        wq = [sb(f"wq{m}", [P, 2048], BF16) for m in range(3)]
        wstat = sb("wstat", [P, 4, 3])
        tok = sb("tok", [P, 8, NT])
        ft = sb("ft", [P, 2, 8])
        xT3 = delta
        q1 = u[:].rearrange("p h t -> p (h t)").bitcast(BF16)[:, 0:NT * D].rearrange("p (j d) -> p j d", j=NT)
        q1T = u[:].rearrange("p h t -> p (h t)").bitcast(BF16)[:, NT * D:].rearrange("p (k t) -> p k t", k=2)
        duflat = duT[:].rearrange("p j e -> p (j e)").bitcast(BF16)
        qh = duflat[:, 0:2 * HID].rearrange("p (i f) -> p i f", i=2)
        qhT = duflat[:, 2 * HID:4 * HID].rearrange("p (i k t) -> p i k t", i=2, k=HB)
        fth = work[:, 0, 0:HID]
        fa = work[:, 0, HID:]
        fb = work[:, 1, :].rearrange("p (i f) -> p i f", i=2)
        fo = work[:, 2, :].rearrange("p (i f) -> p i f", i=2)
        fm = work[:, 3, 0:HID]
        fq = work[:, 3, HID:]
        bT = raw[0][:, 0:2 * HID].rearrange("p (i k t) -> p i k t", i=2, k=HB)

        def bank(k, n=1):
            return PS[:, k:k + n, :].rearrange("p k x -> p (k x)")

        S = {}

        def sm(name):
            if name not in S:
                S[name] = sem(name)
            return S[name]

        block = ctx.enter_context(nc.Block())

        szf = sz[:].rearrange("p j d -> p (j d)")
        ztan = yT[:].rearrange("p j d -> p (j d)")

        def parts(j):
            return [j] if j < 5 else [5, 6] if j == 5 else [j + 1]

        def chain(eng, name):
            s, n = sm(name), [0]

            def link(ins):
                n[0] += 1
                ins.then_inc(s, 1)
                eng.wait_ge(s, n[0])
                return ins
            return link

        out_rows = out.rearrange("b l d -> (b l) d").rearrange("(j p) d -> p j d", p=P)
        x_rows = a["x"].rearrange("b l d -> (b l) d").rearrange("(j p) d -> p j d", p=P)

        @block.sync
        def _(sp):
            lc = sm("ld_const")
            sp.dma_start(ident[:], a["ident"]).then_inc(lc, 16)
            sp.dma_start(identb[:], a["identb"]).then_inc(lc, 16)
            sp.dma_start(sel[:], a["sel"]).then_inc(lc, 16)
            sp.dma_start(had[:], a["had"].rearrange("(k p) f -> p k f", p=P)).then_inc(lc, 16)
            for i, g in enumerate(("g_xattn", "g_ffn")):
                sp.dma_start(gates_in[:, 2 * i:2 * i + 2], a[g].unsqueeze(0).broadcast_to([P, 2])).then_inc(lc, 16)
            sp.dma_start(gwT[:], a["gateT"].rearrange("(k p) e -> p k e", p=P)).then_inc(lc, 16)
            sp.dma_start(chan[:], a["chan"]).then_inc(lc, 16)
            for ly in range(2):
                if ly:
                    sp.wait_ge(sm("front_pe"), 3)
                lw = sm(f"ld_w{ly}")
                sp.dma_start(inw[:], a[f"L{ly}_inT"]).then_inc(lw, 16)
                sp.dma_start(convb[:], a[f"L{ly}_taps"].unsqueeze(0).broadcast_to([P, DC, DI])).then_inc(lw, 16)
                sp.dma_start(xpw[:, :, 0, :], a[f"L{ly}_xpT"].rearrange("(h p) k -> p h k", p=P)).then_inc(lw, 16)
                sp.dma_start(xpw[:, :, 1, 0:2 * DS], a[f"L{ly}_bcT"].rearrange("(h p) k -> p h k", p=P)).then_inc(lw, 16)
                sp.dma_start(dtw[:], a[f"L{ly}_dtT"]).then_inc(lw, 16)
                if ly == 0:
                    sp.wait_ge(sm("ctx_zero"), 1)
                    sp.dma_start(ctxp[:, :, DC - 1:], a["ctxT"].rearrange("d (b l) -> d b l", b=B)).then_inc(sm("ld_ctx"), 16)
                    sp.dma_start(xs[:], x_rows).then_inc(sm("ld_x"), 16)
            sp.wait_ge(sm("front_pe"), 9)
            for m, w in enumerate(("wgT", "wuT", "wdT")):
                sp.dma_start(work[:, m, :].rearrange("p (k f) -> p k f", k=(2, 2, HB)[m]),
                             a[w].rearrange("(k p) f -> p k f", p=P)).then_inc(sm("ld_wq"), 16)
            for c in range(NCH):
                if c >= 2:
                    sp.wait_ge(sm("wlo_done"), 9 * (c - 1))
                r = raw[c % 2]
                s = sm(f"ld_raw{c % 2}")
                sp.dma_start(r[:, 0:GUW].rearrange("p (k f) -> p k f", k=2),
                             a["guT"][c].rearrange("(k p) f -> p k f", p=P)).then_inc(s, 16)
                sp.dma_start(r[:, GUW:].rearrange("p (k f) -> p k f", k=CB),
                             a["dnT"][c].rearrange("(k p) f -> p k f", p=P)).then_inc(s, 16)
            for t in range(NT):
                sp.wait_ge(sm("out_ready"), t + 1)
                sp.dma_start(out_rows[:, t], xs[:, t]).then_inc(sm("stored"), 16)
            sp.wait_ge(sm("stored"), 16 * NT)

        @block.gpsimd
        def _(pool):
            link = chain(pool, "pool_own")
            pool.memset(ctxp[:], 0.0).then_inc(sm("ctx_zero"), 1)
            pool.memset(nhalf[:], -0.5).then_inc(sm("pool_const"), 1)
            pool.memset(ones[:], 1.0).then_inc(sm("pool_const"), 1)
            pool.wait_ge(sm("pool_const"), 2)

            def inverse_root(n):
                pool.wait_ge(sm("var_ready"), n)
                pool.tensor_tensor(rstd[:], rstd[:], nhalf[:], ALU.pow).then_inc(sm("rstd_ready"), 1)

            def taps(ly):
                pool.wait_ge(sm(f"ld_w{ly}"), 80)
                for k in range(DC):
                    ins = pool.tensor_tensor(tapw[:, k], inw[:], convb[:, k], ALU.mult)
                ins.then_inc(sm("tap_ready"), 1)

            taps(0)
            inverse_root(1)
            pool.wait_ge(sm("duT_ready"), 4)
            pool.wait_ge(sm("bct_ready"), 1)
            for k in range(2 * DS):
                bp, n = divmod(k, DS)
                if k >= 2:
                    pool.wait_ge(sm("dbu0_ready"), k - 1)
                pool.tensor_tensor(dBuT0[:, k % 2], duT[:, 4 * bp:4 * bp + 4, :],
                                   BCt[:, 4 * bp:4 * bp + 4, n:n + 1].broadcast_to([P, 4, DI]),
                                   ALU.mult).then_inc(sm("bmul0"), 1)
            taps(1)
            inverse_root(2)

            def split_lo(c, p):
                pool.wait_ge(sm("whi_done"), 9 * c + p + 1)
                if p == 0 and c >= 2:
                    pool.wait_ge(sm("gu_ready"), 8 * (c - 1))
                if p == 6 and c >= 2:
                    pool.wait_ge(sm("down_ready"), 8 * (c - 1))
                z = slice(p * WP, (p + 1) * WP)
                pool.tensor_tensor(wlo[c % 2][:, z], raw[c % 2][:, z], whi[c % 2][:, z].bitcast(F32),
                                   ALU.subtract).then_inc(sm("wlo_done"), 1)

            def bmul1(k):
                n, b = divmod(k, B)
                if k == 0:
                    pool.wait_ge(sm("duT_ready"), 8)
                    pool.wait_ge(sm("bct_ready"), 2)
                    pool.wait_ge(sm("wq_done"), 3)
                if k >= 2:
                    pool.wait_ge(sm("dbu1_ready"), k - 1)
                pool.tensor_tensor(dBuT1[:, k % 2], duT[:, 2 * b:2 * b + 2, :],
                                   BCt[:, 2 * b:2 * b + 2, n:n + 1].broadcast_to([P, 2, DI]),
                                   ALU.mult).then_inc(sm("bmul1"), 1)

            for p in range(9):
                split_lo(0, p)
            bmul1(0)
            for s in range(8 * NCH):
                c, j = divmod(s, 8)
                if s % 2 == 0 and s // 2 + 1 < 64:
                    bmul1(s // 2 + 1)
                if c + 1 < NCH:
                    for p in parts(j):
                        split_lo(c + 1, p)
                if s == 0:
                    pool.wait_ge(sm("comb_ready"), 1)
                pool.wait_ge(sm("umul_done"), s + 1)
                if s >= 3:
                    pool.wait_ge(sm("tr_ready"), s - 2)
                pool.tensor_tensor(actw[:, s % 3].rearrange("p (e f) -> p e f", e=EC),
                                   act[:, s % 3].rearrange("p (e f) -> p e f", e=EC),
                                   comb[:, j, EC * c:EC * c + EC].unsqueeze(2).broadcast_to([P, EC, I]),
                                   ALU.mult).then_inc(sm("wmul_done"), 1)
            inverse_root(3)
            inverse_root(4)
            for t in range(NT):
                pool.wait_ge(sm("ffn_b"), t + 1)
                if t >= 2:
                    pool.wait_ge(sm("ffn_tr"), t - 1)
                src = fb[:, t % 2].rearrange("p (x y r) -> p x y r", x=2, y=2)
                mid = fm.rearrange("p (x y r) -> p x y r", x=2, y=2)
                dst = fo[:, t % 2].rearrange("p (x y r) -> p x y r", x=2, y=2)
                pool.tensor_tensor(mid[:, :, 0], src[:, :, 0], src[:, :, 1], ALU.add)
                link(pool.tensor_tensor(mid[:, :, 1], src[:, :, 0], src[:, :, 1], ALU.subtract))
                pool.tensor_tensor(dst[:, 0], mid[:, 0], mid[:, 1], ALU.add)
                pool.tensor_tensor(dst[:, 1], mid[:, 0], mid[:, 1], ALU.subtract).then_inc(sm("ffn_mix"), 1)
                pool.wait_ge(sm("ffn_mix"), t + 1)

        @block.scalar
        def _(act_e):
            link = chain(act_e, "act_own")
            A = nc.scalar.activation
            act_e.wait_ge(sm("ld_const"), 16 * 8)
            link(A(gates[:], gates_in[:], ACT.Tanh))
            link(A(hgates[:], gates[:], ACT.Copy, scale=0.5))
            link(A(Aneg[:], chan[:, :, :, 3:], ACT.Exp))
            A(Aneg[:], Aneg[:], ACT.Copy, scale=-1.0).then_inc(sm("act_const"), 1)
            A(gwhi[:], gwT[:], ACT.Copy).then_inc(sm("act_const"), 1)

            def front(ly):
                if ly:
                    act_e.wait_ge(sm("x1_done"), 2)
                link(A(hcb[:], chan[:, ly, :, 0], ACT.Copy, scale=0.5))
                act_e.wait_ge(sm("front_pe"), 4 * ly + 1)
                for h in range(NH):
                    A(th_[:, h], bank(2 * h, 2), ACT.Tanh, scale=0.5, bias=hcb[:, h:h + 1])
                    A(w3_[:, h], bank(2 * h, 2), ACT.Identity, scale=0.5, bias=hcb[:, h:h + 1]).then_inc(sm("pre_u"), 1)
                act_e.wait_ge(sm("front_pe"), 4 * ly + 2)
                A(dtlo, PS[96:96 + DR, 4:6, :].rearrange("p k x -> p (k x)"), ACT.Copy).then_inc(sm("dtlo_ready"), 1)
                if ly == 0:
                    A(CS[:], PS[0:80, 4:6, :].rearrange("p k x -> p (k x)"), ACT.Copy).then_inc(sm("c1_ready"), 1)
                act_e.wait_ge(sm("front_pe"), 4 * ly + 3)
                act_e.wait_ge(sm("u_ready"), ly + 1)
                for h in range(NH):
                    bias = chan[:, ly, h, 1:2]
                    link(A(th_[:, h], bank(2 * h, 2), ACT.Abs, bias=bias))
                    A(w3_[:, h], bank(2 * h, 2), ACT.Relu, bias=bias)
                    link(A(ey_[:, h], th_[:, h], ACT.Exp, scale=-1.0))
                for h in range(NH):
                    A(lw_[:, h], ey_[:, h], ACT.Ln, bias=1.0).then_inc(sm("sp_ready"), 1)
                act_e.wait_ge(sm("front_pe"), 4 * ly + 4)
                if ly:
                    act_e.wait_ge(sm("bmul0"), 2 * DS)
                for k in range(4):
                    A(duT[:, 2 * k:2 * k + 2].rearrange("p j e -> p (j e)"), bank(4 + k), ACT.Copy).then_inc(sm("duT_ready"), 1)

            def gate_silu(n, to):
                act_e.wait_ge(sm("z_ready"), n)
                A(to, szf, ACT.Tanh, scale=0.5).then_inc(sm("ztan_ready"), 1)

            front(0)
            gate_silu(1, ztan)
            for k in range(2 * DS):
                bp, n = divmod(k, DS)
                if k == 0:
                    act_e.wait_ge(sm("dA_zero"), 1)
                if k >= 2:
                    act_e.wait_ge(sm("scan0"), k - 1)
                for h in range(NH):
                    src = delta[:, h, bp * HALF_T:(bp + 1) * HALF_T].rearrange("p (b l) -> p b l", b=2)[:, :, 1:]
                    dst = dA0[:, k % 2, h].rearrange("p (b l) -> p b l", b=2)[:, :, 1:]
                    ins = A(dst, src, ACT.Exp, scale=Aneg[:, 0, h, n:n + 1])
                ins.then_inc(sm("exp0"), 1)
            front(1)
            act_e.wait_ge(sm("front_pe"), 9)
            for k in range(4):
                A(yT[:, 2 * k:2 * k + 2].rearrange("p j e -> p (j e)"), bank(k), ACT.Copy).then_inc(sm("yT_init"), 1)
            act_e.wait_ge(sm("ld_wq"), 48)
            for m in range(3):
                A(wq[m][:], work[:, m, :], ACT.Abs, accum_out=wstat[:, 0, m:m + 1]).then_inc(sm("wsum_ready"), 1)
            act_e.wait_ge(sm("xT_ready"), 1)
            act_e.wait_ge(sm("act_const"), 2)
            for k in range(4):
                A(xThi[:].rearrange("p k t -> p (k t)")[:, k * 512:(k + 1) * 512], bank(k), ACT.Copy).then_inc(sm("xhi_ready"), 1)
            act_e.wait_ge(sm("lsub_ready"), 1)
            A(probs[:], left[:], ACT.Exp).then_inc(sm("pexp_ready"), 1)

            def split_hi(c, p):
                if p == 0:
                    act_e.wait_ge(sm(f"ld_raw{c % 2}"), 32 * (c // 2 + 1))
                if p == 0 and c >= 2:
                    act_e.wait_ge(sm("gu_ready"), 8 * (c - 1))
                if p == 6 and c >= 2:
                    act_e.wait_ge(sm("down_ready"), 8 * (c - 1))
                z = slice(p * WP, (p + 1) * WP)
                A(whi[c % 2][:, z], raw[c % 2][:, z], ACT.Copy).then_inc(sm("whi_done"), 1)

            def exp1(k):
                n, b = divmod(k, B)
                if k == 0:
                    act_e.wait_ge(sm("dA_zero"), 2)
                if k >= 2:
                    act_e.wait_ge(sm("scan1"), k - 1)
                for h in range(NH):
                    ins = A(dA1[:, k % 2, h, 1:], delta[:, h, b * L + 1:(b + 1) * L], ACT.Exp,
                            scale=Aneg[:, 1, h, n:n + 1])
                ins.then_inc(sm("exp1"), 1)

            for p in range(9):
                split_hi(0, p)
            exp1(0)
            for s in range(8 * NCH + 3):
                c, j = divmod(s, 8)
                if s < 8 * NCH:
                    act_e.wait_ge(sm("gu_ready"), s + 1)
                    if s >= 2:
                        act_e.wait_ge(sm("umul_done"), s - 1)
                    A(tg[:, s % 2], PS[:, s % 2, 0:CW], ACT.Tanh, scale=0.5).then_inc(sm("tanh_done"), 1)
                    if s % 2 == 0 and s // 2 + 1 < 64:
                        exp1(s // 2 + 1)
                    if c + 1 < NCH:
                        for p in parts(j):
                            split_hi(c + 1, p)
                if 2 <= s < 8 * NCH + 2:
                    r = s - 2
                    act_e.wait_ge(sm("tr_ready"), r + 1)
                    if r >= 2:
                        act_e.wait_ge(sm("down_ready"), r - 1)
                    A(aThi[:, r % 2], PS[:, 4, 0:CW], ACT.Copy).then_inc(sm("ahi_done"), 1)
            gate_silu(2, work[:, 0, :])
            act_e.wait_ge(sm("x3T_ready"), 1)
            for k in range(4):
                A(xT3[:].rearrange("p h t -> p (h t)")[:, k * 512:(k + 1) * 512], bank(k), ACT.Copy).then_inc(sm("xT3_done"), 1)
            act_e.wait_ge(sm("q1T_ready"), 1)
            A(q1T, PS[:, 0:2, :].rearrange("p k x -> p (k x)").bitcast(BF16), ACT.Copy).then_inc(sm("q1T_done"), 1)
            for t in range(NT + 1):
                if t < NT:
                    act_e.wait_ge(sm("ffn_gu"), t + 1)
                    if t >= 1:
                        act_e.wait_ge(sm("ffn_b"), t)
                    if t == 0:
                        act_e.wait_ge(sm("tok_ready"), 1)
                    A(fth, bank(0, 2), ACT.Tanh, scale=tok[:, 3, t:t + 1]).then_inc(sm("ffn_tanh"), 1)
                    act_e.wait_ge(sm("ffn_tr"), t + 1)
                    if t >= 2:
                        act_e.wait_ge(sm("ffn_had"), t - 1)
                    A(bT[:, t % 2].rearrange("p k t -> p (k t)"), bank(4, 2), ACT.Copy).then_inc(sm("ffn_bT"), 1)
                if t >= 1:
                    r = t - 1
                    act_e.wait_ge(sm("ffn_qtr"), r + 1)
                    A(qhT[:, r % 2].rearrange("p k t -> p (k t)"), PS[:, 4, :].bitcast(BF16), ACT.Copy).then_inc(sm("ffn_qhT"), 1)

        @block.tensor
        def _(pe):
            def front(ly):
                if ly == 0:
                    pe.wait_ge(sm("ld_ctx"), 16)
                    pe.wait_ge(sm("ld_w0"), 80)
                else:
                    pe.wait_ge(sm("x1_done"), 2)
                pe.wait_ge(sm("tap_ready"), ly + 1)
                for h in range(NH):
                    for q in range(2):
                        for k in range(DC):
                            ins = pe.matmul(PS[:, 2 * h + q, :], tapw[:, k, h * P:(h + 1) * P],
                                            ctxp[:, 2 * q:2 * q + 2, k:k + L], start=(k == 0), stop=(k == DC - 1))
                ins.then_inc(sm("front_pe"), 1)
                pe.wait_ge(sm("u_ready"), ly + 1)
                for q in range(2):
                    for h in range(NH):
                        pe.matmul(PS[0:104, 4 + q, :], xpw[:, h, 0, :], u[:, h, q * 512:(q + 1) * 512],
                                  start=(h == 0), stop=(h == NH - 1))
                for j in range(NT):
                    for h in range(NH):
                        ins = pe.matmul(PS[:, 6, j * 2 * DS:(j + 1) * 2 * DS], u[:, h, j * P:(j + 1) * P],
                                        xpw[:, h, 1, 0:2 * DS], start=(h == 0), stop=(h == NH - 1))
                ins.then_inc(sm("front_pe"), 1)
                pe.wait_ge(sm("dtlo_ready"), ly + 1)
                for h in range(NH):
                    for q in range(2):
                        ins = pe.matmul(PS[:, 2 * h + q, :], dtw[:, h * P:(h + 1) * P],
                                        dtlo[:, q * 512:(q + 1) * 512], start=True, stop=True)
                ins.then_inc(sm("front_pe"), 1)
                pe.wait_ge(sm("du_ready"), ly + 1)
                for j in range(NT):
                    for h in range(NH):
                        o = (j % 2) * DI + h * P
                        ins = pe.transpose(PS[:, 4 + j // 2, o:o + P], th_[:, h, j * P:(j + 1) * P], ident[:])
                ins.then_inc(sm("front_pe"), 1)
                if ly:
                    pe.wait_ge(sm("Du_ready"), 1)
                    for j in range(NT):
                        for h in range(NH):
                            o = (j % 2) * DI + h * P
                            ins = pe.transpose(PS[:, j // 2, o:o + P], ey_[:, h, j * P:(j + 1) * P], ident[:])
                    ins.then_inc(sm("front_pe"), 1)

            pe.wait_ge(sm("ld_const"), 16 * 8)
            front(0)

            def dbu0(k):
                pe.wait_ge(sm("bmul0"), k + 1)
                if k >= 2:
                    pe.wait_ge(sm("scan0"), k - 1)
                for h in range(NH):
                    for j in range(4):
                        ins = pe.transpose(PS[:, 2 * (k % 2) + h, j * P:(j + 1) * P],
                                           dBuT0[:, k % 2, j, h * P:(h + 1) * P], ident[:])
                ins.then_inc(sm("dbu0_ready"), 1)

            def cb0(k):
                bp, n = divmod(k, DS)
                if k >= 2:
                    pe.wait_ge(sm("cmul0"), k - 1)
                pe.matmul(PS[:, 4 + k % 2, :], sel[:, n, :], CS[:, bp * 512:(bp + 1) * 512],
                          start=True, stop=True).then_inc(sm("cb0_ready"), 1)

            def ysum0(k):
                bp, n = divmod(k, DS)
                pe.wait_ge(sm("cmul0"), k + 1)
                for h in range(NH):
                    ins = pe.matmul(PS[:, 6 + h, :], ident[:], prod0[:, k % 2, h], start=(n == 0), stop=(n == DS - 1))
                ins.then_inc(sm("ysum0"), 1)

            pe.wait_ge(sm("duT_ready"), 4)
            pe.wait_ge(sm("cs_ready"), 1)
            for bp in range(2):
                k0 = bp * DS
                dbu0(k0)
                cb0(k0)
                for n in range(DS):
                    k = k0 + n
                    if n + 1 < DS:
                        dbu0(k + 1)
                        cb0(k + 1)
                    if n == 0 and bp:
                        pe.wait_ge(sm("x1_done"), 1)
                    ysum0(k)
                pe.wait_ge(sm("y2_ready"), bp + 1)
                for j in range(4):
                    for h in range(NH):
                        o = (j % 2) * DI + h * P
                        ins = pe.transpose(PS[:, 6 + j // 2, o:o + P], h0[:, 1, h * 512 + j * P:h * 512 + (j + 1) * P], ident[:])
                ins.then_inc(sm("y2T"), 1)
            front(1)

            pe.wait_ge(sm("wsum_ready"), 3)
            pe.wait_ge(sm("xn_ready"), 1)
            pe.wait_ge(sm("yT_init"), 4)
            pe.matmul(PS[:, 7, 0:3], ones[:], wstat[:, 0, :], start=True, stop=True).then_inc(sm("wtot_ready"), 1)
            for j in range(NT):
                for k in range(2):
                    o = (j % 4) * P
                    ins = pe.transpose(PS[:, 2 * k + j // 4, o:o + P], sz[:, j, k * P:(k + 1) * P], ident[:])
            ins.then_inc(sm("xT_ready"), 1)
            pe.wait_ge(sm("xlo_ready"), 4)
            pe.wait_ge(sm("gwlo_ready"), 1)
            pairs = [(xw, gw) for xw in (xTlo, xThi) for gw in (gwlo, gwhi)]
            for j in range(NT):
                for i, (xw, gw) in enumerate(pairs):
                    for k in range(2):
                        ins = pe.matmul(PS[:, 5, j * E:(j + 1) * E], xw[:, k, j * P:(j + 1) * P], gw[:, k, :],
                                        start=(i == 0 and k == 0), stop=(i == 3 and k == 1))
            ins.then_inc(sm("logits_ready"), 1)

            def dbu1(k):
                pe.wait_ge(sm("bmul1"), k + 1)
                if k == 0:
                    pe.wait_ge(sm("wtot_read"), 1)
                if k >= 1:
                    pe.wait_ge(sm("scan1"), k)
                for h in range(NH):
                    for q in range(2):
                        o = h * L + q * P
                        ins = pe.transpose(PS[:, 6, o:o + P], dBuT1[:, k % 2, q, h * P:(h + 1) * P], ident[:])
                ins.then_inc(sm("dbu1_ready"), 1)

            def hT1(k):
                pe.wait_ge(sm("scan1"), k + 1)
                if k >= 1:
                    pe.wait_ge(sm("yacc1"), k)
                for q in range(2):
                    for h in range(NH):
                        o = h * L + q * P
                        z = q * DI + h * P
                        ins = pe.transpose(PS[:, 7, z:z + P], h1[:, k % 2, o:o + P], ident[:])
                ins.then_inc(sm("hT1_ready"), 1)

            def gate_up(s):
                c, j = divmod(s, 8)
                if j == 0:
                    pe.wait_ge(sm("wlo_done"), 9 * c + 6)
                if s >= 2:
                    pe.wait_ge(sm("umul_done"), s - 1)
                hi = whi[c % 2][:, 0:GUW].rearrange("p (k g f) -> p k g f", k=2, g=2)
                lo = wlo[c % 2][:, 0:GUW].rearrange("p (k g f) -> p k g f", k=2, g=2)
                for g in range(2):
                    n = 0
                    for xw, w in ((xTlo, hi), (xThi, lo), (xThi, hi)):
                        for k in range(2):
                            ins = pe.matmul(PS[:, 2 * g + s % 2, 0:CW], xw[:, k, j * P:(j + 1) * P], w[:, k, g, :],
                                            start=(n == 0), stop=(n == 5))
                            n += 1
                ins.then_inc(sm("gu_ready"), 1)

            def turn(s):
                pe.wait_ge(sm("wmul_done"), s + 1)
                if s >= 1:
                    pe.wait_ge(sm("alo_done"), s)
                for b in range(CB):
                    ins = pe.transpose(PS[:, 4, b * P:(b + 1) * P], actw[:, s % 3, b * P:(b + 1) * P], ident[:])
                ins.then_inc(sm("tr_ready"), 1)

            def down(s):
                c, j = divmod(s, 8)
                if j == 0:
                    pe.wait_ge(sm("wlo_done"), 9 * c + 9)
                pe.wait_ge(sm("alo_done"), s + 1)
                if s >= 1:
                    pe.wait_ge(sm("acc_done"), s)
                hi = whi[c % 2][:, GUW:].rearrange("p (k f) -> p k f", k=CB)
                lo = wlo[c % 2][:, GUW:].rearrange("p (k f) -> p k f", k=CB)
                n = 0
                for aw, w in ((aTlo, hi), (aThi, lo), (aThi, hi)):
                    for b in range(CB):
                        ins = pe.matmul(PS[:, 5, 0:D], aw[:, s % 2, b * P:(b + 1) * P],
                                        w[:, b, :], start=(n == 0), stop=(n == 8))
                        n += 1
                ins.then_inc(sm("down_ready"), 1)

            dbu1(0)
            pe.wait_ge(sm("comb_ready"), 1)
            for s in range(8 * NCH + 3):
                if s < 8 * NCH:
                    gate_up(s)
                if s >= 3:
                    down(s - 3)
                if 2 <= s < 8 * NCH + 2:
                    turn(s - 2)
                if s % 2 == 1 and s // 2 < 64:
                    hT1(s // 2)
                    if s // 2 + 1 < 64:
                        dbu1(s // 2 + 1)

            pe.wait_ge(sm("sz1_ready"), 1)
            for b in range(B):
                for q in range(2):
                    for h in range(NH):
                        o = q * DI + h * P
                        ins = pe.transpose(PS[:, b, o:o + P], sz[:, 2 * b + h, q * P:(q + 1) * P], ident[:])
            ins.then_inc(sm("szT_ready"), 1)

            pe.wait_ge(sm("xn3_ready"), 1)
            for j in range(NT):
                for k in range(2):
                    o = (j % 4) * P
                    ins = pe.transpose(PS[:, 2 * k + j // 4, o:o + P], sz[:, j, k * P:(k + 1) * P], ident[:])
            ins.then_inc(sm("x3T_ready"), 1)
            pe.wait_ge(sm("xT3_done"), 4)
            for j in range(NT):
                for k in range(2):
                    ins = pe.matmul(PS[:, 4 + j // 2, (j % 2) * D:(j % 2 + 1) * D], xT3[:, k, j * P:(j + 1) * P],
                                    had[:, k, :], start=(k == 0), stop=(k == 1))
            ins.then_inc(sm("had_ready"), 1)
            pe.wait_ge(sm("q1_ready"), 1)
            qT_ps = PS[:, 0:2, :].rearrange("p k x -> p (k x)").bitcast(BF16).rearrange("p (k t) -> p k t", k=2)
            for j in range(NT):
                for k in range(2):
                    ins = pe.transpose(qT_ps[:, k, j * P:(j + 1) * P], q1[:, j, k * P:(k + 1) * P], identb[:])
            ins.then_inc(sm("q1T_ready"), 1)
            pe.wait_ge(sm("q1T_done"), 1)
            wg = wq[0][:].rearrange("p (k f) -> p k f", k=2)
            wu = wq[1][:].rearrange("p (k f) -> p k f", k=2)
            wd = wq[2][:].rearrange("p (k f) -> p k f", k=HB)
            for t in range(NT + 1):
                if t < NT:
                    if t >= 1:
                        pe.wait_ge(sm("ffn_b"), t)
                    for g, w in enumerate((wg, wu)):
                        for q in range(2):
                            for k in range(2):
                                ins = pe.matmul(PS[:, 2 * g + q, :], q1T[:, k, t * P:(t + 1) * P],
                                                w[:, k, q * 512:(q + 1) * 512], start=(k == 0), stop=(k == 1))
                    ins.then_inc(sm("ffn_gu"), 1)
                    pe.wait_ge(sm("ffn_mix"), t + 1)
                    if t >= 2:
                        pe.wait_ge(sm("out_ready"), t - 1)
                    for k in range(HB):
                        ins = pe.transpose(PS[:, 4 + k // 4, (k % 4) * P:(k % 4 + 1) * P],
                                           fo[:, t % 2, k * P:(k + 1) * P], ident[:])
                    ins.then_inc(sm("ffn_tr"), 1)
                    pe.wait_ge(sm("ffn_bT"), t + 1)
                    if t >= 1:
                        pe.wait_ge(sm("ffn_qa"), t)
                    for g in range(4):
                        for k in range(2):
                            ins = pe.matmul(PS[:, 6 + g // 2, (g % 2) * D:(g % 2 + 1) * D], bT[:, t % 2, 2 * g + k, :],
                                            had[:, k, :], start=(k == 0), stop=(k == 1))
                    ins.then_inc(sm("ffn_had"), 1)
                if t >= 1:
                    r = t - 1
                    pe.wait_ge(sm("ffn_qh"), r + 1)
                    for k in range(HB):
                        ins = pe.transpose(PS[:, 4, :].bitcast(BF16)[:, k * P:(k + 1) * P],
                                           qh[:, r % 2, k * P:(k + 1) * P], identb[:])
                    ins.then_inc(sm("ffn_qtr"), 1)
                    pe.wait_ge(sm("ffn_qhT"), r + 1)
                    for k in range(HB):
                        ins = pe.matmul(PS[:, 5, 0:D], qhT[:, r % 2, k, :], wd[:, k, :], start=(k == 0), stop=(k == HB - 1))
                    ins.then_inc(sm("ffn_down"), 1)

        @block.vector
        def _(v):
            link = chain(v, "dve_own")

            def norm_stats(n, waits=()):
                for j in range(NT):
                    ins = v.bn_stats(stats[:, j], xs[:, j])
                link(ins)
                for j in range(NT):
                    ins = v.bn_aggr(mv[:, j], stats[:, j])
                link(ins)
                v.tensor_scalar(rstd[:], mv[:, :, 1], LN_EPS, None, ALU.add).then_inc(sm("var_ready"), 1)

            def normalise(n):
                v.wait_ge(sm("rstd_ready"), n)
                for j in range(NT):
                    ins = v.tensor_scalar(sz[:, j], xs[:, j], mv[:, j, 0:1], rstd[:, j:j + 1], ALU.subtract, ALU.mult)
                return ins

            def front(ly):
                v.wait_ge(sm("pre_u"), 2 * ly + 2)
                v.scalar_tensor_tensor(out=u[:], in0=th_, scalar=1.0, in1=w3_, op0=ALU.add, op1=ALU.mult).then_inc(sm("u_ready"), 1)
                v.wait_ge(sm("front_pe"), 4 * ly + 2)
                if ly:
                    v.wait_ge(sm("bmul0"), 2 * DS)
                v.tensor_copy(BCt[:].rearrange("p j c -> p (j c)"), PS[:, 6, 0:NT * 2 * DS]).then_inc(sm("bct_ready"), 1)
                if ly == 0:
                    v.wait_ge(sm("c1_ready"), 1)
                    link(v.tensor_tensor(R0, PS[0:80, 4:6, :].rearrange("p k x -> p (k x)"), CS[:], ALU.subtract))
                    v.tensor_copy(CS[32:64], R0[32:64])
                    link(v.tensor_copy(CS[64:80], R0[64:80]))
                    v.tensor_tensor(CS[64:80], R0[64:80], CS[64:80], ALU.subtract).then_inc(sm("cs_ready"), 1)
                for h in range(NH):
                    v.wait_ge(sm("sp_ready"), 2 * ly + h + 1)
                    link(v.tensor_scalar(th_[:, h], ey_[:, h], 1.0, -1.0, ALU.add, ALU.add))
                    v.tensor_tensor(w3_[:, h], lw_[:, h], w3_[:, h], ALU.add)
                    link(v.tensor_tensor(ey_[:, h], ey_[:, h], th_[:, h], ALU.subtract))
                    link(v.tensor_tensor(delta[:, h], w3_[:, h], ey_[:, h], ALU.add))
                    ins = v.tensor_tensor(th_[:, h], delta[:, h], u[:, h], ALU.mult)
                ins.then_inc(sm("du_ready"), 1)

            v.wait_ge(sm("ld_x"), 16)
            norm_stats(1)
            normalise(1).then_inc(sm("z_ready"), 1)
            front(0)
            v.wait_ge(sm("front_pe"), 4)
            v.memset(dA0.rearrange("p i h (b l) -> p i h b l", b=2)[:, :, :, :, 0:1], 0.0).then_inc(sm("dA_zero"), 1)
            v.wait_ge(sm("ztan_ready"), 1)
            link(v.scalar_tensor_tensor(out=szf, in0=ztan, scalar=1.0, in1=szf, op0=ALU.add, op1=ALU.mult))

            v.wait_ge(sm("act_const"), 2)
            v.tensor_tensor(gwlo[:], gwT[:], gwhi[:].bitcast(F32), ALU.subtract).then_inc(sm("gwlo_ready"), 1)

            def scan0(k):
                v.wait_ge(sm("exp0"), k + 1)
                v.wait_ge(sm("dbu0_ready"), k + 1)
                v.tensor_tensor_scan(h0[:, k % 2], dA0[:, k % 2].rearrange("p h t -> p (h t)"),
                                     bank(2 * (k % 2), 2), 0.0, ALU.mult, ALU.add).then_inc(sm("scan0"), 1)

            def cmul0(k):
                v.wait_ge(sm("scan0"), k + 1)
                v.wait_ge(sm("cb0_ready"), k + 1)
                if k >= 2:
                    v.wait_ge(sm("ysum0"), k - 1)
                v.tensor_tensor(prod0[:, k % 2], h0[:, k % 2].rearrange("p (h t) -> p h t", h=NH),
                                PS[:, 4 + k % 2:5 + k % 2, :].broadcast_to([P, NH, 512]), ALU.mult).then_inc(sm("cmul0"), 1)

            for bp in range(2):
                for n in range(DS + 1):
                    if n < DS:
                        scan0(bp * DS + n)
                    if n:
                        cmul0(bp * DS + n - 1)
                v.wait_ge(sm("ysum0"), (bp + 1) * DS)
                v.wait_ge(sm("cmul0"), (bp + 1) * DS)
                for h in range(NH):
                    link(v.scalar_tensor_tensor(out=h0[:, 0, h * 512:(h + 1) * 512], in0=u[:, h, bp * 512:(bp + 1) * 512],
                                                scalar=chan[:, 0, h, 2:3], in1=PS[:, 6 + h, :], op0=ALU.mult, op1=ALU.add))
                for h in range(NH):
                    ins = v.tensor_tensor(h0[:, 1, h * 512:(h + 1) * 512].rearrange("p (b l) -> p b l", b=2),
                                          h0[:, 0, h * 512:(h + 1) * 512].rearrange("p (b l) -> p b l", b=2),
                                          sz[:, 4 * bp + h:4 * bp + h + 3:2, :], ALU.mult)
                ins.then_inc(sm("y2_ready"), 1)
                v.wait_ge(sm("y2T"), bp + 1)
                xv = xs[:, 4 * bp:4 * bp + 4].rearrange("p j d -> p (j d)")
                v.scalar_tensor_tensor(out=xv, in0=bank(6, 2), scalar=hgates[:, 0:1], in1=xv,
                                       op0=ALU.mult, op1=ALU.add).then_inc(sm("x1_done"), 1)
            v.wait_ge(sm("x1_done"), 2)
            front(1)
            for h in range(NH):
                ins = v.tensor_scalar(ey_[:, h], u[:, h], chan[:, 1, h, 2:3], None, ALU.mult)
            ins.then_inc(sm("Du_ready"), 1)
            norm_stats(2)
            v.wait_ge(sm("Du_ready"), 1)
            v.memset(dA1[:, :, :, 0:1], 0.0).then_inc(sm("dA_zero"), 1)

            normalise(2).then_inc(sm("xn_ready"), 1)
            v.wait_ge(sm("wtot_ready"), 1)
            v.tensor_scalar(wstat[:, 1, :], PS[:, 7, 0:3], 1.0 / (HID * D), Q_EPS, ALU.mult, ALU.max).then_inc(sm("wtot_read"), 1)
            v.wait_ge(sm("wtot_read"), 1)
            v.tensor_scalar(wstat[:, 2, :], wstat[:, 1, :], 0.5, None, ALU.mult)
            link(v.tensor_scalar(wstat[:, 3, :], wstat[:, 1, :], -0.5, None, ALU.mult))
            for k in range(4):
                v.wait_ge(sm("xhi_ready"), k + 1)
                z = slice(k * 512, (k + 1) * 512)
                v.tensor_tensor(xTlo[:].rearrange("p k t -> p (k t)")[:, z], bank(k),
                                xThi[:].rearrange("p k t -> p (k t)")[:, z].bitcast(F32), ALU.subtract).then_inc(sm("xlo_ready"), 1)
            for m in range(3):
                link(v.tensor_scalar(wq[m][:], work[:, m, :], wstat[:, 3, m:m + 1], None, ALU.is_lt))
                v.scalar_tensor_tensor(out=wq[m][:], in0=work[:, m, :], scalar=wstat[:, 2, m:m + 1], in1=wq[m][:],
                                       op0=ALU.is_gt, op1=ALU.subtract).then_inc(sm("wq_done"), 1)
            v.wait_ge(sm("logits_ready"), 1)
            lg = PS[:, 5, :].rearrange("p (j e) -> p j e", j=NT)
            link(v.tensor_reduce(rsm[:, 0, :], lg, AX.X, ALU.max))
            v.tensor_tensor(left[:], lg, rsm[:, 0, :].unsqueeze(2).broadcast_to([P, NT, E]), ALU.subtract).then_inc(sm("lsub_ready"), 1)
            v.wait_ge(sm("pexp_ready"), 1)
            link(v.tensor_reduce(rsm[:, 1, :], probs[:], AX.X, ALU.add))
            link(v.reciprocal(rsm[:, 2, :], rsm[:, 1, :]))
            link(v.tensor_tensor(probs[:], probs[:], rsm[:, 2, :].unsqueeze(2).broadcast_to([P, NT, E]), ALU.mult))
            for j in range(NT):
                ins = v.max(top8[:, j], probs[:, j])
            link(ins)
            for j in range(NT):
                ins = v.match_replace(left[:, j], top8[:, j], probs[:, j], 0.0)
            link(ins)
            link(v.tensor_reduce(rsm[:, 0, :], top8[:], AX.X, ALU.add))
            link(v.scalar_tensor_tensor(out=rsm[:, 1, :], in0=rsm[:, 0, :], scalar=0.0, in1=rsm[:, 0, :], op0=ALU.is_equal, op1=ALU.add))
            link(v.reciprocal(rsm[:, 2, :], rsm[:, 1, :]))
            link(v.tensor_scalar(rsm[:, 3, :], rsm[:, 2, :], hgates[:, 2:3], None, ALU.mult))
            link(v.tensor_tensor(comb[:], probs[:], left[:], ALU.subtract))
            v.tensor_tensor(comb[:], comb[:], rsm[:, 3, :].unsqueeze(2).broadcast_to([P, NT, E]), ALU.mult).then_inc(sm("comb_ready"), 1)

            def yacc1(k):
                n, b = divmod(k, B)
                if k == 0:
                    v.wait_ge(sm("yT_init"), 4)
                if k >= 4:
                    v.wait_ge(sm("yacc1"), k - 3)
                v.wait_ge(sm("hT1_ready"), k + 1)
                for q in range(2):
                    j = 2 * b + q
                    ins = v.scalar_tensor_tensor(out=yT[:, j], in0=PS[:, 7, q * DI:(q + 1) * DI],
                                                 scalar=BCt[:, j, DS + n:DS + n + 1], in1=yT[:, j], op0=ALU.mult, op1=ALU.add)
                ins.then_inc(sm("yacc1"), 1)

            for s in range(8 * NCH + 3):
                if s < 8 * NCH:
                    v.wait_ge(sm("tanh_done"), s + 1)
                    v.scalar_tensor_tensor(out=ga[:, s % 2], in0=tg[:, s % 2], scalar=1.0, in1=PS[:, s % 2, 0:CW],
                                           op0=ALU.add, op1=ALU.mult).then_inc(sm("gated"), 1)
                if s % 2 == 0 and s // 2 < 64:
                    k = s // 2
                    v.wait_ge(sm("exp1"), k + 1)
                    v.wait_ge(sm("dbu1_ready"), k + 1)
                    v.tensor_tensor_scan(h1[:, k % 2], dA1[:, k % 2].rearrange("p h t -> p (h t)"), PS[:, 6, :],
                                         0.0, ALU.mult, ALU.add).then_inc(sm("scan1"), 1)
                if s < 8 * NCH:
                    v.wait_ge(sm("gated"), s + 1)
                    if s >= 3:
                        v.wait_ge(sm("wmul_done"), s - 2)
                    v.tensor_tensor(act[:, s % 3], ga[:, s % 2], PS[:, 2 + s % 2, 0:CW], ALU.mult).then_inc(sm("umul_done"), 1)
                if s % 2 == 0 and 0 <= s // 2 - 1 < 64:
                    yacc1(s // 2 - 1)
                if 2 <= s < 8 * NCH + 2:
                    r = s - 2
                    v.wait_ge(sm("ahi_done"), r + 1)
                    if r >= 2:
                        v.wait_ge(sm("down_ready"), r - 1)
                    v.tensor_tensor(aTlo[:, r % 2], PS[:, 4, 0:CW], aThi[:, r % 2].bitcast(F32), ALU.subtract).then_inc(sm("alo_done"), 1)
                if s >= 3:
                    r = s - 3
                    v.wait_ge(sm("down_ready"), r + 1)
                    if r >= 8:
                        v.wait_ge(sm("acc_done"), r - 7)
                    v.tensor_tensor(xs[:, r % 8], xs[:, r % 8], PS[:, 5, 0:D], ALU.add).then_inc(sm("acc_done"), 1)
            v.wait_ge(sm("acc_done"), 8 * NCH)
            v.wait_ge(sm("yacc1"), 64)

            norm_stats(3)
            normalise(3).then_inc(sm("z_ready"), 1)
            v.wait_ge(sm("ztan_ready"), 2)
            v.scalar_tensor_tensor(out=szf, in0=work[:, 0, :], scalar=1.0, in1=szf, op0=ALU.add, op1=ALU.mult).then_inc(sm("sz1_ready"), 1)
            v.wait_ge(sm("szT_ready"), 1)
            yf = yT[:].rearrange("p j d -> p (j d)")
            xf = xs[:].rearrange("p j d -> p (j d)")
            link(v.tensor_tensor(yf, yf, bank(0, 4), ALU.mult))
            link(v.scalar_tensor_tensor(out=xf, in0=yf, scalar=hgates[:, 1:2], in1=xf, op0=ALU.mult, op1=ALU.add))

            norm_stats(4)
            normalise(4).then_inc(sm("xn3_ready"), 1)
            v.wait_ge(sm("had_ready"), 1)
            hv = PS[:, 4:8, :].rearrange("p k (j d) -> p (k j) d", j=2)
            link(v.tensor_reduce(tok[:, 0, :], hv, AX.X, ALU.max, apply_absolute_value=True))
            link(v.tensor_scalar(tok[:, 1, :], tok[:, 0, :], Q_EPS, None, ALU.max))
            link(v.reciprocal(tok[:, 2, :], tok[:, 1, :]))
            link(v.tensor_scalar(tok[:, 2, :], tok[:, 2, :], 127.0, None, ALU.mult))
            for j in range(NT):
                ins = v.tensor_scalar(sz[:, j], hv[:, j], tok[:, 2, j:j + 1], 127.0, ALU.mult, ALU.min)
            link(ins)
            link(v.tensor_scalar(szf, szf, -128.0, ROUND, ALU.max, ALU.add))
            v.tensor_scalar(q1.rearrange("p j d -> p (j d)"), szf, -ROUND, None, ALU.add).then_inc(sm("q1_ready"), 1)
            link(v.tensor_scalar(tok[:, 3, :], tok[:, 1, :], wstat[:, 1, 0:1], 0.5 / 127, ALU.mult, ALU.mult))
            v.tensor_scalar(tok[:, 5, :], tok[:, 1, :], wstat[:, 1, 1:2], 0.5 / 127, ALU.mult, ALU.mult)
            v.tensor_scalar(tok[:, 6, 0:1], wstat[:, 1, 2:3], gates[:, 3:4], 1.0 / 127, ALU.mult, ALU.mult)
            link(v.tensor_copy(tok[:, 7, :], tok[:, 1, :]))
            v.tensor_tensor(tok[:, 4, :], tok[:, 3, :], tok[:, 5, :], ALU.mult).then_inc(sm("tok_ready"), 1)
            v.wait_ge(sm("tok_ready"), 1)

            def hidden(t):
                v.wait_ge(sm("ffn_tanh"), t + 1)
                link(v.scalar_tensor_tensor(out=fa, in0=fth, scalar=1.0, in1=bank(0, 2), op0=ALU.add, op1=ALU.mult))
                if t >= 2:
                    v.wait_ge(sm("ffn_mix"), t - 1)
                v.tensor_tensor(fb[:, t % 2], fa, bank(2, 2), ALU.mult).then_inc(sm("ffn_b"), 1)

            def quantise(r):
                v.wait_ge(sm("ffn_had"), r + 1)
                f = ft[:, r % 2]
                kf = tok[:, 4, r:r + 1]
                link(v.tensor_reduce(f[:, 0:1], bank(6, 2), AX.X, ALU.max, apply_absolute_value=True))
                link(v.tensor_scalar(f[:, 1:2], f[:, 0:1], kf, Q_EPS, ALU.mult, ALU.max))
                link(v.reciprocal(f[:, 2:3], f[:, 1:2]))
                link(v.tensor_scalar(f[:, 3:4], f[:, 2:3], kf, 127.0, ALU.mult, ALU.mult))
                link(v.tensor_scalar(f[:, 4:5], f[:, 1:2], tok[:, 6, 0:1], None, ALU.mult))
                v.tensor_scalar(fq, bank(6, 2), f[:, 3:4], 127.0, ALU.mult, ALU.min).then_inc(sm("ffn_qa"), 1)
                v.wait_ge(sm("ffn_qa"), r + 1)
                link(v.tensor_scalar(fq, fq, -128.0, ROUND, ALU.max, ALU.add))
                if r >= 2:
                    v.wait_ge(sm("ffn_qtr"), r - 1)
                v.tensor_scalar(qh[:, r % 2], fq, -ROUND, None, ALU.add).then_inc(sm("ffn_qh"), 1)

            def finish(r):
                v.wait_ge(sm("ffn_down"), r + 1)
                v.scalar_tensor_tensor(out=xs[:, r], in0=PS[:, 5, 0:D], scalar=ft[:, r % 2, 4:5], in1=xs[:, r],
                                       op0=ALU.mult, op1=ALU.add).then_inc(sm("out_ready"), 1)

            for t in range(NT + 2):
                if t < NT:
                    hidden(t)
                if t >= 2:
                    finish(t - 2)
                if 1 <= t <= NT:
                    quantise(t - 1)


def kernel(**inputs):
    import ml_dtypes
    import numpy as np
    import concourse.bacc as bacc
    from concourse.bass_utils import run_bass_kernel_spmd

    x = {k: np.asarray(v) for k, v in inputs.items()}
    arrays = {"x": x["x"], "ctxT": x["ctx_1024"].reshape(T, DM).T, "g_xattn": x["g_xattn"], "g_ffn": x["g_ffn"]}
    chan = []
    for ly in range(2):
        p = f"L{ly}_xattn_"
        arrays[f"L{ly}_inT"] = x[p + "in_proj_w"].T
        arrays[f"L{ly}_taps"] = x[p + "conv_w"].reshape(DI, DC).T
        w = x[p + "x_proj_w"].T
        dt, bc, c = w[:, :DR], w[:, DR:], w[:, DR + DS:]
        z = np.zeros_like(c)
        arrays[f"L{ly}_xpT"] = np.concatenate([c, z, c, z, c, z, dt], axis=1)
        arrays[f"L{ly}_bcT"] = bc
        arrays[f"L{ly}_dtT"] = x[p + "dt_proj_w"].T
        v = [x[p + n].reshape(DI, -1) for n in ("conv_b", "dt_proj_b", "D", "A_log")]
        chan.append(np.concatenate(v, axis=1).reshape(NH, P, 3 + DS))
    arrays["chan"] = np.stack(chan).transpose(2, 0, 1, 3)
    arrays["gateT"] = x["L0_ffn_gate_weight"].T
    gu = x["L0_ffn_gate_up_weights"].reshape(NCH, EC, D, 2, I)
    arrays["guT"] = gu.transpose(0, 2, 3, 1, 4).reshape(NCH, D, 2 * CW)
    arrays["dnT"] = x["L0_ffn_down_weights"].reshape(NCH, CW, D)
    arrays["wgT"], arrays["wuT"], arrays["wdT"] = (x[f"L1_ffn_w_{m}"].T for m in ("gate", "up", "down"))
    h = np.ones((1, 1), np.float32)
    while h.shape[0] < D:
        h = np.block([[h, h], [h, -h]])
    arrays["had"] = (h / 16).astype(np.float32)
    arrays["ident"] = np.eye(P, dtype=np.float32)
    arrays["identb"] = np.eye(P).astype(ml_dtypes.bfloat16)
    sel = np.zeros((80, DS, P), ml_dtypes.bfloat16)
    for i in range(3):
        for n in range(DS):
            sel[32 * i + n, n] = 1
    arrays["sel"] = sel
    arrays = {k: np.ascontiguousarray(v) for k, v in arrays.items()}

    nc = bacc.Bacc("TRN2", target_bir_lowering=False, num_devices=1)
    aps = {k: nc.dram_tensor(f"in_{k}", v.shape, mybir.dt.from_np(v.dtype), kind="ExternalInput").ap()
           for k, v in arrays.items()}
    out = nc.dram_tensor("out_0", (B, L, D), F32, kind="ExternalOutput").ap()
    flamingo_gated_block(nc, aps, out)
    r = run_bass_kernel_spmd(nc, [{f"in_{k}": v for k, v in arrays.items()}], core_ids=[0])
    return r.results[0]["out_0"]
```

```python
from contextlib import ExitStack

import concourse.bass as bass
from concourse import mybir

P = 128
F32 = mybir.dt.float32
F32R = mybir.dt.float32r
BF16 = mybir.dt.bfloat16
ALU = mybir.AluOpType
ACT = mybir.ActivationFunctionType
AX = mybir.AxisListType

B, L, D = 4, 256, 256
T = B * L
NT = T // P
DM = 128
DI = 256
NH = DI // P
DS = 16
DC = 4
DR = 8
LP = L + DC - 1
BC = 2 * DS
XP = 3 * BC + DR
E, I = 64, 96
TOPK = 8
EC = 4
CW = EC * I
CB = CW // P
NCH = E // EC
GUW = 2 * 2 * CW
DWW = CB * D
WP = 256
HID = 1024
HB = HID // P
LN_EPS = 1e-5
Q_EPS = 1e-5
ROUND = 12582912.0
HT = T // 2
U0 = 2 * DS
U1 = B * DS
STEPS = NCH * NT


def flamingo_gated_block(nc, a, out):
    ctx = ExitStack()
    with ctx:
        def sb(name, shape, dt=F32):
            return ctx.enter_context(nc.sbuf_tensor(name, shape, dt))

        PS = ctx.enter_context(nc.psum_tensor("banks", [P, 8, 512], F32))

        def bank(k, n=1):
            return PS[:, k:k + n, :].rearrange("p k x -> p (k x)")

        ident = sb("ident", [P, P])
        identb = sb("identb", [P, P], BF16)
        had = sb("had", [P, 2, D])
        sel = sb("sel", [3 * BC, BC, P], BF16)
        ones = sb("ones", [P, P])
        nhalf = sb("nhalf", [P, NT])
        gates_in = sb("gates_in", [P, 4])
        gates = sb("gates", [P, 4])
        hgates = sb("hgates", [P, 4])
        ctxp = sb("ctxp", [P, B, LP])
        inw = sb("inw", [P, 2, DI])
        xpw = sb("xpw", [P, 2, NH, XP])
        dtw = sb("dtw", [DR, 2, DI])
        chan = sb("chan", [P, 2, NH, 3 + DS])
        Aneg = sb("Aneg", [P, 2, NH, DS])
        hcb = sb("hcb", [P, 2, NH])
        xs = sb("xs", [P, NT, D])
        sz = sb("sz", [P, NT, D])
        stats = sb("stats", [P, NT, 6])
        mv = sb("mv", [P, NT, 2])
        rstd = sb("rstd", [P, NT])
        us = [sb(f"u{ly}", [P, NH, T]) for ly in range(2)]
        y1 = us[1]
        delta = sb("delta", [P, NH, T])
        du = sb("du", [P, NH, T])
        CS = [sb(f"CS{ly}", [3 * BC, T], BF16) for ly in range(2)]
        work = sb("work", [P, 4, 2048])
        raw = [sb(f"raw{i}", [P, GUW + DWW]) for i in range(2)]
        rt = sb("rt", [P, 4, NT, E])
        taps = [raw[0][:, ly * 1024:(ly + 1) * 1024].rearrange("p (k e) -> p k e", k=DC) for ly in range(2)]
        ztan = raw[1][:, 0:2048]
        slot = [work[:, i, :].rearrange("p (h t) -> p h t", h=NH) for i in range(4)]
        s_abs, s_exp, s_ln, s_relu = slot
        Bs = work[:, 0, 0:1024].rearrange("p (i t) -> p i t", i=2)
        yg = work[:, 0, 1024:2048].rearrange("p (h t) -> p h t", h=NH)
        dBu0 = work[:, 1, :].rearrange("p (i h t) -> p i h t", i=2, h=NH)
        h0 = work[:, 2, :].rearrange("p (i h t) -> p i h t", i=2, h=NH)
        prod0 = work[:, 3, :].rearrange("p (i h t) -> p i h t", i=2, h=NH)
        xThi = sb("xThi", [P, 2, T], F32R)
        xTlo = sb("xTlo", [P, 2, T], F32R)
        gwT = sb("gwT", [P, 2, E])
        gwhi = sb("gwhi", [P, 2, E], F32R)
        gwlo = sb("gwlo", [P, 2, E], F32R)
        probs, left, comb = rt[:, 0], rt[:, 1], rt[:, 2]
        top8 = sb("top8", [P, NT, TOPK])
        rsm = sb("rsm", [P, 4, NT])
        whi = [sb(f"whi{i}", [P, GUW + DWW], F32R) for i in range(2)]
        wlo = [sb(f"wlo{i}", [P, GUW + DWW], F32R) for i in range(2)]
        tg = work[:, 0, 0:2 * CW].rearrange("p (i f) -> p i f", i=2)
        ga = work[:, 0, 2 * CW:4 * CW].rearrange("p (i f) -> p i f", i=2)
        act = work[:, 1, 0:3 * CW].rearrange("p (i f) -> p i f", i=3)
        actw = work[:, 2, 0:3 * CW].rearrange("p (i f) -> p i f", i=3)
        aThi = sb("aThi", [P, 2, CW], F32R)
        aTlo = sb("aTlo", [P, 2, CW], F32R)
        dA1 = work[:, 3, 0:1024].rearrange("p (i h t) -> p i h t", i=2, h=NH)
        prod1 = work[:, 3, 1024:2048].rearrange("p (i h t) -> p i h t", i=2, h=NH)
        dBu1 = sb("dBu1", [P, NH, L])
        h1 = work[:, 2, 3 * CW:3 * CW + 512].rearrange("p (h t) -> p h t", h=NH)
        wq = [sb(f"wq{m}", [P, 2048], BF16) for m in range(3)]
        R0 = wq[0][:].bitcast(F32)[0:3 * BC]
        dtlo = wq[1][:].bitcast(F32)[0:DR]
        wstat = sb("wstat", [P, 4, 3])
        wstage = us[0][:].rearrange("p h t -> p (h t)")
        tok = sb("tok", [P, 8, NT])
        ft = sb("ft", [P, 3, 8])
        xT3 = delta
        dub = du[:].rearrange("p h t -> p (h t)").bitcast(BF16)
        q1 = dub[:, 0:NT * D].rearrange("p (j d) -> p j d", j=NT)
        q1T = dub[:, NT * D:].rearrange("p (k t) -> p k t", k=2)
        ub = us[0][:].rearrange("p h t -> p (h t)").bitcast(BF16)
        qh = ub[:, 0:2 * HID].rearrange("p (i f) -> p i f", i=2)
        qhT = ub[:, 2 * HID:4 * HID].rearrange("p (i k t) -> p i k t", i=2, k=HB)
        fth = work[:, 0, 0:HID]
        fa = work[:, 0, HID:]
        fb = work[:, 1, :].rearrange("p (i f) -> p i f", i=2)
        fo = work[:, 2, :].rearrange("p (i f) -> p i f", i=2)
        fm = work[:, 3, 0:HID]
        fq = work[:, 3, HID:]
        bT = raw[0][:, 0:2 * HID].rearrange("p (i k t) -> p i k t", i=2, k=HB)

        szf = sz[:].rearrange("p j d -> p (j d)")
        out_rows = out.rearrange("b l d -> (b l) d").rearrange("(j p) d -> p j d", p=P)
        x_rows = a["x"].rearrange("b l d -> (b l) d").rearrange("(j p) d -> p j d", p=P)

        S = {}

        def sm(name):
            if name not in S:
                S[name] = ctx.enter_context(nc.semaphore(name))
            return S[name]

        def chain(eng, name):
            s, n = sm(name), [0]

            def link(ins):
                n[0] += 1
                ins.then_inc(s, 1)
                eng.wait_ge(s, n[0])
            return link

        def parts(j):
            return [j] if j < 5 else [5, 6] if j == 5 else [j + 1]

        def tsl(q):
            return slice(q * HT, (q + 1) * HT)

        def xhalf(q):
            return slice(4 * q, 4 * q + 4)

        WQ_STEPS = {2 * (8 + 16 * m + i) + 1: (m, i) for m in range(3) for i in range(8)}
        block = ctx.enter_context(nc.Block())

        @block.sync
        def _(sp):
            sp.dma_start(ctxp[:], a["ctxT"]).then_inc(sm("ld_ctx"), 16)
            sp.dma_start(xpw[:, 0], a["L0_xpT"].rearrange("(h p) k -> p h k", p=P)).then_inc(sm("ld_w0"), 16)
            sp.dma_start(dtw[:, 0], a["L0_dtT"]).then_inc(sm("ld_w0"), 16)
            sp.dma_start(xs[:], x_rows).then_inc(sm("ld_x"), 16)
            lc = sm("ld_const")
            sp.dma_start(sel[:], a["sel"]).then_inc(lc, 16)
            sp.dma_start(ident[:], a["ident"]).then_inc(lc, 16)
            sp.dma_start(identb[:], a["identb"]).then_inc(lc, 16)
            sp.dma_start(gwT[:], a["gateT"].rearrange("(k p) e -> p k e", p=P)).then_inc(lc, 16)
            sp.dma_start(had[:], a["had"].rearrange("(k p) f -> p k f", p=P)).then_inc(lc, 16)
            sp.dma_start(xpw[:, 1], a["L1_xpT"].rearrange("(h p) k -> p h k", p=P)).then_inc(sm("ld_w1"), 16)
            sp.dma_start(dtw[:, 1], a["L1_dtT"]).then_inc(sm("ld_w1"), 16)

            names = ("wgT", "wuT", "wdT")

            def load_wq(m, to, s):
                sp.dma_start(to.rearrange("p (k f) -> p k f", k=(2, 2, HB)[m]),
                             a[names[m]].rearrange("(k p) f -> p k f", p=P)).then_inc(s, 16)

            sp.wait_ge(sm("conv_done1"), 2)
            sp.wait_ge(sm("u_ready1"), 2)
            load_wq(0, raw[0][:, 0:2048], sm("ld_wq"))
            for m in (1, 2):
                sp.wait_ge(sm("wsum_ready"), m)
                load_wq(m, raw[0][:, 0:2048], sm("ld_wq"))

            def load_chunk(c):
                if c == 0:
                    sp.wait_ge(sm("wsum_ready"), 3)
                if c == 1:
                    sp.wait_ge(sm("sz0_ready"), 1)
                if c >= 2:
                    sp.wait_ge(sm("wlo_done"), 9 * (c - 1))
                r = raw[c % 2]
                s = sm(f"ld_raw{c % 2}")
                sp.dma_start(r[:, 0:GUW].rearrange("p (k f) -> p k f", k=2),
                             a["guT"][c].rearrange("(k p) f -> p k f", p=P)).then_inc(s, 16)
                sp.dma_start(r[:, GUW:].rearrange("p (k f) -> p k f", k=CB),
                             a["dnT"][c].rearrange("(k p) f -> p k f", p=P)).then_inc(s, 16)

            for c in range(NCH):
                load_chunk(c)
                if c == 1:
                    sp.wait_ge(sm("x1_done"), 2)
                    load_wq(0, wstage, sm("ld_wq2"))
                if c in (7, 11):
                    m = 1 if c == 7 else 2
                    sp.wait_ge(sm("wq_done"), 8 * m)
                    load_wq(m, wstage, sm("ld_wq2"))
            for t in range(NT):
                sp.wait_ge(sm("out_ready"), t + 1)
                sp.dma_start(out_rows[:, t], xs[:, t]).then_inc(sm("stored"), 16)
            sp.wait_ge(sm("stored"), 16 * NT)

        @block.gpsimd
        def _(pool):
            link = chain(pool, "pool_own")
            pool.memset(nhalf[:], -0.5)
            pool.memset(ones[:], 1.0).then_inc(sm("ones_ready"), 1)
            pool.wait_ge(sm("ones_ready"), 1)

            def inverse_root(n):
                for q in range(2):
                    i = 2 * (n - 1) + q + 1
                    pool.wait_ge(sm("var_ready"), i)
                    pool.tensor_tensor(rstd[:, xhalf(q)], rstd[:, xhalf(q)], nhalf[:, xhalf(q)], ALU.pow
                                       ).then_inc(sm("rstd_ready"), 1)

            pool.wait_ge(sm("ld_taps1"), 32)
            pool.tensor_tensor(taps[1], taps[1], inw[:, 1:2, :].broadcast_to([P, DC, DI]), ALU.mult
                               ).then_inc(sm("tap_ready1"), 1)
            inverse_root(1)

            for k in range(U0):
                q = k // DS
                if k == 0:
                    pool.wait_ge(sm("du_ready0"), 2)
                pool.wait_ge(sm("Bs_ready"), k + 1)
                if k >= 2:
                    pool.wait_ge(sm("scan0"), k - 1)
                pool.tensor_tensor(dBu0[:, k % 2], du[:, :, tsl(q)],
                                   Bs[:, k % 2:k % 2 + 1, :].broadcast_to([P, NH, HT]), ALU.mult
                                   ).then_inc(sm("bmul0"), 1)
            inverse_root(2)

            def split_lo(c, p):
                pool.wait_ge(sm("whi_done"), 9 * c + p + 1)
                if p == 0 and c >= 2:
                    pool.wait_ge(sm("gu_ready"), NT * (c - 1))
                if p == 6 and c >= 2:
                    pool.wait_ge(sm("down_ready"), NT * (c - 1))
                z = slice(p * WP, (p + 1) * WP)
                pool.tensor_tensor(wlo[c % 2][:, z], raw[c % 2][:, z], whi[c % 2][:, z].bitcast(F32),
                                   ALU.subtract).then_inc(sm("wlo_done"), 1)

            def yacc1(k):
                b = k % B
                pool.wait_ge(sm("cmul1"), k + 1)
                if k >= B:
                    pool.wait_ge(sm("yacc1"), k - B + 1)
                ys = y1[:, :, b * L:(b + 1) * L]
                pool.tensor_tensor(ys, ys, prod1[:, k % 2], ALU.add).then_inc(sm("yacc1"), 1)

            for p in range(9):
                split_lo(0, p)
            for s in range(STEPS):
                c, j = divmod(s, NT)
                if c + 1 < NCH:
                    for p in parts(j):
                        split_lo(c + 1, p)
                if s % 2 == 0 and s >= 2:
                    yacc1(s // 2 - 1)
                if s == 0:
                    pool.wait_ge(sm("comb_ready"), 1)
                pool.wait_ge(sm("umul_done"), s + 1)
                if s >= 3:
                    pool.wait_ge(sm("tr_ready"), s - 2)
                pool.tensor_tensor(actw[:, s % 3].rearrange("p (e f) -> p e f", e=EC),
                                   act[:, s % 3].rearrange("p (e f) -> p e f", e=EC),
                                   comb[:, j, EC * c:EC * c + EC].unsqueeze(2).broadcast_to([P, EC, I]),
                                   ALU.mult).then_inc(sm("wmul_done"), 1)
            yacc1(U1 - 1)
            inverse_root(3)
            inverse_root(4)
            for t in range(NT):
                pool.wait_ge(sm("ffn_b"), t + 1)
                if t >= 2:
                    pool.wait_ge(sm("ffn_tr"), t - 1)
                src = fb[:, t % 2].rearrange("p (x y r) -> p x y r", x=2, y=2)
                mid = fm.rearrange("p (x y r) -> p x y r", x=2, y=2)
                dst = fo[:, t % 2].rearrange("p (x y r) -> p x y r", x=2, y=2)
                pool.tensor_tensor(mid[:, :, 0], src[:, :, 0], src[:, :, 1], ALU.add)
                link(pool.tensor_tensor(mid[:, :, 1], src[:, :, 0], src[:, :, 1], ALU.subtract))
                pool.tensor_tensor(dst[:, 0], mid[:, 0], mid[:, 1], ALU.add)
                pool.tensor_tensor(dst[:, 1], mid[:, 0], mid[:, 1], ALU.subtract).then_inc(sm("ffn_mix"), 1)
                pool.wait_ge(sm("ffn_mix"), t + 1)

        @block.scalar
        def _(act_e):
            link = chain(act_e, "act_own")
            A = nc.scalar.activation
            for ly in range(2):
                lt = sm(f"ld_taps{ly}")
                act_e.dma_start(inw[:, ly], a[f"L{ly}_inT"]).then_inc(lt, 16)
                act_e.dma_start(taps[ly], a[f"L{ly}_taps"].unsqueeze(0).broadcast_to([P, DC, DI])).then_inc(lt, 16)
                if ly == 0:
                    act_e.dma_start(chan[:], a["chan"]).then_inc(sm("ld_chan"), 16)
            for i, g in enumerate(("g_xattn", "g_ffn")):
                act_e.dma_start(gates_in[:, 2 * i:2 * i + 2], a[g].unsqueeze(0).broadcast_to([P, 2])).then_inc(sm("ld_gates"), 16)
            act_e.wait_ge(sm("ld_chan"), 16)
            A(hcb[:], chan[:, :, :, 0], ACT.Copy, scale=0.5).then_inc(sm("hcb_ready"), 1)
            act_e.wait_ge(sm("hcb_ready"), 1)
            link(A(Aneg[:], chan[:, :, :, 3:], ACT.Exp))
            link(A(Aneg[:], Aneg[:], ACT.Copy, scale=-1.0))

            def before_u(ly, q, th, k):
                act_e.wait_ge(sm(f"conv_done{ly}"), q + 1)
                for h in range(NH):
                    A(th[:, h], bank(k + h), ACT.Tanh, scale=0.5, bias=hcb[:, ly, h:h + 1])
                    ins = A(us[ly][:, h, tsl(q)], bank(k + h), ACT.Identity, scale=0.5, bias=hcb[:, ly, h:h + 1])
                ins.then_inc(sm(f"pre_u{ly}"), 1)

            def evacuate_proj(ly, q, k):
                act_e.wait_ge(sm(f"proj_done{ly}"), q + 1)
                A(dtlo[:, tsl(q)], PS[3 * BC:XP, k + q, :], ACT.Copy).then_inc(sm(f"dtlo_ready{ly}"), 1)
                A(CS[ly][:, tsl(q)], PS[0:3 * BC, k + q, :], ACT.Copy).then_inc(sm(f"bc1_ready{ly}"), 1)

            def softplus(ly, q, k):
                act_e.wait_ge(sm(f"pre_done{ly}"), q + 1)
                for h in range(NH):
                    bias = chan[:, ly, h, 1:2]
                    A(s_abs[:, h, tsl(q)], bank(k + h), ACT.Abs, bias=bias)
                    ins = A(s_relu[:, h, tsl(q)], bank(k + h), ACT.Relu, bias=bias)
                ins.then_inc(sm(f"pre_read{ly}"), 1)
                act_e.wait_ge(sm(f"pre_read{ly}"), q + 1)
                link(A(s_exp[:, :, tsl(q)], s_abs[:, :, tsl(q)], ACT.Exp, scale=-1.0))
                A(s_ln[:, :, tsl(q)], s_exp[:, :, tsl(q)], ACT.Ln, bias=1.0).then_inc(sm(f"sp_ready{ly}"), 1)

            for q in range(2):
                before_u(0, q, slot[0][:, :, tsl(q)], 2 * q)
            for q in range(2):
                evacuate_proj(0, q, 4)
            for q in range(2):
                softplus(0, q, 2 * q)
            before_u(1, 0, raw[0][:, 0:1024].rearrange("p (h t) -> p h t", h=NH), 6)
            before_u(1, 1, rt[:, 0:2].rearrange("p i j e -> p i (j e)"), 4)
            act_e.wait_ge(sm("ld_gates"), 32)
            link(A(gates[:], gates_in[:], ACT.Tanh))
            A(hgates[:], gates[:], ACT.Copy, scale=0.5).then_inc(sm("gates_ready"), 1)
            act_e.wait_ge(sm("z_ready"), 2)
            A(ztan, szf, ACT.Tanh, scale=0.5).then_inc(sm("ztan_ready"), 1)
            act_e.wait_ge(sm("ld_const"), 80)
            A(gwhi[:], gwT[:], ACT.Copy).then_inc(sm("gwhi_ready"), 1)

            def copy_B(k):
                act_e.wait_ge(sm("bb0_ready"), k + 1)
                if k >= 2:
                    act_e.wait_ge(sm("bmul0"), k - 1)
                A(Bs[:, k % 2], bank(4), ACT.Copy).then_inc(sm("Bs_ready"), 1)

            act_e.wait_ge(sm("du_ready0"), 2)
            act_e.wait_ge(sm("dA_zero"), 1)
            copy_B(0)
            copy_B(1)
            for k in range(U0):
                q, n = divmod(k, DS)
                if k >= 2:
                    act_e.wait_ge(sm("scan0"), k - 1)
                for h in range(NH):
                    src = delta[:, h, tsl(q)].rearrange("p (b l) -> p b l", b=2)[:, :, 1:]
                    dst = bank(2 * (k % 2) + h).rearrange("p (b l) -> p b l", b=2)[:, :, 1:]
                    ins = A(dst, src, ACT.Exp, scale=Aneg[:, 0, h, n:n + 1])
                ins.then_inc(sm("exp0"), 1)
                if k + 2 < U0:
                    copy_B(k + 2)
                if k in (8, 16, 24):
                    m = k // 8 - 1
                    act_e.wait_ge(sm("ld_wq"), 16 * (m + 1))
                    A(wq[2][:], raw[0][:, 0:2048], ACT.Abs, accum_out=wstat[:, 0, m:m + 1]).then_inc(sm("wsum_ready"), 1)
            for q in range(2):
                evacuate_proj(1, q, 4)
            act_e.wait_ge(sm("x1_done"), 2)
            for q in range(2):
                softplus(1, q, 2 * q)
            for k in range(4):
                act_e.wait_ge(sm("xT_ready"), k + 1)
                A(xThi[:, k % 2, tsl(k // 2)], bank(4 + k), ACT.Copy).then_inc(sm("xhi_ready"), 1)
            act_e.wait_ge(sm("lsub_ready"), 1)
            A(probs, left, ACT.Exp).then_inc(sm("pexp_ready"), 1)

            def split_hi(c, p):
                if p == 0:
                    act_e.wait_ge(sm(f"ld_raw{c % 2}"), 32 * (c // 2 + 1))
                if p == 0 and c >= 2:
                    act_e.wait_ge(sm("gu_ready"), NT * (c - 1))
                if p == 6 and c >= 2:
                    act_e.wait_ge(sm("down_ready"), NT * (c - 1))
                z = slice(p * WP, (p + 1) * WP)
                A(whi[c % 2][:, z], raw[c % 2][:, z], ACT.Copy).then_inc(sm("whi_done"), 1)

            def exp1(k):
                n, b = divmod(k, B)
                if k == 0:
                    act_e.wait_ge(sm("dA_zero"), 2)
                    act_e.wait_ge(sm("du_ready1"), 2)
                if k >= 2:
                    act_e.wait_ge(sm("scan1"), k - 1)
                for h in range(NH):
                    ins = A(dA1[:, k % 2, h, 1:], delta[:, h, b * L + 1:(b + 1) * L], ACT.Exp,
                            scale=Aneg[:, 1, h, n:n + 1])
                ins.then_inc(sm("exp1"), 1)

            for p in range(9):
                split_hi(0, p)
            exp1(0)
            for s in range(STEPS + 3):
                c, j = divmod(s, NT)
                if s < STEPS:
                    act_e.wait_ge(sm("gu_ready"), s + 1)
                    if s >= 2:
                        act_e.wait_ge(sm("umul_done"), s - 1)
                    A(tg[:, s % 2], PS[:, s % 2, 0:CW], ACT.Tanh, scale=0.5).then_inc(sm("tanh_done"), 1)
                if 2 <= s < STEPS + 2:
                    r = s - 2
                    act_e.wait_ge(sm("tr_ready"), r + 1)
                    if r >= 2:
                        act_e.wait_ge(sm("down_ready"), r - 1)
                    A(aThi[:, r % 2], PS[:, 4, 0:CW], ACT.Copy).then_inc(sm("ahi_done"), 1)
                if s < STEPS:
                    if s % 2 == 0 and s // 2 + 1 < U1:
                        exp1(s // 2 + 1)
                    if c + 1 < NCH:
                        for p in parts(j):
                            split_hi(c + 1, p)
            for q in range(2):
                act_e.wait_ge(sm("z_ready"), 3 + q)
                A(work[:, 0, q * 1024:(q + 1) * 1024], szf[:, q * 1024:(q + 1) * 1024], ACT.Tanh, scale=0.5
                  ).then_inc(sm("ztan_ready"), 1)

            for k in range(4):
                act_e.wait_ge(sm("x3T_ready"), k + 1)
                A(xT3[:, k % 2, tsl(k // 2)], bank(k), ACT.Copy).then_inc(sm("xT3_done"), 1)
            for q in range(2):
                act_e.wait_ge(sm("q1T_ready"), q + 1)
                A(q1T[:, :, tsl(q)], PS[:, q, :].bitcast(BF16).rearrange("p (k t) -> p k t", k=2), ACT.Copy
                  ).then_inc(sm("q1T_done"), 1)
            act_e.wait_ge(sm("tok_ready"), 1)
            for t in range(NT + 2):
                if 1 <= t <= NT:
                    r = t - 1
                    act_e.wait_ge(sm("ffn_tr"), r + 1)
                    if r >= 2:
                        act_e.wait_ge(sm("ffn_had"), r - 1)
                    A(bT[:, r % 2].rearrange("p k t -> p (k t)"), bank(4, 2), ACT.Copy).then_inc(sm("ffn_bT"), 1)
                if t < NT:
                    act_e.wait_ge(sm("ffn_gu"), t + 1)
                    if t >= 1:
                        act_e.wait_ge(sm("ffn_b"), t)
                    A(fth, bank(0, 2), ACT.Tanh, scale=tok[:, 3, t:t + 1]).then_inc(sm("ffn_tanh"), 1)
                if t >= 2:
                    r = t - 2
                    act_e.wait_ge(sm("ffn_qtr"), r + 1)
                    if r >= 2:
                        act_e.wait_ge(sm("ffn_down"), r - 1)
                    A(qhT[:, r % 2].rearrange("p k t -> p (k t)"), PS[:, 4, :].bitcast(BF16), ACT.Copy).then_inc(sm("ffn_qhT"), 1)
                if 1 <= t <= NT:
                    r = t - 1
                    act_e.wait_ge(sm("ffn_scales"), r + 1)
                    if r >= 1:
                        act_e.wait_ge(sm("ffn_qh"), r)
                    A(fq, bank(6, 2), ACT.Copy, scale=ft[:, r % 3, 3:4]).then_inc(sm("ffn_qa"), 1)

        @block.tensor
        def _(pe):
            def conv(ly, q, k):
                for h in range(NH):
                    for c in range(DC):
                        ins = pe.matmul(bank(k + h), taps[ly][:, c, h * P:(h + 1) * P],
                                        ctxp[:, 2 * q:2 * q + 2, c:c + L], start=(c == 0), stop=(c == DC - 1))
                ins.then_inc(sm(f"conv_done{ly}"), 1)

            def proj(ly, q, k):
                pe.wait_ge(sm(f"u_ready{ly}"), q + 1)
                for h in range(NH):
                    ins = pe.matmul(PS[0:XP, k + q, :], xpw[:, ly, h, :], us[ly][:, h, tsl(q)],
                                    start=(h == 0), stop=(h == NH - 1))
                ins.then_inc(sm(f"proj_done{ly}"), 1)

            def dt_proj(ly, q, k):
                pe.wait_ge(sm(f"dtlo_ready{ly}"), q + 1)
                for h in range(NH):
                    ins = pe.matmul(bank(k + h), dtw[:, ly, h * P:(h + 1) * P], dtlo[:, tsl(q)], start=True, stop=True)
                ins.then_inc(sm(f"pre_done{ly}"), 1)

            pe.wait_ge(sm("ld_ctx"), 16)
            pe.wait_ge(sm("tap_ready0"), 1)
            conv(0, 0, 0)
            conv(0, 1, 2)
            pe.wait_ge(sm("ld_w0"), 32)
            proj(0, 0, 4)
            proj(0, 1, 4)
            dt_proj(0, 0, 0)
            dt_proj(0, 1, 2)
            pe.wait_ge(sm("tap_ready1"), 1)
            conv(1, 0, 6)
            pe.wait_ge(sm("bc_ready0"), 2)
            conv(1, 1, 4)

            def bb0(k):
                q, n = divmod(k, DS)
                if k == 0:
                    pe.wait_ge(sm("pre_u1"), 2)
                if k >= 1:
                    pe.wait_ge(sm("Bs_ready"), k)
                pe.matmul(bank(4), sel[:, n, :], CS[0][:, tsl(q)], start=True, stop=True).then_inc(sm("bb0_ready"), 1)

            def cb0(k):
                q, n = divmod(k, DS)
                if k >= 1:
                    pe.wait_ge(sm("cmul0"), k)
                pe.matmul(bank(5), sel[:, DS + n, :], CS[0][:, tsl(q)], start=True, stop=True).then_inc(sm("cb0_ready"), 1)

            def ysum0(k):
                q, n = divmod(k, DS)
                if k == DS:
                    pe.wait_ge(sm("x1_done"), 1)
                pe.wait_ge(sm("cmul0"), k + 1)
                for h in range(NH):
                    ins = pe.matmul(bank(6 + h), ident[:], prod0[:, k % 2, h], start=(n == 0), stop=(n == DS - 1))
                ins.then_inc(sm("ysum0"), 1)

            def turn_y0(q):
                pe.wait_ge(sm("yg_ready"), q + 1)
                for j in range(4):
                    for h in range(NH):
                        o = (j % 2) * DI + h * P
                        ins = pe.transpose(PS[:, 6 + j // 2, o:o + P], yg[:, h, j * P:(j + 1) * P], ident[:])
                ins.then_inc(sm("y0T_ready"), 1)

            pe.wait_ge(sm("ld_const"), 80)
            for k in range(3):
                bb0(k)
            for k in range(U0 + 1):
                if k + 3 < U0:
                    bb0(k + 3)
                if k < U0:
                    cb0(k)
                if k >= 1:
                    ysum0(k - 1)
                if k == DS:
                    turn_y0(0)
            pe.wait_ge(sm("ld_w1"), 32)
            proj(1, 0, 4)
            proj(1, 1, 4)
            turn_y0(1)
            dt_proj(1, 0, 0)
            dt_proj(1, 1, 2)

            for k in range(4):
                pe.wait_ge(sm("xn_ready"), k // 2 + 1)
                if k == 0:
                    pe.wait_ge(sm("bc_ready1"), 2)
                    pe.wait_ge(sm("x1_done"), 2)
                for j in range(4):
                    ins = pe.transpose(PS[:, 4 + k, j * P:(j + 1) * P],
                                       sz[:, 4 * (k // 2) + j, (k % 2) * P:(k % 2 + 1) * P], ident[:])
                ins.then_inc(sm("xT_ready"), 1)
            pe.wait_ge(sm("wsum_ready"), 3)
            pe.wait_ge(sm("ones_ready"), 1)
            pe.wait_ge(sm("pre_read1"), 2)
            pe.matmul(PS[:, 1, 0:3], ones[:], wstat[:, 0, :], start=True, stop=True).then_inc(sm("wtot_ready"), 1)
            pe.wait_ge(sm("xlo_ready"), 4)
            pe.wait_ge(sm("gwlo_ready"), 1)
            pairs = [(xw, gw) for xw in (xTlo, xThi) for gw in (gwlo, gwhi)]
            for j in range(NT):
                for i, (xw, gw) in enumerate(pairs):
                    for k in range(2):
                        ins = pe.matmul(PS[:, 0, j * E:(j + 1) * E], xw[:, k, j * P:(j + 1) * P], gw[:, k, :],
                                        start=(i == 0 and k == 0), stop=(i == 3 and k == 1))
            ins.then_inc(sm("logits_ready"), 1)

            def bc1(k):
                n, b = divmod(k, B)
                if k == 0:
                    pe.wait_ge(sm("bc_ready1"), 2)
                if k >= 2:
                    pe.wait_ge(sm("cmul1"), k - 1)
                for i in range(2):
                    ins = pe.matmul(PS[:, 6 + k % 2, i * L:(i + 1) * L], sel[:, i * DS + n, :],
                                    CS[1][:, b * L:(b + 1) * L], start=True, stop=True)
                ins.then_inc(sm("bc1_done"), 1)

            def gate_up(s):
                c, j = divmod(s, NT)
                if j == 0:
                    pe.wait_ge(sm("wlo_done"), 9 * c + 6)
                if s >= 2:
                    pe.wait_ge(sm("umul_done"), s - 1)
                hi = whi[c % 2][:, 0:GUW].rearrange("p (k g f) -> p k g f", k=2, g=2)
                lo = wlo[c % 2][:, 0:GUW].rearrange("p (k g f) -> p k g f", k=2, g=2)
                for g in range(2):
                    n = 0
                    for xw, w in ((xTlo, hi), (xThi, lo), (xThi, hi)):
                        for k in range(2):
                            ins = pe.matmul(PS[:, 2 * g + s % 2, 0:CW], xw[:, k, j * P:(j + 1) * P], w[:, k, g, :],
                                            start=(n == 0), stop=(n == 5))
                            n += 1
                ins.then_inc(sm("gu_ready"), 1)

            def turn(s):
                pe.wait_ge(sm("wmul_done"), s + 1)
                if s >= 1:
                    pe.wait_ge(sm("alo_done"), s)
                for b in range(CB):
                    ins = pe.transpose(PS[:, 4, b * P:(b + 1) * P], actw[:, s % 3, b * P:(b + 1) * P], ident[:])
                ins.then_inc(sm("tr_ready"), 1)

            def down(s):
                c, j = divmod(s, NT)
                if j == 0:
                    pe.wait_ge(sm("wlo_done"), 9 * c + 9)
                pe.wait_ge(sm("alo_done"), s + 1)
                if s >= 1:
                    pe.wait_ge(sm("acc_done"), s)
                hi = whi[c % 2][:, GUW:].rearrange("p (k f) -> p k f", k=CB)
                lo = wlo[c % 2][:, GUW:].rearrange("p (k f) -> p k f", k=CB)
                n = 0
                for aw, w in ((aTlo, hi), (aThi, lo), (aThi, hi)):
                    for b in range(CB):
                        ins = pe.matmul(PS[:, 5, 0:D], aw[:, s % 2, b * P:(b + 1) * P],
                                        w[:, b, :], start=(n == 0), stop=(n == 8))
                        n += 1
                ins.then_inc(sm("down_ready"), 1)

            bc1(0)
            pe.wait_ge(sm("comb_ready"), 1)
            for s in range(STEPS + 3):
                if s < STEPS:
                    gate_up(s)
                if s >= 3:
                    down(s - 3)
                if 2 <= s < STEPS + 2:
                    turn(s - 2)
                if s % 2 == 0 and s // 2 + 1 < U1:
                    bc1(s // 2 + 1)

            for q in range(2):
                pe.wait_ge(sm("yz_ready"), q + 1)
                for j in range(4 * q, 4 * q + 4):
                    for h in range(NH):
                        o = (j % 2) * DI + h * P
                        ins = pe.transpose(PS[:, j // 2, o:o + P], y1[:, h, j * P:(j + 1) * P], ident[:])
                ins.then_inc(sm("y1T_ready"), 1)

            for k in range(4):
                pe.wait_ge(sm("xn3_ready"), k // 2 + 1)
                if k == 0:
                    pe.wait_ge(sm("x3_done"), 2)
                for j in range(4):
                    ins = pe.transpose(PS[:, k, j * P:(j + 1) * P],
                                       sz[:, 4 * (k // 2) + j, (k % 2) * P:(k % 2 + 1) * P], ident[:])
                ins.then_inc(sm("x3T_ready"), 1)
            for q in range(2):
                pe.wait_ge(sm("xT3_done"), 2 * q + 2)
                for j in range(4 * q, 4 * q + 4):
                    for k in range(2):
                        ins = pe.matmul(PS[:, 4 + j // 2, (j % 2) * D:(j % 2 + 1) * D], xT3[:, k, j * P:(j + 1) * P],
                                        had[:, k, :], start=(k == 0), stop=(k == 1))
                ins.then_inc(sm("had_ready"), 1)
            for q in range(2):
                pe.wait_ge(sm("q1_ready"), q + 1)
                for j in range(4):
                    for k in range(2):
                        ins = pe.transpose(PS[:, q, :].bitcast(BF16)[:, k * HT + j * P:k * HT + (j + 1) * P],
                                           q1[:, 4 * q + j, k * P:(k + 1) * P], identb[:])
                ins.then_inc(sm("q1T_ready"), 1)
            pe.wait_ge(sm("q1T_done"), 2)
            wg = wq[0][:].rearrange("p (k f) -> p k f", k=2)
            wu = wq[1][:].rearrange("p (k f) -> p k f", k=2)
            wd = wq[2][:].rearrange("p (k f) -> p k f", k=HB)
            for t in range(NT + 2):
                if 1 <= t <= NT:
                    r = t - 1
                    pe.wait_ge(sm("ffn_mix"), r + 1)
                    if r >= 2:
                        pe.wait_ge(sm("out_ready"), r - 1)
                    for k in range(HB):
                        ins = pe.transpose(PS[:, 4 + k // 4, (k % 4) * P:(k % 4 + 1) * P],
                                           fo[:, r % 2, k * P:(k + 1) * P], ident[:])
                    ins.then_inc(sm("ffn_tr"), 1)
                if t < NT:
                    if t >= 1:
                        pe.wait_ge(sm("ffn_b"), t)
                    for g, w in enumerate((wg, wu)):
                        for q in range(2):
                            for k in range(2):
                                ins = pe.matmul(PS[:, 2 * g + q, :], q1T[:, k, t * P:(t + 1) * P],
                                                w[:, k, q * 512:(q + 1) * 512], start=(k == 0), stop=(k == 1))
                    ins.then_inc(sm("ffn_gu"), 1)
                if t >= 2:
                    r = t - 2
                    pe.wait_ge(sm("ffn_qh"), r + 1)
                    pe.wait_ge(sm("ffn_bT"), min(r + 2, NT))
                    for k in range(HB):
                        ins = pe.transpose(PS[:, 4, :].bitcast(BF16)[:, k * P:(k + 1) * P],
                                           qh[:, r % 2, k * P:(k + 1) * P], identb[:])
                    ins.then_inc(sm("ffn_qtr"), 1)
                if 1 <= t <= NT:
                    r = t - 1
                    pe.wait_ge(sm("ffn_bT"), r + 1)
                    if r >= 1:
                        pe.wait_ge(sm("ffn_qa"), r)
                    for g in range(4):
                        for k in range(2):
                            ins = pe.matmul(PS[:, 6 + g // 2, (g % 2) * D:(g % 2 + 1) * D], bT[:, r % 2, 2 * g + k, :],
                                            had[:, k, :], start=(k == 0), stop=(k == 1))
                    ins.then_inc(sm("ffn_had"), 1)
                if t >= 2:
                    r = t - 2
                    if r >= 1:
                        pe.wait_ge(sm("out_ready"), r)
                    pe.wait_ge(sm("ffn_qhT"), r + 1)
                    for k in range(HB):
                        ins = pe.matmul(PS[:, 5, 0:D], qhT[:, r % 2, k, :], wd[:, k, :], start=(k == 0), stop=(k == HB - 1))
                    ins.then_inc(sm("ffn_down"), 1)

        @block.vector
        def _(v):
            link = chain(v, "dve_own")

            def norm_stats(q):
                z = xhalf(q)
                for j in range(z.start, z.stop):
                    ins = v.bn_stats(stats[:, j], xs[:, j])
                link(ins)
                for j in range(z.start, z.stop):
                    ins = v.bn_aggr(mv[:, j], stats[:, j])
                link(ins)
                v.tensor_scalar(rstd[:, z], mv[:, z, 1], LN_EPS, None, ALU.add).then_inc(sm("var_ready"), 1)

            def normalise(n, q):
                v.wait_ge(sm("rstd_ready"), 2 * (n - 1) + q + 1)
                for j in range(4 * q, 4 * q + 4):
                    ins = v.tensor_scalar(sz[:, j], xs[:, j], mv[:, j, 0:1], rstd[:, j:j + 1], ALU.subtract, ALU.mult)
                return ins

            def make_u(ly, q, th):
                v.wait_ge(sm(f"pre_u{ly}"), q + 1)
                z = us[ly][:, :, tsl(q)]
                v.scalar_tensor_tensor(out=z, in0=th, scalar=1.0, in1=z, op0=ALU.add, op1=ALU.mult
                                       ).then_inc(sm(f"u_ready{ly}"), 1)

            def split_bc(ly, q, k):
                z = tsl(q)
                lo = slice(2 * BC, 3 * BC)
                v.wait_ge(sm(f"bc1_ready{ly}"), q + 1)
                link(v.tensor_tensor(R0[:, z], PS[0:3 * BC, k + q, :], CS[ly][:, z], ALU.subtract))
                v.tensor_copy(CS[ly][BC:2 * BC, z], R0[BC:2 * BC, z])
                link(v.tensor_copy(CS[ly][lo, z], R0[lo, z]))
                v.tensor_tensor(CS[ly][lo, z], R0[lo, z], CS[ly][lo, z], ALU.subtract).then_inc(sm(f"bc_ready{ly}"), 1)

            def make_delta(ly, q):
                z = tsl(q)
                v.wait_ge(sm(f"sp_ready{ly}"), q + 1)
                v.tensor_scalar(s_abs[:, :, z], s_exp[:, :, z], 1.0, -1.0, ALU.add, ALU.add)
                link(v.tensor_tensor(s_relu[:, :, z], s_ln[:, :, z], s_relu[:, :, z], ALU.add))
                link(v.tensor_tensor(s_exp[:, :, z], s_exp[:, :, z], s_abs[:, :, z], ALU.subtract))
                link(v.tensor_tensor(delta[:, :, z], s_relu[:, :, z], s_exp[:, :, z], ALU.add))
                v.tensor_tensor(du[:, :, z], delta[:, :, z], us[ly][:, :, z], ALU.mult).then_inc(sm(f"du_ready{ly}"), 1)

            v.wait_ge(sm("ld_taps0"), 32)
            v.tensor_tensor(taps[0], taps[0], inw[:, 0:1, :].broadcast_to([P, DC, DI]), ALU.mult
                            ).then_inc(sm("tap_ready0"), 1)
            v.wait_ge(sm("ld_x"), 16)
            for q in range(2):
                norm_stats(q)
            for q in range(2):
                make_u(0, q, slot[0][:, :, tsl(q)])
            for q in range(2):
                split_bc(0, q, 4)
            for q in range(2):
                normalise(1, q).then_inc(sm("z_ready"), 1)
            for q in range(2):
                make_delta(0, q)
            v.wait_ge(sm("pre_read0"), 2)
            v.memset(PS[:, 0:4, 0:512:L], 0.0).then_inc(sm("dA_zero"), 1)
            make_u(1, 0, raw[0][:, 0:1024].rearrange("p (h t) -> p h t", h=NH))
            make_u(1, 1, rt[:, 0:2].rearrange("p i j e -> p i (j e)"))

            def scan0(k):
                v.wait_ge(sm("exp0"), k + 1)
                v.wait_ge(sm("bmul0"), k + 1)
                if k >= 2:
                    v.wait_ge(sm("cmul0"), k - 1)
                v.tensor_tensor_scan(h0[:, k % 2].rearrange("p h t -> p (h t)"), bank(2 * (k % 2), 2),
                                     dBu0[:, k % 2].rearrange("p h t -> p (h t)"), 0.0, ALU.mult, ALU.add
                                     ).then_inc(sm("scan0"), 1)

            def cmul0(k):
                v.wait_ge(sm("scan0"), k + 1)
                v.wait_ge(sm("cb0_ready"), k + 1)
                if k >= 2:
                    v.wait_ge(sm("ysum0"), k - 1)
                v.tensor_tensor(prod0[:, k % 2], h0[:, k % 2], PS[:, 5:6, :].broadcast_to([P, NH, HT]), ALU.mult
                                ).then_inc(sm("cmul0"), 1)

            def gate_y0(q):
                v.wait_ge(sm("ysum0"), (q + 1) * DS)
                for h in range(NH):
                    ins = v.scalar_tensor_tensor(out=yg[:, h], in0=us[0][:, h, tsl(q)], scalar=chan[:, 0, h, 2:3],
                                                 in1=bank(6 + h), op0=ALU.mult, op1=ALU.add)
                link(ins)
                for h in range(NH):
                    z = yg[:, h].rearrange("p (b l) -> p b l", b=2)
                    ins = v.tensor_tensor(z, z, sz[:, 4 * q + h:4 * q + h + 3:2, :], ALU.mult)
                ins.then_inc(sm("yg_ready"), 1)

            def add_y0(q):
                v.wait_ge(sm("y0T_ready"), q + 1)
                if q == 0:
                    v.wait_ge(sm("gates_ready"), 1)
                xv = xs[:, xhalf(q)].rearrange("p j d -> p (j d)")
                v.scalar_tensor_tensor(out=xv, in0=bank(6, 2), scalar=hgates[:, 0:1], in1=xv,
                                       op0=ALU.mult, op1=ALU.add).then_inc(sm("x1_done"), 1)

            for k in range(U0 + 1):
                if k < U0:
                    scan0(k)
                if k >= 1:
                    cmul0(k - 1)
                if k == 2:
                    v.wait_ge(sm("ztan_ready"), 1)
                    v.scalar_tensor_tensor(out=szf, in0=ztan, scalar=1.0, in1=szf, op0=ALU.add, op1=ALU.mult
                                           ).then_inc(sm("sz0_ready"), 1)
                    v.wait_ge(sm("sz0_ready"), 1)
                if k == 4:
                    v.wait_ge(sm("gwhi_ready"), 1)
                    v.tensor_tensor(gwlo[:], gwT[:], gwhi[:].bitcast(F32), ALU.subtract).then_inc(sm("gwlo_ready"), 1)
                if k == DS:
                    gate_y0(0)
                if k == DS:
                    add_y0(0)
            gate_y0(1)
            v.wait_ge(sm("x1_done"), 1)
            norm_stats(0)
            split_bc(1, 0, 4)
            add_y0(1)
            v.wait_ge(sm("x1_done"), 2)
            norm_stats(1)
            split_bc(1, 1, 4)
            normalise(2, 0).then_inc(sm("xn_ready"), 1)
            normalise(2, 1).then_inc(sm("xn_ready"), 1)
            make_delta(1, 0)

            for k in range(4):
                v.wait_ge(sm("xhi_ready"), k + 1)
                z = (slice(None), k % 2, tsl(k // 2))
                v.tensor_tensor(xTlo[z], bank(4 + k), xThi[z].bitcast(F32), ALU.subtract).then_inc(sm("xlo_ready"), 1)
            make_delta(1, 1)
            v.wait_ge(sm("du_ready1"), 2)
            for h in range(NH):
                ins = v.tensor_scalar(y1[:, h], us[1][:, h], chan[:, 1, h, 2:3], None, ALU.mult)
            link(ins)
            v.memset(dA1[:, :, :, 0:1], 0.0).then_inc(sm("dA_zero"), 1)
            v.wait_ge(sm("wtot_ready"), 1)
            link(v.tensor_scalar(wstat[:, 1, :], PS[:, 1, 0:3], 1.0 / (HID * D), Q_EPS, ALU.mult, ALU.max))
            v.tensor_scalar(wstat[:, 2, :], wstat[:, 1, :], 0.5, None, ALU.mult)
            link(v.tensor_scalar(wstat[:, 3, :], wstat[:, 1, :], -0.5, None, ALU.mult))
            v.wait_ge(sm("logits_ready"), 1)
            lg = bank(0).rearrange("p (j e) -> p j e", j=NT)
            link(v.tensor_reduce(rsm[:, 0, :], lg, AX.X, ALU.max))
            v.tensor_tensor(left, lg, rsm[:, 0, :].unsqueeze(2).broadcast_to([P, NT, E]), ALU.subtract).then_inc(sm("lsub_ready"), 1)
            v.wait_ge(sm("pexp_ready"), 1)
            link(v.tensor_reduce(rsm[:, 1, :], probs, AX.X, ALU.add))
            link(v.reciprocal(rsm[:, 2, :], rsm[:, 1, :]))
            link(v.tensor_tensor(probs, probs, rsm[:, 2, :].unsqueeze(2).broadcast_to([P, NT, E]), ALU.mult))
            for j in range(NT):
                ins = v.max(top8[:, j], probs[:, j])
            link(ins)
            for j in range(NT):
                ins = v.match_replace(left[:, j], top8[:, j], probs[:, j], 0.0)
            link(ins)
            link(v.tensor_reduce(rsm[:, 0, :], top8[:], AX.X, ALU.add))
            link(v.scalar_tensor_tensor(out=rsm[:, 1, :], in0=rsm[:, 0, :], scalar=0.0, in1=rsm[:, 0, :],
                                        op0=ALU.is_equal, op1=ALU.add))
            link(v.reciprocal(rsm[:, 2, :], rsm[:, 1, :]))
            link(v.tensor_scalar(rsm[:, 3, :], rsm[:, 2, :], hgates[:, 2:3], None, ALU.mult))
            link(v.tensor_tensor(comb, probs, left, ALU.subtract))
            v.tensor_tensor(comb, comb, rsm[:, 3, :].unsqueeze(2).broadcast_to([P, NT, E]), ALU.mult).then_inc(sm("comb_ready"), 1)

            def bmul1(k):
                b = k % B
                v.wait_ge(sm("bc1_done"), k + 1)
                if k >= 1:
                    v.wait_ge(sm("scan1"), k)
                v.tensor_tensor(dBu1[:], du[:, :, b * L:(b + 1) * L],
                                PS[:, 6 + k % 2, 0:L].unsqueeze(1).broadcast_to([P, NH, L]), ALU.mult
                                ).then_inc(sm("bmul1"), 1)

            def scan1(k):
                v.wait_ge(sm("bmul1"), k + 1)
                v.wait_ge(sm("exp1"), k + 1)
                if k >= 1:
                    v.wait_ge(sm("cmul1"), k)
                v.tensor_tensor_scan(h1.rearrange("p h t -> p (h t)"), dA1[:, k % 2].rearrange("p h t -> p (h t)"),
                                     dBu1[:].rearrange("p h t -> p (h t)"), 0.0, ALU.mult, ALU.add
                                     ).then_inc(sm("scan1"), 1)

            def cmul1(k):
                v.wait_ge(sm("scan1"), k + 1)
                if k >= 2:
                    v.wait_ge(sm("yacc1"), k - 1)
                v.tensor_tensor(prod1[:, k % 2], h1, PS[:, 6 + k % 2, L:2 * L].unsqueeze(1).broadcast_to([P, NH, L]),
                                ALU.mult).then_inc(sm("cmul1"), 1)

            def ternary(m, i):
                z = slice(i * 256, (i + 1) * 256)
                if i == 0:
                    v.wait_ge(sm("ld_wq2"), 16 * (m + 1))
                link(v.tensor_scalar(wq[m][:, z], wstage[:, z], wstat[:, 3, m:m + 1], None, ALU.is_lt))
                v.scalar_tensor_tensor(out=wq[m][:, z], in0=wstage[:, z], scalar=wstat[:, 2, m:m + 1],
                                       in1=wq[m][:, z], op0=ALU.is_gt, op1=ALU.subtract).then_inc(sm("wq_done"), 1)

            for s in range(STEPS + 3):
                if s < STEPS:
                    v.wait_ge(sm("tanh_done"), s + 1)
                    v.scalar_tensor_tensor(out=ga[:, s % 2], in0=tg[:, s % 2], scalar=1.0, in1=PS[:, s % 2, 0:CW],
                                           op0=ALU.add, op1=ALU.mult).then_inc(sm("gated"), 1)
                    if s % 2 == 0:
                        bmul1(s // 2)
                    else:
                        cmul1(s // 2)
                    v.wait_ge(sm("gated"), s + 1)
                    if s >= 3:
                        v.wait_ge(sm("wmul_done"), s - 2)
                    v.tensor_tensor(act[:, s % 3], ga[:, s % 2], PS[:, 2 + s % 2, 0:CW], ALU.mult).then_inc(sm("umul_done"), 1)
                if 2 <= s < STEPS + 2:
                    r = s - 2
                    v.wait_ge(sm("ahi_done"), r + 1)
                    if r >= 2:
                        v.wait_ge(sm("down_ready"), r - 1)
                    v.tensor_tensor(aTlo[:, r % 2], PS[:, 4, 0:CW], aThi[:, r % 2].bitcast(F32), ALU.subtract).then_inc(sm("alo_done"), 1)
                if s < STEPS and s % 2 == 0:
                    scan1(s // 2)
                if s in WQ_STEPS:
                    ternary(*WQ_STEPS[s])
                if s >= 3:
                    r = s - 3
                    v.wait_ge(sm("down_ready"), r + 1)
                    if r >= NT:
                        v.wait_ge(sm("acc_done"), r - NT + 1)
                    v.tensor_tensor(xs[:, r % NT], xs[:, r % NT], PS[:, 5, 0:D], ALU.add).then_inc(sm("acc_done"), 1)
            v.wait_ge(sm("acc_done"), STEPS)
            v.wait_ge(sm("yacc1"), U1)

            for q in range(2):
                norm_stats(q)
            for q in range(2):
                normalise(3, q).then_inc(sm("z_ready"), 1)
            for q in range(2):
                z = szf[:, q * 1024:(q + 1) * 1024]
                v.wait_ge(sm("ztan_ready"), 2 + q)
                link(v.scalar_tensor_tensor(out=z, in0=work[:, 0, q * 1024:(q + 1) * 1024], scalar=1.0, in1=z,
                                            op0=ALU.add, op1=ALU.mult))
                for h in range(NH):
                    yv = y1[:, h, tsl(q)].rearrange("p (b l) -> p b l", b=2)
                    ins = v.tensor_tensor(yv, yv, sz[:, 4 * q + h:4 * q + h + 3:2, :], ALU.mult)
                ins.then_inc(sm("yz_ready"), 1)
            for q in range(2):
                v.wait_ge(sm("y1T_ready"), q + 1)
                xv = xs[:, xhalf(q)].rearrange("p j d -> p (j d)")
                v.scalar_tensor_tensor(out=xv, in0=bank(2 * q, 2), scalar=hgates[:, 1:2], in1=xv,
                                       op0=ALU.mult, op1=ALU.add).then_inc(sm("x3_done"), 1)
                v.wait_ge(sm("x3_done"), q + 1)
                norm_stats(q)

            for q in range(2):
                normalise(4, q).then_inc(sm("xn3_ready"), 1)
            for q in range(2):
                z = xhalf(q)
                v.wait_ge(sm("had_ready"), q + 1)
                hv = PS[:, 4 + 2 * q:6 + 2 * q, :].rearrange("p k (j d) -> p (k j) d", j=2)
                link(v.tensor_reduce(tok[:, 0, z], hv, AX.X, ALU.max, apply_absolute_value=True))
                link(v.tensor_scalar(tok[:, 1, z], tok[:, 0, z], Q_EPS, None, ALU.max))
                link(v.reciprocal(tok[:, 2, z], tok[:, 1, z]))
                link(v.tensor_scalar(tok[:, 2, z], tok[:, 2, z], 127.0, None, ALU.mult))
                for j in range(4):
                    i = 4 * q + j
                    ins = v.tensor_scalar(sz[:, i], hv[:, j], tok[:, 2, i:i + 1], 127.0, ALU.mult, ALU.min)
                link(ins)
                szq = szf[:, q * 1024:(q + 1) * 1024]
                link(v.tensor_scalar(szq, szq, -128.0, ROUND, ALU.max, ALU.add))
                v.tensor_scalar(q1[:, z].rearrange("p j d -> p (j d)"), szq, -ROUND, None, ALU.add).then_inc(sm("q1_ready"), 1)
            link(v.tensor_scalar(tok[:, 3, :], tok[:, 1, :], wstat[:, 1, 0:1], 0.5 / 127, ALU.mult, ALU.mult))
            v.tensor_scalar(tok[:, 6, 0:1], wstat[:, 1, 2:3], gates[:, 3:4], 1.0 / 127, ALU.mult, ALU.mult)
            link(v.tensor_scalar(tok[:, 5, :], tok[:, 1, :], wstat[:, 1, 1:2], 0.5 / 127, ALU.mult, ALU.mult))
            v.tensor_tensor(tok[:, 4, :], tok[:, 3, :], tok[:, 5, :], ALU.mult).then_inc(sm("tok_ready"), 1)
            v.wait_ge(sm("tok_ready"), 1)

            def hidden(t):
                v.wait_ge(sm("ffn_tanh"), t + 1)
                link(v.scalar_tensor_tensor(out=fa, in0=fth, scalar=1.0, in1=bank(0, 2), op0=ALU.add, op1=ALU.mult))
                if t >= 2:
                    v.wait_ge(sm("ffn_mix"), t - 1)
                v.tensor_tensor(fb[:, t % 2], fa, bank(2, 2), ALU.mult).then_inc(sm("ffn_b"), 1)

            def scales(r):
                v.wait_ge(sm("ffn_had"), r + 1)
                f = ft[:, r % 3]
                kf = tok[:, 4, r:r + 1]
                link(v.tensor_reduce(f[:, 0:1], bank(6, 2), AX.X, ALU.max, apply_absolute_value=True))
                link(v.tensor_scalar(f[:, 1:2], f[:, 0:1], kf, Q_EPS, ALU.mult, ALU.max))
                link(v.reciprocal(f[:, 2:3], f[:, 1:2]))
                v.tensor_scalar(f[:, 3:4], f[:, 2:3], kf, 127.0, ALU.mult, ALU.mult).then_inc(sm("ffn_scales"), 1)
                v.tensor_scalar(f[:, 4:5], f[:, 1:2], tok[:, 6, 0:1], None, ALU.mult)

            def quantise(r):
                v.wait_ge(sm("ffn_qa"), r + 1)
                link(v.tensor_scalar(fq, fq, 127.0, -128.0, ALU.min, ALU.max))
                if r >= 2:
                    v.wait_ge(sm("ffn_qtr"), r - 1)
                v.tensor_scalar(qh[:, r % 2], fq, ROUND, -ROUND, ALU.add, ALU.add).then_inc(sm("ffn_qh"), 1)

            def finish(r):
                v.wait_ge(sm("ffn_down"), r + 1)
                v.scalar_tensor_tensor(out=xs[:, r], in0=PS[:, 5, 0:D], scalar=ft[:, r % 3, 4:5], in1=xs[:, r],
                                       op0=ALU.mult, op1=ALU.add).then_inc(sm("out_ready"), 1)

            for t in range(NT + 3):
                if t >= 3:
                    finish(t - 3)
                if 1 <= t <= NT:
                    scales(t - 1)
                if t < NT:
                    hidden(t)
                if 1 <= t <= NT:
                    quantise(t - 1)


def kernel(**inputs):
    import ml_dtypes
    import numpy as np
    import concourse.bacc as bacc
    from concourse.bass_utils import run_bass_kernel_spmd

    x = {k: np.asarray(v) for k, v in inputs.items()}
    ctxp = np.zeros((DM, B, LP), np.float32)
    ctxp[:, :, DC - 1:] = x["ctx_1024"].transpose(2, 0, 1)
    arrays = {"x": x["x"], "ctxT": ctxp, "g_xattn": x["g_xattn"], "g_ffn": x["g_ffn"]}
    chan = []
    for ly in range(2):
        p = f"L{ly}_xattn_"
        arrays[f"L{ly}_inT"] = x[p + "in_proj_w"].T
        arrays[f"L{ly}_taps"] = x[p + "conv_w"].reshape(DI, DC).T
        w = x[p + "x_proj_w"].T
        dt, bc = w[:, :DR], w[:, DR:]
        arrays[f"L{ly}_xpT"] = np.concatenate([bc, bc, bc, dt], axis=1)
        arrays[f"L{ly}_dtT"] = x[p + "dt_proj_w"].T
        v = [x[p + n].reshape(DI, -1) for n in ("conv_b", "dt_proj_b", "D", "A_log")]
        chan.append(np.concatenate(v, axis=1).reshape(NH, P, 3 + DS))
    arrays["chan"] = np.stack(chan).transpose(2, 0, 1, 3)
    arrays["gateT"] = x["L0_ffn_gate_weight"].T
    gu = x["L0_ffn_gate_up_weights"].reshape(NCH, EC, D, 2, I)
    arrays["guT"] = gu.transpose(0, 2, 3, 1, 4).reshape(NCH, D, 2 * CW)
    arrays["dnT"] = x["L0_ffn_down_weights"].reshape(NCH, CW, D)
    arrays["wgT"], arrays["wuT"], arrays["wdT"] = (x[f"L1_ffn_w_{m}"].T for m in ("gate", "up", "down"))
    h = np.ones((1, 1), np.float32)
    while h.shape[0] < D:
        h = np.block([[h, h], [h, -h]])
    arrays["had"] = (h / 16).astype(np.float32)
    arrays["ident"] = np.eye(P, dtype=np.float32)
    arrays["identb"] = np.eye(P).astype(ml_dtypes.bfloat16)
    sel = np.zeros((3 * BC, BC, P), ml_dtypes.bfloat16)
    for i in range(3):
        for n in range(BC):
            sel[BC * i + n, n] = 1
    arrays["sel"] = sel
    arrays = {k: np.ascontiguousarray(v) for k, v in arrays.items()}

    nc = bacc.Bacc("TRN2", target_bir_lowering=False, num_devices=1)
    aps = {k: nc.dram_tensor(f"in_{k}", v.shape, mybir.dt.from_np(v.dtype), kind="ExternalInput").ap()
           for k, v in arrays.items()}
    out = nc.dram_tensor("out_0", (B, L, D), F32, kind="ExternalOutput").ap()
    flamingo_gated_block(nc, aps, out)
    r = run_bass_kernel_spmd(nc, [{f"in_{k}": v for k, v in arrays.items()}], core_ids=[0])
    return r.results[0]["out_0"]
```

```python
from contextlib import ExitStack

import concourse.bass as bass
from concourse import mybir

P = 128
F32 = mybir.dt.float32
F32R = mybir.dt.float32r
BF16 = mybir.dt.bfloat16
ALU = mybir.AluOpType
ACT = mybir.ActivationFunctionType
AX = mybir.AxisListType

B, L, D = 4, 256, 256
T = B * L
NT = T // P
DM = 128
DI = 256
NH = DI // P
DS = 16
DC = 4
DR = 8
LP = L + DC - 1
BC = 2 * DS
XP = 3 * BC + DR
E, I = 64, 96
TOPK = 8
EC = 4
CW = EC * I
CB = CW // P
NCH = E // EC
GUW = 2 * 2 * CW
DWW = CB * D
WP = 256
HID = 1024
HB = HID // P
LN_EPS = 1e-5
Q_EPS = 1e-5
ROUND = 12582912.0
HT = T // 2
U0 = 2 * DS
U1 = B * DS
CSTEPS = 2 * CB
STEPS = NCH * CSTEPS
NPAIR = 2 * NCH


def flamingo_gated_block(nc, a, out):
    ctx = ExitStack()
    with ctx:
        def sb(name, shape, dt=F32):
            return ctx.enter_context(nc.sbuf_tensor(name, shape, dt))

        PS = ctx.enter_context(nc.psum_tensor("banks", [P, 8, 512], F32))

        def bank(k, n=1):
            return PS[:, k:k + n, :].rearrange("p k x -> p (k x)")

        ident = sb("ident", [P, P])
        identb = sb("identb", [P, P], BF16)
        sel = sb("sel", [3 * BC, BC, P], BF16)
        ones = sb("ones", [P, P])
        nhalf = sb("nhalf", [P, NT])
        gates_in = sb("gates_in", [P, 4])
        gates = sb("gates", [P, 4])
        hgates = sb("hgates", [P, 4])
        ctxp = sb("ctxp", [P, B, LP])
        xpw = sb("xpw", [P, 2, NH, XP])
        dtw = sb("dtw", [DR, 2, DI])
        chan = sb("chan", [P, 2, NH, 3 + DS])
        Aneg = sb("Aneg", [P, 2, NH, DS])
        hcb = sb("hcb", [P, 2, NH])
        xs = sb("xs", [P, NT, D])
        sz = sb("sz", [P, NT, D])
        stats = sb("stats", [P, NT, 6])
        mv = sb("mv", [P, NT, 2])
        rstd = sb("rstd", [P, NT])
        us = [sb(f"u{ly}", [P, NH, T]) for ly in range(2)]
        y1 = us[1]
        delta = sb("delta", [P, NH, T])
        inw = delta[:, 0, 0:2 * DI].rearrange("p (i e) -> p i e", i=2)
        du = sb("du", [P, NH, T])
        CS = [sb(f"CS{ly}", [3 * BC, T], BF16) for ly in range(2)]
        work = sb("work", [P, 4, 2048])
        raw = [sb(f"raw{i}", [P, GUW + DWW]) for i in range(2)]
        had = raw[1][:, 0:2 * D].rearrange("p (k f) -> p k f", k=2)
        rt = sb("rt", [P, 4, NT, E])
        taps = [raw[0][:, ly * 1024:(ly + 1) * 1024].rearrange("p (k e) -> p k e", k=DC) for ly in range(2)]
        ztan = raw[1][:, 0:2048]
        s_abs, s_exp, s_ln, s_relu = [
            [work[:, i, q * 1024:(q + 1) * 1024].rearrange("p (h t) -> p h t", h=NH) for q in range(2)] for i in range(4)]
        Bs = work[:, 0, 0:1024].rearrange("p (i t) -> p i t", i=2)
        yg = work[:, 0, 1024:2048].rearrange("p (h t) -> p h t", h=NH)
        dBu0 = work[:, 1, :].rearrange("p (i h t) -> p i h t", i=2, h=NH)
        h0 = [work[:, 2, i * 1024:(i + 1) * 1024].rearrange("p (h t) -> p h t", h=NH) for i in range(2)]
        h0.append(rt[:, 2:4].rearrange("p i j e -> p (i j e)").rearrange("p (h t) -> p h t", h=NH))
        prod0 = work[:, 3, :].rearrange("p (i h t) -> p i h t", i=2, h=NH)
        xThi = sb("xThi", [P, 2, T], F32R)
        xTlo = sb("xTlo", [P, 2, T], F32R)
        gwT = sb("gwT", [P, 2, E])
        gwhi = sb("gwhi", [P, 2, E], F32R)
        gwlo = sb("gwlo", [P, 2, E], F32R)
        lgT = ctxp[:].rearrange("p b l -> p (b l)")[0:E, 0:T]
        probs, left = rt[:, 0], rt[:, 1]
        comb2 = rt[:, 2:4].rearrange("p i j e -> p (i j e)").rearrange("p (j x) -> p j x", j=NT)
        combT = sb("combT", [P, T], F32R)
        eye2 = sb("eye2", [P, E], F32R)
        top8 = sb("top8", [P, NT, TOPK])
        rsm = sb("rsm", [P, 4, NT])
        whi = [sb(f"whi{i}", [P, GUW + DWW], F32R) for i in range(2)]
        wlo = [sb(f"wlo{i}", [P, GUW + DWW], F32R) for i in range(2)]
        ctx_parts = [w[1][:, 0:B * LP].rearrange("p (b l) -> p b l", b=B) for w in (whi, wlo)]
        tap_parts = [[w[0][:, ly * 1024:(ly + 1) * 1024].rearrange("p (k e) -> p k e", k=DC) for w in (whi, wlo)]
                     for ly in range(2)]
        tg = work[:, 0, 0:2 * HT].rearrange("p (i t) -> p i t", i=2)
        ga = work[:, 0, 2 * HT:].rearrange("p (i t) -> p i t", i=2)
        act = work[:, 1, 0:2 * HT].rearrange("p (i t) -> p i t", i=2)
        actw = work[:, 1, 2 * HT:].rearrange("p (i t) -> p i t", i=2)
        combB = work[:, 2, 0:2 * HT].rearrange("p (i t) -> p i t", i=2)
        ahi = sb("ahi", [P, 2, HT], F32R)
        alo = sb("alo", [P, 2, HT], F32R)
        accT = sz[:].rearrange("p j d -> p (j d)").rearrange("p (h t) -> p h t", h=NH)
        dA1 = work[:, 3, 0:1024].rearrange("p (i h t) -> p i h t", i=2, h=NH)
        prod1 = work[:, 3, 1024:2048].rearrange("p (i h t) -> p i h t", i=2, h=NH)
        dBu1 = ctxp[:].rearrange("p b l -> p (b l)")[:, 0:NH * L].rearrange("p (h t) -> p h t", h=NH)
        h1 = work[:, 2, 2 * HT:3 * HT].rearrange("p (h t) -> p h t", h=NH)
        pick = sb("pick", [P, 2, P], F32R)
        wq = [sb(f"wq{m}", [P, 2048], BF16) for m in range(3)]
        R0 = wq[0][:].bitcast(F32)[0:3 * BC]
        dtlo = wq[1][:].bitcast(F32)[0:DR]
        wsum = sb("wsum", [P, 3, 4])
        wstat = sb("wstat", [P, 4, 3])
        wstage = us[0][:].rearrange("p h t -> p (h t)")
        tok = sb("tok", [P, 8, NT])
        ft = sb("ft", [P, 3, 8])
        xT3 = delta
        dub = du[:].rearrange("p h t -> p (h t)").bitcast(BF16)
        q1 = dub[:, 0:NT * D].rearrange("p (j d) -> p j d", j=NT)
        q1T = dub[:, NT * D:].rearrange("p (k t) -> p k t", k=2)
        ub = us[0][:].rearrange("p h t -> p (h t)").bitcast(BF16)
        qh = ub[:, 0:2 * HID].rearrange("p (i f) -> p i f", i=2)
        qhT = ub[:, 2 * HID:4 * HID].rearrange("p (i k t) -> p i k t", i=2, k=HB)
        fth = work[:, 0, 0:HID]
        fa = work[:, 0, HID:]
        fb = work[:, 1, :].rearrange("p (i f) -> p i f", i=2)
        fo = work[:, 2, :].rearrange("p (i f) -> p i f", i=2)
        fm = work[:, 3, 0:HID]
        fq = work[:, 3, HID:]
        bT = raw[0][:, 0:2 * HID].rearrange("p (i k t) -> p i k t", i=2, k=HB)

        szf = sz[:].rearrange("p j d -> p (j d)")
        out_rows = out.rearrange("b l d -> (b l) d").rearrange("(j p) d -> p j d", p=P)
        x_rows = a["x"].rearrange("b l d -> (b l) d").rearrange("(j p) d -> p j d", p=P)

        S = {}

        def sm(name):
            if name not in S:
                S[name] = ctx.enter_context(nc.semaphore(name))
            return S[name]

        def chain(eng, name):
            s, n = sm(name), [0]

            def link(ins):
                n[0] += 1
                ins.then_inc(s, 1)
                eng.wait_ge(s, n[0])
            return link

        def parts(j):
            return ([0, 1], [2], [3, 4], [5], [6, 7], [8])[j]

        def comb_bank(m):
            return 6 + (m + 1) % 2

        def scan_bank(k):
            return 6 + (3 * (k // 2) + 1 + k % 2) % 2

        def tsl(q):
            return slice(q * HT, (q + 1) * HT)

        def xhalf(q):
            return slice(4 * q, 4 * q + 4)

        WSUM_UNITS = {k0 + i: (m, i) for m, k0 in enumerate((5, 11, 20)) for i in range(4)}
        WQ_STEPS = {3 * (4 + 9 * m + i): (m, i) for m in range(3) for i in range(8)}
        block = ctx.enter_context(nc.Block())

        @block.sync
        def _(sp):
            sp.dma_start(ctxp[:], a["ctxT"]).then_inc(sm("ld_ctx"), 16)
            sp.dma_start(xpw[:, 0], a["L0_xpT"].rearrange("(h p) k -> p h k", p=P)).then_inc(sm("ld_w0"), 16)
            sp.dma_start(dtw[:, 0], a["L0_dtT"]).then_inc(sm("ld_w0"), 16)
            sp.dma_start(xs[:], x_rows).then_inc(sm("ld_x"), 16)
            lc = sm("ld_const")
            sp.dma_start(sel[:], a["sel"]).then_inc(lc, 16)
            sp.dma_start(ident[:], a["ident"]).then_inc(lc, 16)
            sp.dma_start(identb[:], a["identb"]).then_inc(lc, 16)
            sp.dma_start(gwT[:], a["gateT"].rearrange("(k p) e -> p k e", p=P)).then_inc(lc, 16)
            sp.dma_start(xpw[:, 1], a["L1_xpT"].rearrange("(h p) k -> p h k", p=P)).then_inc(sm("ld_w1"), 16)
            sp.dma_start(dtw[:, 1], a["L1_dtT"]).then_inc(sm("ld_w1"), 16)

            names = ("wgT", "wuT", "wdT")

            def load_wq(m, to, s):
                sp.dma_start(to.rearrange("p (k f) -> p k f", k=(2, 2, HB)[m]),
                             a[names[m]].rearrange("(k p) f -> p k f", p=P)).then_inc(s, 16)

            sp.wait_ge(sm("conv_done1"), 2)
            sp.wait_ge(sm("u_ready1"), 2)
            load_wq(0, raw[0][:, 0:2048], sm("ld_wq"))
            for m in (1, 2):
                sp.wait_ge(sm("wsum_ready"), 4 * m)
                load_wq(m, raw[0][:, 0:2048], sm("ld_wq"))

            def load_chunk(c):
                if c == 0:
                    sp.wait_ge(sm("wsum_ready"), 12)
                if c == 1:
                    sp.wait_ge(sm("sz0_ready"), 1)
                if c >= 2:
                    sp.wait_ge(sm("wlo_done"), 9 * (c - 1))
                r = raw[c % 2]
                s = sm(f"ld_raw{c % 2}")
                sp.dma_start(r[:, 0:GUW].rearrange("p (k f) -> p k f", k=2),
                             a["guT"][c].rearrange("(k p) f -> p k f", p=P)).then_inc(s, 16)
                sp.dma_start(r[:, GUW:].rearrange("p (k f) -> p k f", k=CB),
                             a["dnT"][c].rearrange("(k p) f -> p k f", p=P)).then_inc(s, 16)

            for c in range(NCH):
                load_chunk(c)
                if c == 1:
                    sp.wait_ge(sm("x1_done"), 2)
                    load_wq(0, wstage, sm("ld_wq2"))
                if c in (7, 12):
                    m = 1 if c == 7 else 2
                    sp.wait_ge(sm("wq_done"), 8 * m)
                    load_wq(m, wstage, sm("ld_wq2"))
            sp.wait_ge(sm("wlo_done"), 9 * NCH)
            sp.dma_start(had, a["had"].rearrange("(k p) f -> p k f", p=P)).then_inc(sm("ld_had"), 16)
            for t in range(NT):
                sp.wait_ge(sm("out_ready"), t + 1)
                sp.dma_start(out_rows[:, t], xs[:, t]).then_inc(sm("stored"), 16)
            sp.wait_ge(sm("stored"), 16 * NT)

        @block.gpsimd
        def _(pool):
            link = chain(pool, "pool_own")
            pool.memset(nhalf[:], -0.5)
            pool.memset(ones[:], 1.0).then_inc(sm("ones_ready"), 1)
            pool.wait_ge(sm("ones_ready"), 1)

            def inverse_root(n, halves=(0, 1)):
                for q in halves:
                    i = 2 * (n - 1) + q + 1
                    pool.wait_ge(sm("var_ready"), i)
                    pool.tensor_tensor(rstd[:, xhalf(q)], rstd[:, xhalf(q)], nhalf[:, xhalf(q)], ALU.pow
                                       ).then_inc(sm("rstd_ready"), 1)

            pool.wait_ge(sm("ld_taps1"), 32)
            pool.tensor_tensor(taps[1], taps[1], inw[:, 1:2, :].broadcast_to([P, DC, DI]), ALU.mult
                               ).then_inc(sm("tap_ready1"), 1)
            pool.wait_ge(sm("tap_hi_ready1"), 1)
            pool.tensor_tensor(tap_parts[1][1], taps[1], tap_parts[1][0].bitcast(F32), ALU.subtract
                               ).then_inc(sm("tap_lo_ready1"), 1)
            inverse_root(1)

            for k in range(U0):
                q = k // DS
                if k <= 1:
                    pool.wait_ge(sm("du_ready0"), k + 1)
                pool.wait_ge(sm("Bs_ready"), k + 1)
                if k >= 2:
                    pool.wait_ge(sm("scan0"), k - 1)
                pool.tensor_tensor(dBu0[:, k % 2], du[:, :, tsl(q)],
                                   Bs[:, k % 2:k % 2 + 1, :].broadcast_to([P, NH, HT]), ALU.mult
                                   ).then_inc(sm("bmul0"), 1)
                if k == DS + 4:
                    inverse_root(2, (0,))

            def split_lo(c, p):
                pool.wait_ge(sm("whi_done"), 9 * c + p + 1)
                if p == 0 and c >= 2:
                    pool.wait_ge(sm("gu_ready"), CSTEPS * (c - 1))
                if p == 6 and c >= 2:
                    pool.wait_ge(sm("down_ready"), CSTEPS * (c - 1))
                z = slice(p * WP, (p + 1) * WP)
                pool.tensor_tensor(wlo[c % 2][:, z], raw[c % 2][:, z], whi[c % 2][:, z].bitcast(F32),
                                   ALU.subtract).then_inc(sm("wlo_done"), 1)

            def yacc1(k):
                b = k % B
                pool.wait_ge(sm("cmul1"), k + 1)
                if k >= B:
                    pool.wait_ge(sm("yacc1"), k - B + 1)
                ys = y1[:, :, b * L:(b + 1) * L]
                pool.tensor_tensor(ys, ys, prod1[:, k % 2], ALU.add).then_inc(sm("yacc1"), 1)

            for p in range(9):
                split_lo(0, p)
            inverse_root(2, (1,))
            z = tsl(1)
            pool.wait_ge(sm("sp_ready1"), 2)
            pool.wait_ge(sm("round_ready"), 1)
            link(pool.tensor_tensor(s_relu[1], s_ln[1], s_relu[1], ALU.add))
            link(pool.tensor_tensor(s_exp[1], s_exp[1], s_abs[1], ALU.subtract))
            link(pool.tensor_tensor(delta[:, :, z], s_relu[1], s_exp[1], ALU.add))
            pool.tensor_tensor(du[:, :, z], delta[:, :, z], us[1][:, :, z], ALU.mult).then_inc(sm("du_ready1b"), 1)
            for s in range(STEPS):
                c, j = divmod(s, CSTEPS)
                m = s // CB
                pool.wait_ge(sm("combB_ready"), m + 1)
                pool.wait_ge(sm("umul_done"), s + 1)
                if s >= 2:
                    pool.wait_ge(sm("alo_done"), s - 1)
                pool.tensor_tensor(actw[:, s % 2], act[:, s % 2], combB[:, m % 2], ALU.mult).then_inc(sm("wmul_done"), 1)
                if s % CB == 2:
                    yacc1(2 * m)
                if s % CB == 1 and m >= 1:
                    yacc1(2 * m - 1)
                if c + 1 < NCH:
                    for p in parts(j):
                        split_lo(c + 1, p)
            yacc1(U1 - 1)
            inverse_root(3)
            for q in range(2):
                pool.wait_ge(sm("sz1_ready"), q + 1)
                for h in range(NH):
                    yv = y1[:, h, tsl(q)].rearrange("p (b l) -> p b l", b=2)
                    ins = pool.tensor_tensor(yv, yv, sz[:, 4 * q + h:4 * q + h + 3:2, :], ALU.mult)
                ins.then_inc(sm("yz_ready"), 1)
            inverse_root(4)
            for t in range(NT):
                pool.wait_ge(sm("ffn_b"), t + 1)
                if t >= 2:
                    pool.wait_ge(sm("ffn_tr"), t - 1)
                src = fb[:, t % 2].rearrange("p (x y r) -> p x y r", x=2, y=2)
                mid = fm.rearrange("p (x y r) -> p x y r", x=2, y=2)
                dst = fo[:, t % 2].rearrange("p (x y r) -> p x y r", x=2, y=2)
                pool.tensor_tensor(mid[:, :, 0], src[:, :, 0], src[:, :, 1], ALU.add)
                link(pool.tensor_tensor(mid[:, :, 1], src[:, :, 0], src[:, :, 1], ALU.subtract))
                pool.tensor_tensor(dst[:, 0], mid[:, 0], mid[:, 1], ALU.add)
                pool.tensor_tensor(dst[:, 1], mid[:, 0], mid[:, 1], ALU.subtract).then_inc(sm("ffn_mix"), 1)
                pool.wait_ge(sm("ffn_mix"), t + 1)

        @block.scalar
        def _(act_e):
            link = chain(act_e, "act_own")
            A = nc.scalar.activation
            for ly in range(2):
                lt = sm(f"ld_taps{ly}")
                act_e.dma_start(inw[:, ly], a[f"L{ly}_inT"]).then_inc(lt, 16)
                act_e.dma_start(taps[ly], a[f"L{ly}_taps"].unsqueeze(0).broadcast_to([P, DC, DI])).then_inc(lt, 16)
                if ly == 0:
                    act_e.dma_start(chan[:], a["chan"]).then_inc(sm("ld_chan"), 16)
            for i, g in enumerate(("g_xattn", "g_ffn")):
                act_e.dma_start(gates_in[:, 2 * i:2 * i + 2], a[g].unsqueeze(0).broadcast_to([P, 2])).then_inc(sm("ld_gates"), 16)
            act_e.wait_ge(sm("ld_ctx"), 16)
            A(ctx_parts[0], ctxp[:], ACT.Copy).then_inc(sm("ctx_hi_ready"), 1)
            act_e.wait_ge(sm("tap_ready0"), 1)
            A(tap_parts[0][0], taps[0], ACT.Copy).then_inc(sm("tap_hi_ready0"), 1)
            act_e.wait_ge(sm("ld_chan"), 16)
            A(hcb[:], chan[:, :, :, 0], ACT.Copy, scale=0.5).then_inc(sm("hcb_ready"), 1)
            act_e.wait_ge(sm("hcb_ready"), 1)
            link(A(Aneg[:], chan[:, :, :, 3:], ACT.Exp))
            link(A(Aneg[:], Aneg[:], ACT.Copy, scale=-1.0))

            def before_u(ly, q, th, k):
                act_e.wait_ge(sm(f"conv_done{ly}"), q + 1)
                for h in range(NH):
                    A(th[:, h], bank(k + h), ACT.Tanh, scale=0.5, bias=hcb[:, ly, h:h + 1])
                    ins = A(us[ly][:, h, tsl(q)], bank(k + h), ACT.Identity, scale=0.5, bias=hcb[:, ly, h:h + 1])
                ins.then_inc(sm(f"pre_u{ly}"), 1)

            def evacuate_proj(ly, q, k):
                act_e.wait_ge(sm(f"proj_done{ly}"), q + 1)
                A(dtlo[:, tsl(q)], PS[3 * BC:XP, k + q, :], ACT.Copy).then_inc(sm(f"dtlo_ready{ly}"), 1)
                A(CS[ly][:, tsl(q)], PS[0:3 * BC, k + q, :], ACT.Copy).then_inc(sm(f"bc1_ready{ly}"), 1)

            def softplus(ly, q, k):
                act_e.wait_ge(sm(f"pre_done{ly}"), q + 1)
                for h in range(NH):
                    bias = chan[:, ly, h, 1:2]
                    A(s_abs[q][:, h], bank(k + h), ACT.Abs, bias=bias)
                    ins = A(s_relu[q][:, h], bank(k + h), ACT.Relu, bias=bias)
                ins.then_inc(sm(f"pre_read{ly}"), 1)

            def softplus_exp(ly, q):
                act_e.wait_ge(sm(f"pre_read{ly}"), q + 1)
                A(s_exp[q], s_abs[q], ACT.Exp, scale=-1.0).then_inc(sm(f"exp_ready{ly}"), 1)
                act_e.wait_ge(sm(f"exp_ready{ly}"), q + 1)

            def softplus_log(ly, q):
                A(s_ln[q], s_exp[q], ACT.Ln, bias=1.0).then_inc(sm(f"sp_ready{ly}"), 1)

            def split_hi(c, p):
                if p == 0:
                    act_e.wait_ge(sm(f"ld_raw{c % 2}"), 32 * (c // 2 + 1))
                if p == 0 and c >= 2:
                    act_e.wait_ge(sm("gu_ready"), CSTEPS * (c - 1))
                if p == 6 and c >= 2:
                    act_e.wait_ge(sm("down_ready"), CSTEPS * (c - 1))
                z = slice(p * WP, (p + 1) * WP)
                A(whi[c % 2][:, z], raw[c % 2][:, z], ACT.Copy).then_inc(sm("whi_done"), 1)

            def exp1(k):
                n, b = divmod(k, B)
                if k == 0:
                    act_e.wait_ge(sm("dA_zero"), 3)
                    act_e.wait_ge(sm("du_ready1"), 1)
                    act_e.wait_ge(sm("du_ready1b"), 1)
                if k >= 2:
                    act_e.wait_ge(sm("scan1"), k - 1)
                for h in range(NH):
                    ins = A(dA1[:, k % 2, h, 1:], delta[:, h, b * L + 1:(b + 1) * L], ACT.Exp,
                            scale=Aneg[:, 1, h, n:n + 1])
                ins.then_inc(sm("exp1"), 1)

            def copy_B(k):
                act_e.wait_ge(sm("bb0_ready"), k + 1)
                if k >= 2:
                    act_e.wait_ge(sm("bmul0"), k - 1)
                A(Bs[:, k % 2], bank(4), ACT.Copy).then_inc(sm("Bs_ready"), 1)

            def exp0(k):
                q, n = divmod(k, DS)
                if k >= 2:
                    act_e.wait_ge(sm("scan0"), k - 1)
                for h in range(NH):
                    src = delta[:, h, tsl(q)].rearrange("p (b l) -> p b l", b=2)[:, :, 1:]
                    dst = bank(2 * (k % 2) + h).rearrange("p (b l) -> p b l", b=2)[:, :, 1:]
                    ins = A(dst, src, ACT.Exp, scale=Aneg[:, 0, h, n:n + 1])
                ins.then_inc(sm("exp0"), 1)

            act_e.wait_ge(sm("tap_ready1"), 1)
            A(tap_parts[1][0], taps[1], ACT.Copy).then_inc(sm("tap_hi_ready1"), 1)
            for q in range(2):
                before_u(0, q, s_abs[q], 2 * q)
            evacuate_proj(0, 0, 4)
            softplus(0, 0, 0)
            evacuate_proj(0, 1, 4)
            softplus_exp(0, 0)
            softplus_log(0, 0)
            softplus(0, 1, 2)
            softplus_exp(0, 1)
            softplus_log(0, 1)
            act_e.wait_ge(sm("ld_gates"), 32)
            before_u(1, 0, raw[0][:, 0:1024].rearrange("p (h t) -> p h t", h=NH), 6)
            act_e.wait_ge(sm("du_ready0"), 1)
            act_e.wait_ge(sm("dA_zero"), 1)
            copy_B(0)
            exp0(0)
            copy_B(1)
            before_u(1, 1, rt[:, 0:2].rearrange("p i j e -> p i (j e)"), 2)
            act_e.wait_ge(sm("dA_zero"), 2)
            for k in range(U0):
                if k >= 1:
                    exp0(k)
                if k + 2 < U0:
                    copy_B(k + 2)
                if k == U0 - 1:
                    evacuate_proj(1, 0, 4)
                if k in (1, 3):
                    z = slice(512 * (k - 1), 512 * (k + 1))
                    act_e.wait_ge(sm("z_ready"), 2)
                    A(ztan[:, z], szf[:, z], ACT.Tanh, scale=0.5).then_inc(sm("ztan_ready"), 1)
                if k == 3:
                    link(A(gates[:], gates_in[:], ACT.Tanh))
                    A(hgates[:], gates[:], ACT.Copy, scale=0.5).then_inc(sm("gates_ready"), 1)
                    A(gwhi[:], gwT[:], ACT.Copy).then_inc(sm("gwhi_ready"), 1)
                if k in WSUM_UNITS:
                    m, i = WSUM_UNITS[k]
                    z = slice(i * 512, (i + 1) * 512)
                    act_e.wait_ge(sm("ld_wq"), 16 * (m + 1))
                    A(wq[2][:, z], raw[0][:, z], ACT.Abs, accum_out=wsum[:, m, i:i + 1]).then_inc(sm("wsum_ready"), 1)
                if k >= 27:
                    for p in range(2 * (k - 27), min(2 * (k - 27) + 2, 9)):
                        split_hi(0, p)

            def turn_hi(k):
                act_e.wait_ge(sm("xT_ready"), k + 1)
                A(xThi[:, k % 2, tsl(k // 2)], bank((6, 7, 4, 5)[k]), ACT.Copy).then_inc(sm("xhi_ready"), 1)

            evacuate_proj(1, 1, 4)
            act_e.wait_ge(sm("bmul0"), U0)
            act_e.wait_ge(sm("ysum0"), U0 - 1)
            softplus(1, 0, 0)
            softplus_exp(1, 0)
            softplus_log(1, 0)
            turn_hi(0)
            turn_hi(1)
            act_e.wait_ge(sm("y0T_ready"), 2)
            softplus(1, 1, 2)
            turn_hi(2)
            turn_hi(3)
            softplus_exp(1, 1)
            softplus_log(1, 1)
            for q in range(2):
                act_e.wait_ge(sm("lgT_ready"), q + 1)
                A(lgT[:, tsl(q)], PS[0:E, 6 - 2 * q, :], ACT.Copy).then_inc(sm("lgT_copied"), 1)
            act_e.wait_ge(sm("lsub_ready"), 1)
            A(probs, left, ACT.Exp).then_inc(sm("pexp_ready"), 1)

            def tanh_gate(s):
                act_e.wait_ge(sm("gu_ready"), s + 1)
                if s == 0:
                    act_e.wait_ge(sm("du_ready1"), 1)
                if s >= 2:
                    act_e.wait_ge(sm("gated"), s - 1)
                A(tg[:, s % 2], PS[:, s % 2, :], ACT.Tanh, scale=0.5).then_inc(sm("tanh_done"), 1)

            tanh_gate(0)
            tanh_gate(1)

            def comb_copy(m):
                act_e.wait_ge(sm("cb_ready"), m + 1)
                if m >= 2:
                    act_e.wait_ge(sm("wmul_done"), CB * (m - 1))
                A(combB[:, m % 2], PS[:, comb_bank(m), :], ACT.Copy).then_inc(sm("combB_ready"), 1)

            def pick_experts(c):
                if c >= 2:
                    act_e.wait_ge(sm("cb_ready"), 2 * (c - 1))
                A(pick[:, c % 2].rearrange("p (e f) -> p e f", e=EC),
                  eye2[:, EC * c:EC * c + EC].bitcast(F32).unsqueeze(2).broadcast_to([P, EC, I // CB]), ACT.Copy
                  ).then_inc(sm("pick_ready"), 1)

            act_e.wait_ge(sm("eye_ready"), 1)
            pick_experts(0)
            for s in range(STEPS + 1):
                c, j = divmod(s, CSTEPS)
                m = s // CB
                if 2 <= s < STEPS:
                    tanh_gate(s)
                if s >= 1:
                    r = s - 1
                    act_e.wait_ge(sm("wmul_done"), r + 1)
                    if r >= 2:
                        act_e.wait_ge(sm("down_ready"), r - 1)
                    A(ahi[:, r % 2], actw[:, r % 2], ACT.Copy).then_inc(sm("ahi_done"), 1)
                if s < STEPS:
                    if s == 0:
                        act_e.wait_ge(sm("combT_turned"), 1)
                        A(combT[:], bank(4, 2), ACT.Copy).then_inc(sm("combT_ready"), 1)
                        comb_copy(0)
                        exp1(0)
                    if s % CB == 0 and m + 1 < NPAIR:
                        comb_copy(m + 1)
                    if s % CB == 0 and m >= 1:
                        exp1(2 * m)
                    if s % CB == 2:
                        exp1(2 * m + 1)
                        if m % 2 == 0 and c + 1 < NCH:
                            pick_experts(c + 1)
                    if c + 1 < NCH:
                        for p in parts(j):
                            split_hi(c + 1, p)
            for q in range(2):
                act_e.wait_ge(sm("z_ready"), 3 + q)
                A(work[:, 0, q * 1024:(q + 1) * 1024], szf[:, q * 1024:(q + 1) * 1024], ACT.Tanh, scale=0.5
                  ).then_inc(sm("ztan_ready"), 1)

            for k in range(4):
                act_e.wait_ge(sm("x3T_ready"), k + 1)
                A(xT3[:, k % 2, tsl(k // 2)], bank(k), ACT.Copy).then_inc(sm("xT3_done"), 1)

            def copy_q1T(q):
                act_e.wait_ge(sm("q1T_ready"), q + 1)
                A(q1T[:, :, tsl(q)], PS[:, 4 + q, :].bitcast(BF16).rearrange("p (k t) -> p k t", k=2), ACT.Copy
                  ).then_inc(sm("q1T_done"), 1)

            copy_q1T(0)
            for t in range(NT + 4):
                if 2 <= t < NT + 2:
                    r = t - 2
                    act_e.wait_ge(sm("ffn_tr"), r + 1)
                    if r >= 2:
                        act_e.wait_ge(sm("ffn_had"), r - 1)
                    A(bT[:, r % 2].rearrange("p k t -> p (k t)"), bank(4, 2), ACT.Copy).then_inc(sm("ffn_bT"), 1)
                if 3 <= t < NT + 3:
                    r = t - 3
                    act_e.wait_ge(sm("ffn_scales"), r + 1)
                    if r >= 1:
                        act_e.wait_ge(sm("ffn_qh"), r)
                    A(fq, bank(6, 2), ACT.Copy, scale=ft[:, r % 3, 3:4]).then_inc(sm("ffn_qa"), 1)
                if t < NT:
                    if t % 4 == 0:
                        act_e.wait_ge(sm("tok_ready"), t // 4 + 1)
                    act_e.wait_ge(sm("ffn_gu"), t + 1)
                    if t >= 1:
                        act_e.wait_ge(sm("ffn_b"), t)
                    A(fth, bank(0, 2), ACT.Tanh, scale=tok[:, 3, t:t + 1]).then_inc(sm("ffn_tanh"), 1)
                    if t == 0:
                        copy_q1T(1)
                if 3 <= t < NT + 3:
                    r = t - 3
                    act_e.wait_ge(sm("ffn_qtr"), r + 1)
                    if r >= 2:
                        act_e.wait_ge(sm("ffn_down"), r - 1)
                    A(qhT[:, r % 2].rearrange("p k t -> p (k t)"), PS[:, 4, :].bitcast(BF16), ACT.Copy).then_inc(sm("ffn_qhT"), 1)

        @block.tensor
        def _(pe):
            def conv(ly, q, k):
                for n, (t, x) in enumerate(((0, 0), (0, 1), (1, 0))):
                    if q == 0 and ly == 0 and n == 1:
                        pe.wait_ge(sm("ctx_lo_ready"), 1)
                    if q == 0 and n == 2:
                        pe.wait_ge(sm(f"tap_lo_ready{ly}"), 1)
                    for h in range(NH):
                        for c in range(DC):
                            ins = pe.matmul(bank(k + h), tap_parts[ly][t][:, c, h * P:(h + 1) * P],
                                            ctx_parts[x][:, 2 * q:2 * q + 2, c:c + L],
                                            start=(n == 0 and c == 0), stop=(n == 2 and c == DC - 1))
                ins.then_inc(sm(f"conv_done{ly}"), 1)

            def proj(ly, q, k):
                pe.wait_ge(sm(f"u_ready{ly}"), q + 1)
                for h in range(NH):
                    ins = pe.matmul(PS[0:XP, k + q, :], xpw[:, ly, h, :], us[ly][:, h, tsl(q)],
                                    start=(h == 0), stop=(h == NH - 1))
                ins.then_inc(sm(f"proj_done{ly}"), 1)

            def dt_proj(ly, q, k):
                pe.wait_ge(sm(f"dtlo_ready{ly}"), q + 1)
                for h in range(NH):
                    ins = pe.matmul(bank(k + h), dtw[:, ly, h * P:(h + 1) * P], dtlo[:, tsl(q)], start=True, stop=True)
                ins.then_inc(sm(f"pre_done{ly}"), 1)

            pe.wait_ge(sm("ctx_hi_ready"), 1)
            pe.wait_ge(sm("tap_hi_ready0"), 1)
            conv(0, 0, 0)
            conv(0, 1, 2)
            pe.wait_ge(sm("ld_w0"), 32)
            for q in range(2):
                proj(0, q, 4)
                dt_proj(0, q, 2 * q)
            def bb0(k):
                q, n = divmod(k, DS)
                if k >= 1:
                    pe.wait_ge(sm("Bs_ready"), k)
                pe.matmul(bank(4), sel[:, n, :], CS[0][:, tsl(q)], start=True, stop=True).then_inc(sm("bb0_ready"), 1)

            def cb0(k):
                q, n = divmod(k, DS)
                if k >= 1:
                    pe.wait_ge(sm("cmul0"), k)
                pe.matmul(bank(5), sel[:, DS + n, :], CS[0][:, tsl(q)], start=True, stop=True).then_inc(sm("cb0_ready"), 1)

            def ysum0(k):
                q, n = divmod(k, DS)
                if k == DS:
                    pe.wait_ge(sm("x1_done"), 1)
                pe.wait_ge(sm("cmul0"), k + 1)
                for h in range(NH):
                    ins = pe.matmul(bank(6 + h), ident[:], prod0[:, k % 2, h], start=(n == 0), stop=(n == DS - 1))
                ins.then_inc(sm("ysum0"), 1)

            def turn_y0(q):
                pe.wait_ge(sm("yg_ready"), q + 1)
                for j in range(4):
                    for h in range(NH):
                        o = (j % 2) * DI + h * P
                        ins = pe.transpose(PS[:, 6 + j // 2, o:o + P], yg[:, h, j * P:(j + 1) * P], ident[:])
                ins.then_inc(sm("y0T_ready"), 1)

            def turn_x(q):
                pe.wait_ge(sm("xn_ready"), q + 1)
                for k in range(2):
                    for j in range(4):
                        ins = pe.transpose(PS[:, 6 - 2 * q + k, j * P:(j + 1) * P],
                                           sz[:, 4 * q + j, k * P:(k + 1) * P], ident[:])
                    ins.then_inc(sm("xT_ready"), 1)

            pe.wait_ge(sm("tap_hi_ready1"), 1)
            conv(1, 0, 6)
            pe.wait_ge(sm("ld_const"), 64)
            pe.wait_ge(sm("bc_ready0"), 2)
            bb0(0)
            pe.wait_ge(sm("pre_read0"), 2)
            conv(1, 1, 2)
            bb0(1)
            cb0(0)
            bb0(2)
            for k in range(U0 + 1):
                if k + 3 < U0 and k != DS + 2:
                    bb0(k + 3)
                if k == DS + 1:
                    turn_y0(0)
                if 1 <= k < U0:
                    cb0(k)
                if k == DS + 1:
                    bb0(k + 4)
                if k >= 1:
                    ysum0(k - 1)
                if k == U0 - 2:
                    pe.wait_ge(sm("ld_w1"), 32)
                    pe.wait_ge(sm("Bs_ready"), U0)
                    proj(1, 0, 4)
            proj(1, 1, 4)
            dt_proj(1, 0, 0)

            def logitsT(q):
                n = 0
                for i, xw in enumerate((xThi, xTlo)):
                    pe.wait_ge(sm(("xhi_ready", "xlo_ready")[i]), 2 * q + 2)
                    if i == 0:
                        pe.wait_ge(sm("xlo_ready"), 2 * q + 1)
                    for gw in (gwlo, gwhi):
                        for k in range(2):
                            ins = pe.matmul(PS[0:E, 6 - 2 * q, :], gw[:, k, :], xw[:, k, tsl(q)], start=(n == 0), stop=(n == 7))
                            n += 1
                ins.then_inc(sm("lgT_ready"), 1)

            turn_y0(1)
            dt_proj(1, 1, 2)
            pe.wait_ge(sm("x1_done"), 2)
            turn_x(0)
            pe.wait_ge(sm("bc_ready1"), 2)
            turn_x(1)
            pe.wait_ge(sm("gw_ready"), 1)
            logitsT(0)
            logitsT(1)
            pe.wait_ge(sm("wsum_ready"), 12)
            pe.wait_ge(sm("ones_ready"), 1)
            pe.matmul(PS[:, 5, 0:12], ones[:], wsum[:].rearrange("p m i -> p (m i)"), start=True, stop=True).then_inc(sm("wtot_ready"), 1)
            pe.wait_ge(sm("lgT_copied"), 2)
            for j in range(NT):
                ins = pe.transpose(PS[:, 7, j * E:(j + 1) * E], lgT[:, j * P:(j + 1) * P], ident[0:E, 0:E])
            ins.then_inc(sm("logits_ready"), 1)

            def bc1(k):
                n, b = divmod(k, B)
                if k == 0:
                    pe.wait_ge(sm("bc_ready1"), 2)
                if k % 2 == 0:
                    if k >= 2:
                        pe.wait_ge(sm("cmul1"), k)
                    else:
                        pe.wait_ge(sm("combB_ready"), 1)
                else:
                    pe.wait_ge(sm("combB_ready"), min((k + 3) // 2, NPAIR))
                    if k >= 3:
                        pe.wait_ge(sm("cmul1"), k - 2)
                for i in range(2):
                    ins = pe.matmul(PS[:, scan_bank(k), i * L:(i + 1) * L], sel[:, i * DS + n, :],
                                    CS[1][:, b * L:(b + 1) * L], start=True, stop=True)
                ins.then_inc(sm("bc1_done"), 1)

            def spread_comb(m):
                c, q = divmod(m, 2)
                pe.wait_ge(sm("pick_ready"), c + 1)
                if m >= 2:
                    pe.wait_ge(sm("cmul1"), 2 * m - 3)
                pe.matmul(PS[:, comb_bank(m), :], pick[:, c % 2], combT[:, tsl(q)], start=True, stop=True).then_inc(sm("cb_ready"), 1)

            def gate_up(s):
                c, j = divmod(s, CSTEPS)
                q, b = divmod(j, CB)
                if j == 0:
                    pe.wait_ge(sm("wlo_done"), 9 * c + 6)
                if s >= 2:
                    pe.wait_ge(sm("umul_done"), s - 1)
                if s == 0:
                    pe.wait_ge(sm("pre_read1"), 2)
                hi = whi[c % 2][:, 0:GUW].rearrange("p (k g f) -> p k g f", k=2, g=2)
                lo = wlo[c % 2][:, 0:GUW].rearrange("p (k g f) -> p k g f", k=2, g=2)
                for g in range(2):
                    n = 0
                    for xw, w in ((xTlo, hi), (xThi, lo), (xThi, hi)):
                        for k in range(2):
                            ins = pe.matmul(PS[:, 2 * g + s % 2, :], w[:, k, g, b * P:(b + 1) * P], xw[:, k, tsl(q)],
                                            start=(n == 0), stop=(n == 5))
                            n += 1
                ins.then_inc(sm("gu_ready"), 1)

            def down(s):
                c, j = divmod(s, CSTEPS)
                b = j % CB
                if j == 0:
                    pe.wait_ge(sm("wlo_done"), 9 * c + 9)
                pe.wait_ge(sm("alo_done"), s + 1)
                if b == 0 and s >= CB:
                    pe.wait_ge(sm("acc_done"), s // CB)
                hi = whi[c % 2][:, GUW:].rearrange("p (k f) -> p k f", k=CB)
                lo = wlo[c % 2][:, GUW:].rearrange("p (k f) -> p k f", k=CB)
                for h in range(NH):
                    for n, (aw, w) in enumerate(((alo, hi), (ahi, lo), (ahi, hi))):
                        ins = pe.matmul(bank(4 + h), w[:, b, h * P:(h + 1) * P], aw[:, s % 2],
                                        start=(b == 0 and n == 0), stop=(b == CB - 1 and n == 2))
                ins.then_inc(sm("down_ready"), 1)

            def turn_acc(q):
                pe.wait_ge(sm("acc_done"), NPAIR - 1 + q)
                pe.wait_ge(sm("umul_done"), STEPS - 1 + q)
                for j in range(4 * q, 4 * q + 4):
                    for h in range(NH):
                        o = (j % 2) * D + h * P
                        ins = pe.transpose(PS[:, q + 2 * (j // 2 % 2), o:o + P], accT[:, h, j * P:(j + 1) * P], ident[:])
                ins.then_inc(sm("x2T_ready"), 1)

            for s in range(STEPS + 2):
                m, b = divmod(s, CB)
                if s == 0:
                    gate_up(0)
                    gate_up(1)
                elif 4 <= s < STEPS:
                    gate_up(s)
                if s == STEPS:
                    turn_acc(0)
                if s == 0:
                    pe.wait_ge(sm("comb_ready"), 1)
                    for j in range(NT):
                        ins = pe.transpose(PS[:, 4 + j // 4, (j % 4) * P:(j % 4 + 1) * P], comb2[:, j], ident[:])
                    ins.then_inc(sm("combT_turned"), 1)
                    pe.wait_ge(sm("combT_ready"), 1)
                    spread_comb(0)
                    pe.wait_ge(sm("wstat_ready"), 1)
                    spread_comb(1)
                    gate_up(2)
                    bc1(0)
                    gate_up(3)
                if s < STEPS:
                    if b == 0 and 1 <= m < NPAIR - 1:
                        spread_comb(m + 1)
                    if b == 1 and m >= 1:
                        bc1(2 * m)
                    if b == 2:
                        bc1(2 * m + 1)
                if s >= 2:
                    down(s - 2)
            turn_acc(1)

            for q in range(2):
                pe.wait_ge(sm("yz_ready"), q + 1)
                if q == 1:
                    pe.wait_ge(sm("cmul1"), U1)
                for j in range(4 * q, 4 * q + 4):
                    for h in range(NH):
                        o = (j % 2) * DI + h * P
                        ins = pe.transpose(PS[:, 4 + j // 2, o:o + P], y1[:, h, j * P:(j + 1) * P], ident[:])
                ins.then_inc(sm("y1T_ready"), 1)

            pe.wait_ge(sm("x2_done"), 2)
            pe.wait_ge(sm("ld_had"), 16)
            for q in range(2):
                pe.wait_ge(sm("xn3_ready"), q + 1)
                for k in range(2):
                    for j in range(4):
                        ins = pe.transpose(PS[:, 2 * q + k, j * P:(j + 1) * P],
                                           sz[:, 4 * q + j, k * P:(k + 1) * P], ident[:])
                    ins.then_inc(sm("x3T_ready"), 1)
                pe.wait_ge(sm("xT3_done"), 2 * q + 2)
                for j in range(4 * q, 4 * q + 4):
                    for k in range(2):
                        ins = pe.matmul(PS[:, 4 + j // 2, (j % 2) * D:(j % 2 + 1) * D], xT3[:, k, j * P:(j + 1) * P],
                                        had[:, k, :], start=(k == 0), stop=(k == 1))
                ins.then_inc(sm("had_ready"), 1)

            def turn_q1(q):
                pe.wait_ge(sm("q1_ready"), q + 1)
                for j in range(4):
                    for k in range(2):
                        ins = pe.transpose(PS[:, 4 + q, :].bitcast(BF16)[:, k * HT + j * P:k * HT + (j + 1) * P],
                                           q1[:, 4 * q + j, k * P:(k + 1) * P], identb[:])
                ins.then_inc(sm("q1T_ready"), 1)

            turn_q1(0)
            pe.wait_ge(sm("q1T_done"), 1)
            wg = wq[0][:].rearrange("p (k f) -> p k f", k=2)
            wu = wq[1][:].rearrange("p (k f) -> p k f", k=2)
            wd = wq[2][:].rearrange("p (k f) -> p k f", k=HB)
            def transform(r, i):
                if i == 0:
                    pe.wait_ge(sm("ffn_bT"), r + 1)
                    if r >= 1:
                        pe.wait_ge(sm("ffn_qa"), r)
                for g in (2 * i, 2 * i + 1):
                    for k in range(2):
                        ins = pe.matmul(PS[:, 6 + i, (g % 2) * D:(g % 2 + 1) * D], bT[:, r % 2, 2 * g + k, :],
                                        had[:, k, :], start=(k == 0), stop=(k == 1))
                if i == 1:
                    ins.then_inc(sm("ffn_had"), 1)

            for t in range(NT + 4):
                if t < NT:
                    if t == 1:
                        turn_q1(1)
                        pe.wait_ge(sm("q1T_done"), 2)
                    if t >= 1:
                        pe.wait_ge(sm("ffn_b"), t)
                    for g, w in enumerate((wg, wu)):
                        for q in range(2):
                            for k in range(2):
                                ins = pe.matmul(PS[:, 2 * g + q, :], q1T[:, k, t * P:(t + 1) * P],
                                                w[:, k, q * 512:(q + 1) * 512], start=(k == 0), stop=(k == 1))
                    ins.then_inc(sm("ffn_gu"), 1)
                if t >= 4:
                    r = t - 4
                    pe.wait_ge(sm("ffn_qhT"), r + 1)
                    pe.wait_ge(sm("ffn_bT"), min(r + 3, NT))
                    if r >= 1:
                        pe.wait_ge(sm("out_ready"), r)
                    for k in range(HB):
                        ins = pe.matmul(PS[:, 5, 0:D], qhT[:, r % 2, k, :], wd[:, k, :], start=(k == 0), stop=(k == HB - 1))
                    ins.then_inc(sm("ffn_down"), 1)
                if 2 <= t < NT + 2:
                    transform(t - 2, 0)
                if 3 <= t < NT + 3:
                    r = t - 3
                    pe.wait_ge(sm("ffn_qh"), r + 1)
                    pe.wait_ge(sm("ffn_bT"), min(r + 2, NT))
                    if r >= 1:
                        pe.wait_ge(sm("ffn_qhT"), r)
                    for k in range(HB):
                        ins = pe.transpose(PS[:, 4, :].bitcast(BF16)[:, k * P:(k + 1) * P],
                                           qh[:, r % 2, k * P:(k + 1) * P], identb[:])
                    ins.then_inc(sm("ffn_qtr"), 1)
                if 2 <= t < NT + 2:
                    transform(t - 2, 1)
                if 1 <= t < NT + 1:
                    r = t - 1
                    pe.wait_ge(sm("ffn_mix"), r + 1)
                    if r >= 1:
                        pe.wait_ge(sm("ffn_bT"), r)
                    if r >= 3:
                        pe.wait_ge(sm("out_ready"), r - 2)
                    for k in (4, 5, 6, 7, 0, 1, 2, 3):
                        if k == 0 and r >= 2:
                            pe.wait_ge(sm("ffn_qhT"), r - 1)
                        ins = pe.transpose(PS[:, 4 + k // 4, (k % 4) * P:(k % 4 + 1) * P],
                                           fo[:, r % 2, k * P:(k + 1) * P], ident[:])
                    ins.then_inc(sm("ffn_tr"), 1)

        @block.vector
        def _(v):
            link = chain(v, "dve_own")

            def norm_stats(q):
                z = xhalf(q)
                for j in range(z.start, z.stop):
                    ins = v.bn_stats(stats[:, j], xs[:, j])
                link(ins)
                for j in range(z.start, z.stop):
                    ins = v.bn_aggr(mv[:, j], stats[:, j])
                link(ins)
                v.tensor_scalar(rstd[:, z], mv[:, z, 1], LN_EPS, None, ALU.add).then_inc(sm("var_ready"), 1)

            def normalise(n, q):
                v.wait_ge(sm("rstd_ready"), 2 * (n - 1) + q + 1)
                for j in range(4 * q, 4 * q + 4):
                    ins = v.tensor_scalar(sz[:, j], xs[:, j], mv[:, j, 0:1], rstd[:, j:j + 1], ALU.subtract, ALU.mult)
                return ins

            def make_u(ly, q, th):
                v.wait_ge(sm(f"pre_u{ly}"), q + 1)
                z = us[ly][:, :, tsl(q)]
                v.scalar_tensor_tensor(out=z, in0=th, scalar=1.0, in1=z, op0=ALU.add, op1=ALU.mult
                                       ).then_inc(sm(f"u_ready{ly}"), 1)

            def split_bc(ly, q, k):
                z = tsl(q)
                lo = slice(2 * BC, 3 * BC)
                v.wait_ge(sm(f"bc1_ready{ly}"), q + 1)
                link(v.tensor_tensor(R0[:, z], PS[0:3 * BC, k + q, :], CS[ly][:, z], ALU.subtract))
                v.tensor_copy(CS[ly][BC:2 * BC, z], R0[BC:2 * BC, z])
                link(v.tensor_copy(CS[ly][lo, z], R0[lo, z]))
                v.tensor_tensor(CS[ly][lo, z], R0[lo, z], CS[ly][lo, z], ALU.subtract).then_inc(sm(f"bc_ready{ly}"), 1)

            def make_delta(ly, q):
                v.wait_ge(sm(f"sp_ready{ly}"), q + 1)
                v.tensor_scalar(s_abs[q], s_exp[q], 1.0, -1.0, ALU.add, ALU.add)
                link(v.tensor_tensor(s_relu[q], s_ln[q], s_relu[q], ALU.add))
                link(v.tensor_tensor(s_exp[q], s_exp[q], s_abs[q], ALU.subtract))

            def finish_delta(ly, q):
                z = tsl(q)
                link(v.tensor_tensor(delta[:, :, z], s_relu[q], s_exp[q], ALU.add))
                v.tensor_tensor(du[:, :, z], delta[:, :, z], us[ly][:, :, z], ALU.mult).then_inc(sm(f"du_ready{ly}"), 1)

            v.wait_ge(sm("ld_taps0"), 32)
            v.tensor_tensor(taps[0], taps[0], inw[:, 0:1, :].broadcast_to([P, DC, DI]), ALU.mult
                            ).then_inc(sm("tap_ready0"), 1)
            v.wait_ge(sm("ctx_hi_ready"), 1)
            v.tensor_tensor(ctx_parts[1], ctxp[:], ctx_parts[0].bitcast(F32), ALU.subtract).then_inc(sm("ctx_lo_ready"), 1)
            v.wait_ge(sm("tap_hi_ready0"), 1)
            v.wait_ge(sm("tap_ready0"), 1)
            v.tensor_tensor(tap_parts[0][1], taps[0], tap_parts[0][0].bitcast(F32), ALU.subtract
                            ).then_inc(sm("tap_lo_ready0"), 1)
            v.wait_ge(sm("ld_x"), 16)
            for q in range(2):
                norm_stats(q)
            for q in range(2):
                make_u(0, q, s_abs[q])
            for q in range(2):
                split_bc(0, q, 4)
            for q in range(2):
                normalise(1, q).then_inc(sm("z_ready"), 1)
            v.wait_ge(sm("pre_read0"), 2)
            v.memset(PS[:, 0:2, 0:512:L], 0.0).then_inc(sm("dA_zero"), 1)
            for q in range(2):
                make_delta(0, q)
                finish_delta(0, q)
            make_u(1, 0, raw[0][:, 0:1024].rearrange("p (h t) -> p h t", h=NH))

            def scan0(k):
                v.wait_ge(sm("exp0"), k + 1)
                v.wait_ge(sm("bmul0"), k + 1)
                if k >= 3:
                    v.wait_ge(sm("cmul0"), k - 2)
                v.tensor_tensor_scan(h0[k % 3].rearrange("p h t -> p (h t)"), bank(2 * (k % 2), 2),
                                     dBu0[:, k % 2].rearrange("p h t -> p (h t)"), 0.0, ALU.mult, ALU.add
                                     ).then_inc(sm("scan0"), 1)

            def cmul0(k):
                v.wait_ge(sm("scan0"), k + 1)
                v.wait_ge(sm("cb0_ready"), k + 1)
                if k >= 2:
                    v.wait_ge(sm("ysum0"), k - 1)
                v.tensor_tensor(prod0[:, k % 2], h0[k % 3], PS[:, 5:6, :].broadcast_to([P, NH, HT]), ALU.mult
                                ).then_inc(sm("cmul0"), 1)

            def gate_y0(q):
                v.wait_ge(sm("ysum0"), (q + 1) * DS)
                for h in range(NH):
                    ins = v.scalar_tensor_tensor(out=yg[:, h], in0=us[0][:, h, tsl(q)], scalar=chan[:, 0, h, 2:3],
                                                 in1=bank(6 + h), op0=ALU.mult, op1=ALU.add)
                link(ins)
                for h in range(NH):
                    z = yg[:, h].rearrange("p (b l) -> p b l", b=2)
                    ins = v.tensor_tensor(z, z, sz[:, 4 * q + h:4 * q + h + 3:2, :], ALU.mult)
                ins.then_inc(sm("yg_ready"), 1)

            def add_y0(q):
                v.wait_ge(sm("y0T_ready"), q + 1)
                if q == 0:
                    v.wait_ge(sm("gates_ready"), 1)
                xv = xs[:, xhalf(q)].rearrange("p j d -> p (j d)")
                v.scalar_tensor_tensor(out=xv, in0=bank(6, 2), scalar=hgates[:, 0:1], in1=xv,
                                       op0=ALU.mult, op1=ALU.add).then_inc(sm("x1_done"), 1)

            for k in range(U0 + 1):
                if k < U0:
                    scan0(k)
                if k == DS + 1:
                    gate_y0(0)
                if k == DS + 2:
                    add_y0(0)
                if k >= 1:
                    cmul0(k - 1)
                if k == 0:
                    v.wait_ge(sm("pre_u1"), 2)
                    v.memset(PS[:, 2:4, 0:512:L], 0.0).then_inc(sm("dA_zero"), 1)
                    make_u(1, 1, rt[:, 0:2].rearrange("p i j e -> p i (j e)"))
                if k == 4:
                    v.wait_ge(sm("ld_const"), 64)
                    v.tensor_tensor(eye2[:], ident[:, 0:E], ident[:, E:], ALU.add).then_inc(sm("eye_ready"), 1)
                    v.wait_ge(sm("gwhi_ready"), 1)
                    v.tensor_tensor(gwlo[:], gwT[:], gwhi[:].bitcast(F32), ALU.subtract).then_inc(sm("gw_ready"), 1)
                if k == 5:
                    v.wait_ge(sm("ztan_ready"), 2)
                    v.scalar_tensor_tensor(out=szf, in0=ztan, scalar=1.0, in1=szf, op0=ALU.add, op1=ALU.mult
                                           ).then_inc(sm("sz0_ready"), 1)
                    v.wait_ge(sm("sz0_ready"), 1)
                if k == DS + 3:
                    v.wait_ge(sm("x1_done"), 1)
                    norm_stats(0)
                if k == DS + 6:
                    normalise(2, 0).then_inc(sm("xn_ready"), 1)

            def lo_x(k):
                v.wait_ge(sm("xhi_ready"), k + 1)
                z = (slice(None), k % 2, tsl(k // 2))
                v.tensor_tensor(xTlo[z], bank((6, 7, 4, 5)[k]), xThi[z].bitcast(F32), ALU.subtract).then_inc(sm("xlo_ready"), 1)

            split_bc(1, 0, 4)
            gate_y0(1)
            split_bc(1, 1, 4)
            add_y0(1)
            v.wait_ge(sm("x1_done"), 2)
            norm_stats(1)
            normalise(2, 1).then_inc(sm("xn_ready"), 1)
            lo_x(0)
            lo_x(1)
            make_delta(1, 0)
            lo_x(2)
            lo_x(3)
            finish_delta(1, 0)
            v.wait_ge(sm("exp_ready1"), 2)
            v.tensor_scalar(s_abs[1], s_exp[1], 1.0, -1.0, ALU.add, ALU.add).then_inc(sm("round_ready"), 1)

            def gate(s):
                v.wait_ge(sm("tanh_done"), s + 1)
                if s == 0:
                    v.wait_ge(sm("du_ready1b"), 1)
                if s >= 2:
                    v.wait_ge(sm("umul_done"), s - 1)
                v.scalar_tensor_tensor(out=ga[:, s % 2], in0=tg[:, s % 2], scalar=1.0, in1=PS[:, s % 2, :],
                                       op0=ALU.add, op1=ALU.mult).then_inc(sm("gated"), 1)

            def times_up(s):
                v.wait_ge(sm("gated"), s + 1)
                if s >= 2:
                    v.wait_ge(sm("wmul_done"), s - 1)
                v.tensor_tensor(act[:, s % 2], ga[:, s % 2], PS[:, 2 + s % 2, :], ALU.mult).then_inc(sm("umul_done"), 1)

            v.wait_ge(sm("wtot_ready"), 1)
            link(v.tensor_reduce(wstat[:, 0, :], PS[:, 5, 0:12].rearrange("p (m i) -> p m i", m=3), AX.X, ALU.add))
            link(v.tensor_scalar(wstat[:, 1, :], wstat[:, 0, :], 1.0 / (HID * D), Q_EPS, ALU.mult, ALU.max))
            v.tensor_scalar(wstat[:, 2, :], wstat[:, 1, :], 0.5, None, ALU.mult)
            v.tensor_scalar(wstat[:, 3, :], wstat[:, 1, :], -0.5, None, ALU.mult).then_inc(sm("wstat_ready"), 1)
            v.wait_ge(sm("logits_ready"), 1)
            lg = bank(7).rearrange("p (j e) -> p j e", j=NT)
            link(v.tensor_reduce(rsm[:, 0, :], lg, AX.X, ALU.max))
            v.tensor_tensor(left, lg, rsm[:, 0, :].unsqueeze(2).broadcast_to([P, NT, E]), ALU.subtract).then_inc(sm("lsub_ready"), 1)
            v.wait_ge(sm("pexp_ready"), 1)
            link(v.tensor_reduce(rsm[:, 1, :], probs, AX.X, ALU.add))
            link(v.reciprocal(rsm[:, 2, :], rsm[:, 1, :]))
            link(v.tensor_tensor(probs, probs, rsm[:, 2, :].unsqueeze(2).broadcast_to([P, NT, E]), ALU.mult))
            for j in range(NT):
                ins = v.max(top8[:, j], probs[:, j])
            link(ins)
            for j in range(NT):
                ins = v.match_replace(left[:, j], top8[:, j], probs[:, j], 0.0)
            link(ins)
            link(v.tensor_reduce(rsm[:, 0, :], top8[:], AX.X, ALU.add))
            link(v.scalar_tensor_tensor(out=rsm[:, 1, :], in0=rsm[:, 0, :], scalar=0.0, in1=rsm[:, 0, :],
                                        op0=ALU.is_equal, op1=ALU.add))
            link(v.reciprocal(rsm[:, 2, :], rsm[:, 1, :]))
            link(v.tensor_scalar(rsm[:, 3, :], rsm[:, 2, :], hgates[:, 2:3], None, ALU.mult))
            link(v.tensor_tensor(left, probs, left, ALU.subtract))
            link(v.tensor_tensor(left, left, rsm[:, 3, :].unsqueeze(2).broadcast_to([P, NT, E]), ALU.mult))
            link(v.tensor_copy(comb2[:, :, 0:E].bitcast(F32R), left))
            v.tensor_tensor(comb2[:, :, E:], left, comb2[:, :, 0:E], ALU.subtract).then_inc(sm("comb_ready"), 1)
            for i in range(2):
                gate(i)
                times_up(i)

            def bmul1(k):
                b = k % B
                v.wait_ge(sm("bc1_done"), k + 1)
                if k >= 1:
                    v.wait_ge(sm("scan1"), k)
                v.tensor_tensor(dBu1, du[:, :, b * L:(b + 1) * L],
                                PS[:, scan_bank(k), 0:L].unsqueeze(1).broadcast_to([P, NH, L]), ALU.mult
                                ).then_inc(sm("bmul1"), 1)

            def scan1(k):
                v.wait_ge(sm("bmul1"), k + 1)
                v.wait_ge(sm("exp1"), k + 1)
                if k >= 1:
                    v.wait_ge(sm("cmul1"), k)
                v.tensor_tensor_scan(h1.rearrange("p h t -> p (h t)"), dA1[:, k % 2].rearrange("p h t -> p (h t)"),
                                     dBu1.rearrange("p h t -> p (h t)"), 0.0, ALU.mult, ALU.add
                                     ).then_inc(sm("scan1"), 1)

            def cmul1(k):
                v.wait_ge(sm("scan1"), k + 1)
                if k >= 2:
                    v.wait_ge(sm("yacc1"), k - 1)
                v.tensor_tensor(prod1[:, k % 2], h1, PS[:, scan_bank(k), L:2 * L].unsqueeze(1).broadcast_to([P, NH, L]),
                                ALU.mult).then_inc(sm("cmul1"), 1)

            def ternary(m, i):
                z = slice(i * 256, (i + 1) * 256)
                if i == 0:
                    v.wait_ge(sm("ld_wq2"), 16 * (m + 1))
                link(v.tensor_scalar(wq[m][:, z], wstage[:, z], wstat[:, 3, m:m + 1], None, ALU.is_lt))
                v.scalar_tensor_tensor(out=wq[m][:, z], in0=wstage[:, z], scalar=wstat[:, 2, m:m + 1],
                                       in1=wq[m][:, z], op0=ALU.is_gt, op1=ALU.subtract).then_inc(sm("wq_done"), 1)

            def gate_z1(q):
                z = szf[:, q * 1024:(q + 1) * 1024]
                v.wait_ge(sm("ztan_ready"), 3 + q)
                v.scalar_tensor_tensor(out=z, in0=work[:, 0, q * 1024:(q + 1) * 1024], scalar=1.0, in1=z,
                                       op0=ALU.add, op1=ALU.mult).then_inc(sm("sz1_ready"), 1)

            def add_experts(q):
                v.wait_ge(sm("x2T_ready"), q + 1)
                xv = xs[:, xhalf(q)].rearrange("p (a b) d -> p a (b d)", a=2)
                v.tensor_tensor(xv, xv, PS[:, q:q + 3:2, :], ALU.add).then_inc(sm("x2_done"), 1)

            for s in range(STEPS + 3):
                m, b = divmod(s, CB)
                if 2 <= s < STEPS:
                    gate(s)
                if s < STEPS and b == 2:
                    cmul1(2 * m)
                if b == 0 and 1 <= m <= NPAIR:
                    scan1(2 * m - 1)
                if 2 <= s < STEPS:
                    times_up(s)
                if s == 0:
                    v.wait_ge(sm("du_ready1"), 1)
                    for h in range(NH):
                        ins = v.tensor_scalar(y1[:, h], us[1][:, h], chan[:, 1, h, 2:3], None, ALU.mult)
                    link(ins)
                    v.memset(dA1[:, :, :, 0:1], 0.0).then_inc(sm("dA_zero"), 1)
                if 1 <= s <= STEPS:
                    r = s - 1
                    v.wait_ge(sm("ahi_done"), r + 1)
                    if r >= 2:
                        v.wait_ge(sm("down_ready"), r - 1)
                    v.tensor_tensor(alo[:, r % 2], actw[:, r % 2], ahi[:, r % 2].bitcast(F32), ALU.subtract
                                    ).then_inc(sm("alo_done"), 1)
                if b == 0 and 1 <= m <= NPAIR:
                    cmul1(2 * m - 1)
                if s >= 4 and (s - 2) % CB == 2:
                    r = (s - 2) // CB
                    q = r % 2
                    v.wait_ge(sm("down_ready"), CB * (r + 1))
                    if r < 2:
                        v.tensor_copy(accT[:, :, tsl(q)], PS[:, 4:6, :]).then_inc(sm("acc_done"), 1)
                    else:
                        v.wait_ge(sm("acc_done"), r - 1)
                        v.tensor_tensor(accT[:, :, tsl(q)], accT[:, :, tsl(q)], PS[:, 4:6, :], ALU.add
                                        ).then_inc(sm("acc_done"), 1)
                if s < STEPS and b == 1:
                    bmul1(2 * m)
                    scan1(2 * m)
                if s < STEPS and b == 2:
                    bmul1(2 * m + 1)
                if s in WQ_STEPS:
                    ternary(*WQ_STEPS[s])
                if s == STEPS:
                    add_experts(0)
            v.wait_ge(sm("x2_done"), 1)
            norm_stats(0)
            add_experts(1)
            normalise(3, 0).then_inc(sm("z_ready"), 1)
            v.wait_ge(sm("x2_done"), 2)
            norm_stats(1)
            gate_z1(0)
            normalise(3, 1).then_inc(sm("z_ready"), 1)
            gate_z1(1)

            def add_y1(q):
                v.wait_ge(sm("y1T_ready"), q + 1)
                xv = xs[:, xhalf(q)].rearrange("p j d -> p (j d)")
                v.scalar_tensor_tensor(out=xv, in0=bank(4 + 2 * q, 2), scalar=hgates[:, 1:2], in1=xv,
                                       op0=ALU.mult, op1=ALU.add).then_inc(sm("x3_done"), 1)
                v.wait_ge(sm("x3_done"), q + 1)
                norm_stats(q)

            add_y1(0)
            normalise(4, 0).then_inc(sm("xn3_ready"), 1)
            add_y1(1)
            normalise(4, 1).then_inc(sm("xn3_ready"), 1)

            v.tensor_scalar(tok[:, 6, 0:1], wstat[:, 1, 2:3], gates[:, 3:4], 1.0 / 127, ALU.mult, ALU.mult)
            for q in range(2):
                z = xhalf(q)
                v.wait_ge(sm("had_ready"), q + 1)
                hv = PS[:, 4 + 2 * q:6 + 2 * q, :].rearrange("p k (j d) -> p (k j) d", j=2)
                link(v.tensor_reduce(tok[:, 0, z], hv, AX.X, ALU.max, apply_absolute_value=True))
                link(v.tensor_scalar(tok[:, 1, z], tok[:, 0, z], Q_EPS, None, ALU.max))
                link(v.reciprocal(tok[:, 2, z], tok[:, 1, z]))
                link(v.tensor_scalar(tok[:, 2, z], tok[:, 2, z], 127.0, None, ALU.mult))
                for j in range(4):
                    i = 4 * q + j
                    ins = v.tensor_scalar(sz[:, i], hv[:, j], tok[:, 2, i:i + 1], 127.0, ALU.mult, ALU.min)
                link(ins)
                szq = szf[:, q * 1024:(q + 1) * 1024]
                link(v.tensor_scalar(szq, szq, -128.0, ROUND, ALU.max, ALU.add))
                v.tensor_scalar(q1[:, z].rearrange("p j d -> p (j d)"), szq, -ROUND, None, ALU.add).then_inc(sm("q1_ready"), 1)
                v.tensor_scalar(tok[:, 3, z], tok[:, 1, z], wstat[:, 1, 0:1], 0.5 / 127, ALU.mult, ALU.mult)
                link(v.tensor_scalar(tok[:, 5, z], tok[:, 1, z], wstat[:, 1, 1:2], 0.5 / 127, ALU.mult, ALU.mult))
                v.tensor_tensor(tok[:, 4, z], tok[:, 3, z], tok[:, 5, z], ALU.mult).then_inc(sm("tok_ready"), 1)
            v.wait_ge(sm("tok_ready"), 2)

            def hidden(t):
                v.wait_ge(sm("ffn_tanh"), t + 1)
                link(v.scalar_tensor_tensor(out=fa, in0=fth, scalar=1.0, in1=bank(0, 2), op0=ALU.add, op1=ALU.mult))
                if t >= 2:
                    v.wait_ge(sm("ffn_mix"), t - 1)
                v.tensor_tensor(fb[:, t % 2], fa, bank(2, 2), ALU.mult).then_inc(sm("ffn_b"), 1)

            def scales(r):
                v.wait_ge(sm("ffn_had"), r + 1)
                f = ft[:, r % 3]
                kf = tok[:, 4, r:r + 1]
                link(v.tensor_reduce(f[:, 0:1], bank(6, 2), AX.X, ALU.max, apply_absolute_value=True))
                link(v.tensor_scalar(f[:, 1:2], f[:, 0:1], kf, Q_EPS, ALU.mult, ALU.max))
                link(v.reciprocal(f[:, 2:3], f[:, 1:2]))
                v.tensor_scalar(f[:, 3:4], f[:, 2:3], kf, 127.0, ALU.mult, ALU.mult).then_inc(sm("ffn_scales"), 1)
                v.tensor_scalar(f[:, 4:5], f[:, 1:2], tok[:, 6, 0:1], None, ALU.mult)

            def quantise(r):
                v.wait_ge(sm("ffn_qa"), r + 1)
                link(v.tensor_scalar(fq, fq, 127.0, -128.0, ALU.min, ALU.max))
                if r >= 2:
                    v.wait_ge(sm("ffn_qtr"), r - 1)
                v.tensor_scalar(qh[:, r % 2], fq, ROUND, -ROUND, ALU.add, ALU.add).then_inc(sm("ffn_qh"), 1)

            def finish(r):
                v.wait_ge(sm("ffn_down"), r + 1)
                v.scalar_tensor_tensor(out=xs[:, r], in0=PS[:, 5, 0:D], scalar=ft[:, r % 3, 4:5], in1=xs[:, r],
                                       op0=ALU.mult, op1=ALU.add).then_inc(sm("out_ready"), 1)

            for t in range(NT + 4):
                if 3 <= t < NT + 3:
                    quantise(t - 3)
                if t >= 4:
                    finish(t - 4)
                if t < NT:
                    hidden(t)
                if 2 <= t < NT + 2:
                    scales(t - 2)


def kernel(**inputs):
    import ml_dtypes
    import numpy as np
    import concourse.bacc as bacc
    from concourse.bass_utils import run_bass_kernel_spmd

    x = {k: np.asarray(v) for k, v in inputs.items()}
    ctxp = np.zeros((DM, B, LP), np.float32)
    ctxp[:, :, DC - 1:] = x["ctx_1024"].transpose(2, 0, 1)
    arrays = {"x": x["x"], "ctxT": ctxp, "g_xattn": x["g_xattn"], "g_ffn": x["g_ffn"]}
    chan = []
    for ly in range(2):
        p = f"L{ly}_xattn_"
        arrays[f"L{ly}_inT"] = x[p + "in_proj_w"].T
        arrays[f"L{ly}_taps"] = x[p + "conv_w"].reshape(DI, DC).T
        w = x[p + "x_proj_w"].T
        dt, bc = w[:, :DR], w[:, DR:]
        arrays[f"L{ly}_xpT"] = np.concatenate([bc, bc, bc, dt], axis=1)
        arrays[f"L{ly}_dtT"] = x[p + "dt_proj_w"].T
        v = [x[p + n].reshape(DI, -1) for n in ("conv_b", "dt_proj_b", "D", "A_log")]
        chan.append(np.concatenate(v, axis=1).reshape(NH, P, 3 + DS))
    arrays["chan"] = np.stack(chan).transpose(2, 0, 1, 3)
    arrays["gateT"] = x["L0_ffn_gate_weight"].T
    gu = x["L0_ffn_gate_up_weights"].reshape(NCH, EC, D, 2, CB, I // CB)
    arrays["guT"] = gu.transpose(0, 2, 3, 4, 1, 5).reshape(NCH, D, 2 * CW)
    dn = x["L0_ffn_down_weights"].reshape(NCH, EC, CB, I // CB, D)
    arrays["dnT"] = dn.transpose(0, 2, 1, 3, 4).reshape(NCH, CW, D)
    arrays["wgT"], arrays["wuT"], arrays["wdT"] = (x[f"L1_ffn_w_{m}"].T for m in ("gate", "up", "down"))
    h = np.ones((1, 1), np.float32)
    while h.shape[0] < D:
        h = np.block([[h, h], [h, -h]])
    arrays["had"] = (h / 16).astype(np.float32)
    arrays["ident"] = np.eye(P, dtype=np.float32)
    arrays["identb"] = np.eye(P).astype(ml_dtypes.bfloat16)
    sel = np.zeros((3 * BC, BC, P), ml_dtypes.bfloat16)
    for i in range(3):
        for n in range(BC):
            sel[BC * i + n, n] = 1
    arrays["sel"] = sel
    arrays = {k: np.ascontiguousarray(v) for k, v in arrays.items()}

    nc = bacc.Bacc("TRN2", target_bir_lowering=False, num_devices=1)
    aps = {k: nc.dram_tensor(f"in_{k}", v.shape, mybir.dt.from_np(v.dtype), kind="ExternalInput").ap()
           for k, v in arrays.items()}
    out = nc.dram_tensor("out_0", (B, L, D), F32, kind="ExternalOutput").ap()
    flamingo_gated_block(nc, aps, out)
    r = run_bass_kernel_spmd(nc, [{f"in_{k}": v for k, v in arrays.items()}], core_ids=[0])
    return r.results[0]["out_0"]
```
